# Optimizing a Trainium2 kernel written in Bass

```python
import numpy as np
import jax
import jax.numpy as jnp

def _softmax(x, axis=-1):
    return jax.nn.softmax(x, axis=axis)

def _gelu(x):
    return jax.nn.gelu(x, approximate=True)

def _silu(x):
    return jax.nn.silu(x)

def _sigmoid(x):
    return jax.nn.sigmoid(x)

def _layernorm(x, axis=-1, eps=1e-05):
    m = jnp.mean(x, axis=axis, keepdims=True)
    v = jnp.var(x, axis=axis, keepdims=True)
    return (x - m) / jnp.sqrt(v + eps)

def _scatter_add(tgt, idx, src, axis=0):
    return tgt.at[idx].add(src)

def _segment_sum(src, seg, n):
    return jax.ops.segment_sum(src, seg, n)
kernel_name = 'mk_gnn_resnorm_d1_gnn_r8_97a9ef'

def setup_inputs(seed: int=0):
    np.random.seed(seed)
    _w = jnp.asarray

    def _rec_inputs():
        import jax
        import jax.numpy as jnp
        _gk = jax.random.key(seed)
        x = -0.000202 + 1 * jax.random.normal(jax.random.fold_in(_gk, 1), (6250, 128), jnp.float32)
        _s = jax.random.randint(jax.random.fold_in(_gk, 2), (100000,), 0, 6250, jnp.int32)
        _d = jax.random.randint(jax.random.fold_in(_gk, 3), (100000,), 0, 6250, jnp.int32)
        _loop = jnp.arange(6250, dtype=jnp.int32)
        src = jnp.concatenate([_s, _d, _loop])
        dst = jnp.concatenate([_d, _s, _loop])
        _o = jnp.argsort(dst, stable=True)
        src = src[_o]
        dst = dst[_o]
        edge_type_6 = jax.random.randint(jax.random.fold_in(_gk, 12), (206250,), 0, 6, jnp.int32)
        node_type_3 = jax.random.randint(jax.random.fold_in(_gk, 13), (6250,), 0, 3, jnp.int32)
        return (x, src, dst, edge_type_6, node_type_3)
    x, src, dst, edge_type_6, node_type_3 = _rec_inputs()

    def _L0_gnn_setup():
        import jax, jax.numpy as jnp
        import numpy as np
        N, D, H, HD = (6250, 128, 8, 16)
        E = 100000
        NT, ET, L = (3, 6, 2)
        SQRT_D = float(np.sqrt(HD))

        def typed_linear(x, tids, W):
            out = jnp.zeros((x.shape[0], W.shape[-1]), x.dtype)
            for t in range(W.shape[0]):
                out = out + jnp.where((tids == t)[:, None], x @ W[t], 0.0)
            return out

        def hgt_layer(x, ntype, src, dst, etype, Wk, Wq, Wv, Wa, pri, Watt, Wmsg, skip):
            n = x.shape[0]
            k = typed_linear(x, ntype, Wk).reshape(n, H, HD)
            q = typed_linear(x, ntype, Wq).reshape(n, H, HD)
            v = typed_linear(x, ntype, Wv).reshape(n, H, HD)
            k_e, q_e, v_e = (k[src], q[dst], v[src])
            kw = jnp.zeros_like(k_e)
            mv = jnp.zeros_like(v_e)
            for t in range(ET):
                m = (etype == t)[:, None, None]
                kw = kw + jnp.where(m, jnp.einsum('ehd,hdo->eho', k_e, Watt[:, t]), 0.0)
                mv = mv + jnp.where(m, jnp.einsum('ehd,hdo->eho', v_e, Wmsg[:, t]), 0.0)
            a = jnp.sum(kw * q_e, axis=-1) * pri.T[etype] / SQRT_D
            amax = jax.ops.segment_max(a, dst, num_segments=n)
            amax = jnp.where(jnp.isfinite(amax), amax, 0.0)
            ea = jnp.exp(a - amax[dst])
            esum = jax.ops.segment_sum(ea, dst, num_segments=n)
            attn = ea / esum[dst]
            msg = (mv * attn[:, :, None]).reshape(-1, H * HD)
            h = jax.ops.segment_sum(msg, dst, num_segments=n)
            h = typed_linear(h, ntype, Wa)
            alpha = jax.nn.sigmoid(skip)[ntype][:, None]
            return h * alpha + x * (1.0 - alpha)
        key = jax.random.key(seed)
        ks = jax.random.split(key, 12)
        x = jax.random.normal(ks[0], (N, D), dtype=jnp.float32)
        ntype = jnp.sort(jax.random.randint(ks[1], (N,), 0, NT))
        src = jax.random.randint(ks[2], (E,), 0, N)
        dst = jax.random.randint(ks[3], (E,), 0, N)
        etype = jnp.sort(jax.random.randint(ks[4], (E,), 0, ET))
        s = 1.0 / np.sqrt(D)
        Wk = jax.random.normal(ks[5], (L, NT, D, D), dtype=jnp.float32) * s
        Wq = jax.random.normal(ks[6], (L, NT, D, D), dtype=jnp.float32) * s
        Wv = jax.random.normal(ks[7], (L, NT, D, D), dtype=jnp.float32) * s
        Wa = jax.random.normal(ks[8], (L, NT, D, D), dtype=jnp.float32) * s
        sh = 1.0 / np.sqrt(HD)
        Watt = jax.random.normal(ks[9], (L, H, ET, HD, HD), dtype=jnp.float32) * sh
        Wmsg = jax.random.normal(ks[10], (L, H, ET, HD, HD), dtype=jnp.float32) * sh
        pri = jnp.ones((L, H, ET), dtype=jnp.float32)
        skip = jnp.ones((L, NT), dtype=jnp.float32)
        return dict(x=x, ntype=ntype, src=src, dst=dst, etype=etype, Wk=Wk, Wq=Wq, Wv=Wv, Wa=Wa, pri=pri, Watt=Watt, Wmsg=Wmsg, skip=skip)
    _L0_gnn_all = _L0_gnn_setup()
    _L0_gnn_in = {k: v for k, v in _L0_gnn_all.items() if k in ('Wk', 'Wq', 'Wv', 'Wa', 'pri', 'Watt', 'Wmsg', 'skip')}
    del _L0_gnn_all
    return {'x': x, 'src': src, 'dst': dst, 'edge_type_6': edge_type_6, 'node_type_3': node_type_3, 'L0_gnn_Wk': _L0_gnn_in['Wk'], 'L0_gnn_Wq': _L0_gnn_in['Wq'], 'L0_gnn_Wv': _L0_gnn_in['Wv'], 'L0_gnn_Wa': _L0_gnn_in['Wa'], 'L0_gnn_pri': _L0_gnn_in['pri'], 'L0_gnn_Watt': _L0_gnn_in['Watt'], 'L0_gnn_Wmsg': _L0_gnn_in['Wmsg'], 'L0_gnn_skip': _L0_gnn_in['skip']}

def reference(x, src, dst, edge_type_6, node_type_3, L0_gnn_Wk, L0_gnn_Wq, L0_gnn_Wv, L0_gnn_Wa, L0_gnn_pri, L0_gnn_Watt, L0_gnn_Wmsg, L0_gnn_skip):
    import jax
    import jax.numpy as jnp

    def _L0_gnn_ref(x, ntype, src, dst, etype, Wk, Wq, Wv, Wa, pri, Watt, Wmsg, skip):
        import jax, jax.numpy as jnp
        import numpy as np
        N, D, H, HD = (6250, 128, 8, 16)
        E = 100000
        NT, ET, L = (3, 6, 2)
        SQRT_D = float(np.sqrt(HD))

        def typed_linear(x, tids, W):
            out = jnp.zeros((x.shape[0], W.shape[-1]), x.dtype)
            for t in range(W.shape[0]):
                out = out + jnp.where((tids == t)[:, None], x @ W[t], 0.0)
            return out

        def hgt_layer(x, ntype, src, dst, etype, Wk, Wq, Wv, Wa, pri, Watt, Wmsg, skip):
            n = x.shape[0]
            k = typed_linear(x, ntype, Wk).reshape(n, H, HD)
            q = typed_linear(x, ntype, Wq).reshape(n, H, HD)
            v = typed_linear(x, ntype, Wv).reshape(n, H, HD)
            k_e, q_e, v_e = (k[src], q[dst], v[src])
            kw = jnp.zeros_like(k_e)
            mv = jnp.zeros_like(v_e)
            for t in range(ET):
                m = (etype == t)[:, None, None]
                kw = kw + jnp.where(m, jnp.einsum('ehd,hdo->eho', k_e, Watt[:, t]), 0.0)
                mv = mv + jnp.where(m, jnp.einsum('ehd,hdo->eho', v_e, Wmsg[:, t]), 0.0)
            a = jnp.sum(kw * q_e, axis=-1) * pri.T[etype] / SQRT_D
            amax = jax.ops.segment_max(a, dst, num_segments=n)
            amax = jnp.where(jnp.isfinite(amax), amax, 0.0)
            ea = jnp.exp(a - amax[dst])
            esum = jax.ops.segment_sum(ea, dst, num_segments=n)
            attn = ea / esum[dst]
            msg = (mv * attn[:, :, None]).reshape(-1, H * HD)
            h = jax.ops.segment_sum(msg, dst, num_segments=n)
            h = typed_linear(h, ntype, Wa)
            alpha = jax.nn.sigmoid(skip)[ntype][:, None]
            return h * alpha + x * (1.0 - alpha)
        h = x
        for l in range(L):
            h = hgt_layer(h, ntype, src, dst, etype, Wk[l], Wq[l], Wv[l], Wa[l], pri[l], Watt[l], Wmsg[l], skip[l])
        return h
    x = _layernorm(x + _L0_gnn_ref(x, node_type_3, src, dst, edge_type_6, L0_gnn_Wk, L0_gnn_Wq, L0_gnn_Wv, L0_gnn_Wa, L0_gnn_pri, L0_gnn_Watt, L0_gnn_Wmsg, L0_gnn_skip), axis=-1)
    return x

_drawn_inputs = setup_inputs


def setup_inputs(seed=0):
    import zlib

    import numpy as np

    out = dict(_drawn_inputs(seed))
    spreads = {'L0_gnn_pri': (1.0, 0.6), 'L0_gnn_skip': (1.0, 0.6)}
    factors = {}
    for name, (base, spread) in spreads.items():
        noise = np.random.default_rng([zlib.crc32(name.encode()), seed]).standard_normal(out[name].shape)
        drawn = base * np.exp(spread * noise) if base else spread * noise
        out[name] = jnp.asarray(drawn.astype(out[name].dtype))
    for name, factor in factors.items():
        out[name] = (out[name] * factor).astype(out[name].dtype)
    return out
```

```python
from contextlib import ExitStack

import concourse.bass as bass
from concourse import mybir

ALU = mybir.AluOpType
ACT = mybir.ActivationFunctionType
F32 = mybir.dt.float32
BF16 = mybir.dt.bfloat16
I32 = mybir.dt.int32
X_AXIS = mybir.AxisListType.X

P = 128
N, D, H = 6250, 128, 8
HD = D // H
NT, ET, L = 3, 6, 2
E = 206250
EPS = 1e-5
BIG = 2.0 ** 100

TE = P
CT = P // H
QT = 4
NQ = CT // QT
NCH = -(-E // (TE * CT))
TILES = NCH * CT
NG = -(-TILES // P)
FULL = E // TE
REST = E - FULL * TE
GL = TILES - (NG - 1) * P
NPAD = 6400
NB = 256
NBLK = NPAD // NB
XT = -(-N // P)
XR = N - (XT - 1) * P
ROW = 2 * D

M_A, M_C, M_D, M_AM, M_CM, M_DM, M_W = 0, 129, 257, 385, 513, 641, 770
R_A, R_C, R_CR, R_AR, R_W = 0, 16, 32, 48, 128

STEPS = [
    "run_max_fwd", "run_max", "max_edges", "max_carry", "max_left", "max_right_in", "max_right_top",
    "max_right", "max_carry_on", "max_pick", "max_picked", "max_first", "max_all", "shifted",
    "alpha_arg", "run_sum_fwd", "run_sum", "sum_edges", "sum_carry_in", "sum_carry", "sum_left",
    "sum_right_in", "sum_right_top", "sum_right", "sum_pick", "sum_picked", "sum_first", "sum_all",
    "sum_inverse", "weights", "acc_factor",
]
K_DVE = len(STEPS)
PE_STEPS = ["scores_t", "max_rows", "max_cols", "sum_rows", "sum_cols", "factor_cols", "weights_e"]
K_PE = len(PE_STEPS)
ACT_STEPS = ["alpha", "exps", "weights_sb"]
K_ACT = len(ACT_STEPS)


class Chunk:

    def __init__(self, l, c, par, half):
        self.c, self.par, self.half = c, par, half
        self.all = l * NCH + c
        self.use = l * ((NCH + 1 - par) // 2) + half

    def quarters(self, q):
        return self.all * NQ + (q + 1)


def wait(eng, sem, value):
    if not (isinstance(value, int) and value <= 0):
        eng.wait_ge(sem, value)


def over_chunks(eng, l, body):
    def at(c):
        return Chunk(l, c, c % 2, c // 2)

    pairs = (NCH - 3) // 2
    assert NCH % 2 == 1
    body(at(0), None, at(1))
    body(at(1), at(0), at(2))
    with eng.Fori(0, pairs) as i:
        one = Chunk(l, i * 2 + 2, 0, i + 1)
        two = Chunk(l, i * 2 + 3, 1, i + 1)
        body(one, Chunk(l, i * 2 + 1, 1, i), two)
        body(two, one, Chunk(l, i * 2 + 4, 0, i + 2))
    body(at(NCH - 1), at(NCH - 2), None)
    body(None, at(NCH - 1), None)


def hgt_kernel(nc, x, src, dst, etype, ntype, Wk, Wq, Wv, Wa, pri, Watt, Wmsg, skip, out):
    table = nc.dram_tensor("kv_table", [NPAD * ET, ROW], F32).ap()
    queries = nc.dram_tensor("queries", [NPAD, D], F32).ap()
    dst_pad = nc.dram_tensor("dst_pad", [TILES, TE], I32).ap()
    edge_masks = nc.dram_tensor("edge_masks", [TILES, M_W], BF16).ap()
    tile_masks = nc.dram_tensor("tile_masks", [NCH, R_W], F32).ap()

    with ExitStack() as kept:
        def sb(name, shape, dt=F32, ctx=kept):
            return ctx.enter_context(nc.sbuf_tensor(name, shape, dt))

        def sem(name):
            return kept.enter_context(nc.semaphore(name))

        banks = [kept.enter_context(nc.psum_tensor(f"bank{i}", [P, 512], F32)) for i in range(8)]

        x_t = sb("x_t", [P, NPAD])
        acc = sb("acc", [P, NPAD])
        ntype_b = sb("ntype_b", [P, NPAD], I32)
        edge_ix = sb("edge_ix", [P, NCH, 2 * CT], I32)
        windows = sb("windows", [1, TILES], I32)
        ident = sb("ident", [P, P])
        ramp = sb("ramp", [P, TE])
        tile_sel = sb("tile_sel", [P, CT])
        head_sel = sb("head_sel", [P, H])
        head_rep = sb("head_rep", [H, P])
        head_exp = sb("head_exp", [H, P])

        prepare(nc, sb, sem, banks, x, src, dst, etype, ntype, x_t, ntype_b, edge_ix, windows, ident,
                ramp, tile_sel, head_sel, head_rep, head_exp, dst_pad, edge_masks, tile_masks)
        node_sems = {n: sem(n) for n in (
            "w_in", "bd_zero", "bd_scaled", "masked", "tables_kv", "kvq_done", "kv_sb", "q_sb", "tables_mm", "evac_act",
            "evac_dve", "query_out", "acc_zero")}
        node_sems["table_out"] = [sem(f"table_out_{i}") for i in range(2)]
        edge_sems = edge_semaphores(sem)
        out_sems = {n: sem(n) for n in (
            "wa_in", "neg_exp", "gates", "wa_scaled", "h_masked", "mixed", "x_new", "x_rows", "rows_t",
            "resid", "stats", "aggr", "root", "norm_step", "normed", "stored")}
        for l in range(L):
            tables(nc, l, node_sems, banks, x_t, acc, ntype_b, Wk, Wq, Wv, pri, Watt, Wmsg, table, queries)
            edges(nc, l, edge_sems, banks, acc, edge_ix, windows, ident, ramp, tile_sel, head_sel,
                  head_rep, head_exp, table, queries, edge_masks, tile_masks)
            node_out(nc, l, out_sems, banks, x_t, acc, ntype_b, ident, Wa, skip, x, out)


def prepare(nc, sb, sem, banks, x, src, dst, etype, ntype, x_t, ntype_b, edge_ix, windows, ident, ramp,
            tile_sel, head_sel, head_rep, head_exp, dst_pad, edge_masks, tile_masks):
    with ExitStack() as ctx:
        dst_i = sb("dst_i", [P, NG, TE], I32, ctx)
        src_i = sb("src_i", [P, NG, TE], I32, ctx)
        et_i = sb("et_i", [P, NG, TE], I32, ctx)
        dst_f = sb("dst_f", [P, NG, TE], F32, ctx)
        row_f = sb("row_f", [P, NG, TE], F32, ctx)
        rel_f = sb("rel_f", [P, NG, TE], F32, ctx)
        masks = sb("masks", [P, NG, M_W], BF16, ctx)
        x_in = sb("x_in", [P, XT, D], F32, ctx)
        first_i = sb("first_i", [NCH, CT], I32, ctx)
        last_i = sb("last_i", [NCH, CT + 1], I32, ctx)
        goes_on = sb("goes_on", [NCH, CT], F32, ctx)
        whole = sb("whole", [NCH, CT], F32, ctx)
        rowm = sb("rowm", [NCH, R_W], F32, ctx)

        filled = sem("filled")
        edges_in = sem("edges_in")
        x_loaded = sem("x_loaded")
        ntype_in = sem("ntype_in")
        dst_padded = sem("dst_padded")
        ends_in = sem("ends_in")
        windows_in = sem("windows_in")
        ident_step = sem("ident_step")
        consts = sem("consts")
        prep = sem("prep")
        turned = sem("turned")
        put = sem("put")
        rows_made = sem("rows_made")
        masks_out = sem("masks_out")
        sels = sem("sels")

        def tiles_view(a, g0, g1):
            return a[g0 * P * TE:g1 * P * TE].rearrange("(g p e) -> p g e", p=P, e=TE)

        with nc.Block() as block:
            @block.sync
            def _(sp):
                sp.dma_start(x_in[:, 0:XT - 1, :], x[0:(XT - 1) * P, :].rearrange("(b p) f -> p b f", p=P)).then_inc(x_loaded, 16)
                sp.dma_start(x_in[0:XR, XT - 1, :], x[(XT - 1) * P:N, :]).then_inc(x_loaded, 16)
                sp.wait_ge(filled, 4)
                g = (NG - 1) * P
                for tile, a in ((dst_i, dst), (src_i, src), (et_i, etype)):
                    sp.dma_start(tile[:, 0:NG - 1, :], tiles_view(a, 0, NG - 1)).then_inc(edges_in, 16)
                    sp.dma_start(tile[0:FULL - g, NG - 1, :], a[g * TE:FULL * TE].rearrange("(p e) -> p e", e=TE)).then_inc(edges_in, 16)
                    sp.dma_start(tile[FULL - g:FULL - g + 1, NG - 1, 0:REST], a[FULL * TE:E].rearrange("(p e) -> p e", p=1)).then_inc(edges_in, 16)
                sp.dma_start(ntype_b[:, 0:N], ntype.rearrange("(a n) -> a n", a=1).to_broadcast([P, N])).then_inc(ntype_in, 16)
                sp.wait_ge(edges_in, 16 * 9)
                sp.dma_start(dst_pad[0:g, :].rearrange("(g p) e -> p g e", p=P), dst_i[:, 0:NG - 1, :]).then_inc(dst_padded, 16)
                sp.dma_start(dst_pad[g:TILES, :], dst_i[0:GL, NG - 1, :]).then_inc(dst_padded, 16)
                sp.wait_ge(dst_padded, 32)
                with nc.allow_non_contiguous_dma(reason="one node of each tile, once"):
                    by_chunk = dst_pad.rearrange("(c t) e -> c t e", t=CT)
                    sp.dma_start(first_i[:, :], by_chunk[:, :, 0]).then_inc(ends_in, 16)
                    sp.dma_start(last_i[:, 1:CT + 1], by_chunk[:, :, TE - 1]).then_inc(ends_in, 16)
                    sp.dma_start(last_i[1:NCH, 0:1], by_chunk[0:NCH - 1, CT - 1:CT, TE - 1]).then_inc(ends_in, 16)
                    sp.dma_start(windows[0:1, :], dst_pad[:, 0:1].rearrange("t a -> a t")).then_inc(windows_in, 16)
                sp.wait_ge(prep, 15)
                sp.dma_start(edge_masks[0:g, :].rearrange("(g p) m -> p g m", p=P), masks[:, 0:NG - 1, :]).then_inc(masks_out, 16)
                sp.dma_start(edge_masks[g:TILES, :], masks[0:GL, NG - 1, :]).then_inc(masks_out, 16)
                sp.wait_ge(rows_made, 9)
                sp.dma_start(tile_masks[:, :], rowm[:, :]).then_inc(masks_out, 16)
                sp.wait_ge(masks_out, 48)
                sp.wait_ge(ntype_in, 16)
                sp.wait_ge(windows_in, 16)

            @block.gpsimd
            def _(pool):
                pool.memset(dst_i[:, :, :], N).then_inc(filled, 1)
                pool.memset(src_i[:, :, :], 0).then_inc(filled, 1)
                pool.memset(et_i[:, :, :], 0).then_inc(filled, 1)
                pool.memset(last_i[:, :], -1).then_inc(filled, 1)
                pool.memset(ident[:, :], 0.0).then_inc(ident_step, 1)
                pool.memset(head_rep[:, :], 0.0).then_inc(ident_step, 1)
                pool.memset(head_exp[:, :], 0.0).then_inc(ident_step, 1)
                pool.wait_ge(ident_step, 3)
                pool.affine_select(out=ident[:, :], in_=ident[:, :], compare_op=ALU.not_equal, fill=1.0,
                                   base=0, pattern=[[-1, P]], channel_multiplier=1).then_inc(consts, 1)
                v = head_rep[:, :].rearrange("p (t h) -> p t h", h=H)
                pool.affine_select(out=v, in_=v, compare_op=ALU.not_equal, fill=1.0, base=0,
                                   pattern=[[0, CT], [-1, H]], channel_multiplier=1).then_inc(consts, 1)
                v = head_exp[:, :].rearrange("p (h d) -> p h d", h=H)
                pool.affine_select(out=v, in_=v, compare_op=ALU.not_equal, fill=1.0, base=0,
                                   pattern=[[-1, H], [0, HD]], channel_multiplier=1).then_inc(consts, 1)
                pool.iota(ramp[:, :], [[1, TE]], base=0, channel_multiplier=0,
                          allow_small_or_imprecise_dtypes=True).then_inc(consts, 1)
                pool.memset(x_t[:, N:NPAD], 0.0).then_inc(consts, 1)
                pool.memset(ntype_b[:, N:NPAD], 0).then_inc(consts, 1)

            @block.vector
            def _(dve):
                v = nc.vector
                dve.wait_ge(consts, 1)
                v.tensor_reduce(tile_sel[:, :], ident[:, :].rearrange("p (t h) -> p t h", h=H), X_AXIS, ALU.add).then_inc(sels, 1)
                v.tensor_reduce(head_sel[:, :], ident[:, :].rearrange("p (t h) -> p h t", h=H), X_AXIS, ALU.add).then_inc(sels, 1)
                dve.wait_ge(edges_in, 16 * 9)
                v.tensor_copy(dst_f[:, :, :], dst_i[:, :, :]).then_inc(prep, 1)
                v.scalar_tensor_tensor(row_f[:, :, :], src_i[:, :, :], float(ET), et_i[:, :, :], ALU.mult, ALU.add).then_inc(prep, 1)
                dve.wait_ge(prep, 1)
                first = dst_f[:, :, 0:1].to_broadcast([P, NG, TE])
                last = dst_f[:, :, TE - 1:TE].to_broadcast([P, NG, TE])
                d = dst_f[:, :, :]
                v.tensor_tensor(rel_f[:, :, :], d, first, ALU.subtract).then_inc(prep, 1)
                v.memset(masks[:, :, M_A:M_A + TE + 1], -BIG).then_inc(prep, 1)
                v.memset(masks[:, :, M_AM:M_AM + 1], 0.0).then_inc(prep, 1)
                v.memset(masks[:, :, M_DM + TE:M_W], 0.0).then_inc(prep, 1)
                v.tensor_tensor(masks[:, :, M_AM + 1:M_AM + TE], dst_f[:, :, 1:TE], dst_f[:, :, 0:TE - 1], ALU.is_equal).then_inc(prep, 1)
                v.tensor_tensor(masks[:, :, M_CM:M_CM + TE], d, first, ALU.is_equal).then_inc(prep, 1)
                v.tensor_tensor(masks[:, :, M_DM:M_DM + TE], d, last, ALU.is_equal).then_inc(prep, 1)
                dve.wait_ge(prep, 9)
                for k, (to, of, n) in enumerate(((M_A + 1, M_AM + 1, TE - 1), (M_C, M_CM, TE), (M_D, M_DM, TE))):
                    v.tensor_scalar(masks[:, :, to:to + n], masks[:, :, of:of + n], 1.0, BIG, ALU.subtract, ALU.mult).then_inc(prep, 2)
                dve.wait_ge(ends_in, 48)
                v.memset(rowm[:, :], 0.0).then_inc(rows_made, 1)
                v.tensor_tensor(goes_on[:, :], first_i[:, :], last_i[:, 0:CT], ALU.is_equal).then_inc(rows_made, 1)
                v.tensor_tensor(whole[:, :], first_i[:, :], last_i[:, 1:CT + 1], ALU.is_equal).then_inc(rows_made, 1)
                dve.wait_ge(rows_made, 3)
                f = R_W // 2
                v.tensor_tensor(rowm[:, f + R_A:f + R_A + CT], goes_on[:, :], whole[:, :], ALU.mult).then_inc(rows_made, 1)
                v.tensor_copy(rowm[:, f + R_C:f + R_C + CT], goes_on[:, :]).then_inc(rows_made, 1)
                v.tensor_copy(rowm[:, f + R_CR:f + R_CR + CT - 1], goes_on[:, 1:CT]).then_inc(rows_made, 1)
                v.tensor_tensor(rowm[:, f + R_AR:f + R_AR + CT - 1], goes_on[:, 1:CT], whole[:, 1:CT], ALU.mult).then_inc(rows_made, 1)
                dve.wait_ge(rows_made, 7)
                v.tensor_scalar(rowm[:, 0:f], rowm[:, f:2 * f], 1.0, BIG, ALU.subtract, ALU.mult).then_inc(rows_made, 2)

            @block.tensor
            def _(pe):
                pe.wait_ge(consts, 1)
                pe.wait_ge(x_loaded, 32)
                for g in range(NT_GROUPS):
                    if g >= 2:
                        pe.wait_ge(put, g - 1)
                    for k, b in enumerate(range(g * 4, min(g * 4 + 4, XT))):
                        n = P if b < XT - 1 else XR
                        last = nc.tensor.transpose(banks[g % 2][:, k * P:k * P + n], x_in[0:n, b, :], ident[0:n, 0:n])
                    last.then_inc(turned, 1)
                pe.wait_ge(prep, 3)
                for g in range(NG):
                    pe.wait_ge(put, NT_GROUPS + g - 1)
                    n = P if g < NG - 1 else GL
                    bank = banks[(NT_GROUPS + g) % 2]
                    nc.tensor.transpose(bank[:, 0:n], row_f[0:n, g, :], ident[0:n, 0:n])
                    nc.tensor.transpose(bank[:, P:P + n], rel_f[0:n, g, :], ident[0:n, 0:n]).then_inc(turned, 1)

            @block.scalar
            def _(act):
                a = nc.scalar
                for g in range(NT_GROUPS):
                    act.wait_ge(turned, g + 1)
                    n = min(N, (g + 1) * 4 * P) - g * 4 * P
                    a.activation(x_t[:, g * 4 * P:g * 4 * P + n], banks[g % 2][:, 0:n], ACT.Copy).then_inc(put, 1)
                for g in range(NG):
                    act.wait_ge(turned, NT_GROUPS + g + 1)
                    n = P if g < NG - 1 else GL
                    c0, c1 = g * P // CT, (g * P + n) // CT
                    bank = banks[(NT_GROUPS + g) % 2]
                    a.activation(edge_ix[:, c0:c1, 0:CT], bank[:, 0:n].rearrange("p (c t) -> p c t", t=CT), ACT.Copy)
                    a.activation(edge_ix[:, c0:c1, CT:2 * CT].bitcast(F32), bank[:, P:P + n].rearrange("p (c t) -> p c t", t=CT), ACT.Copy).then_inc(put, 1)


NT_GROUPS = -(-XT // 4)


def tables(nc, l, s, banks, x_t, acc, ntype_b, Wk, Wq, Wv, pri, Watt, Wmsg, table, queries):
    HALF = ET // 2 * D
    with ExitStack() as ctx:
        def sb(name, shape, dt=F32):
            return ctx.enter_context(nc.sbuf_tensor(f"tab_{name}_{l}", shape, dt))

        wk, wq, wv = sb("wk", [P, NT, D]), sb("wq", [P, NT, D]), sb("wv", [P, NT, D])
        bd = sb("bd", [P, 2, ET, D])
        prior = sb("prior", [P, ET])
        masked = sb("masked", [P, NT, NB])
        kv_t = sb("kv_t", [P, 2, NB])
        q_rows = sb("q_rows", [P, 2, D])
        rows = sb("rows", [P, 2, ET, 2, D])
        kv_ps, q_ps, tab_ps = banks[0], banks[1], banks[2:6]
        loads = 3 + 1 + 2 * H

        def blocks(b):
            return l * NBLK + b

        with nc.Block() as block:
            @block.sync
            def _(sp):
                for w, a in ((wk, Wk), (wv, Wv), (wq, Wq)):
                    sp.dma_start(w[:, :, :], a[l].rearrange("t k n -> k t n")).then_inc(s["w_in"], 16)
                with nc.allow_non_contiguous_dma(reason="48 values"):
                    sp.dma_start(prior[:, :], pri[l].rearrange("h (a t) -> h a t", a=1).to_broadcast([H, HD, ET])).then_inc(s["w_in"], 16)
                sp.wait_ge(s["bd_zero"], l + 1)
                for i, a in ((0, Watt), (1, Wmsg)):
                    for h in range(H):
                        r = slice(h * HD, (h + 1) * HD)
                        sp.dma_start(bd[r, i, :, r], a[l, h].rearrange("t d o -> d t o")).then_inc(s["w_in"], 16)
                with sp.Fori(0, NBLK) as b:
                    for i in range(2):
                        if i == 0:
                            sp.wait_ge(s["q_sb"], (blocks(b) + 1))
                            sp.dma_start(queries[bass.ds(b * NB, NB), :].rearrange("(i p) f -> p i f", p=P), q_rows[:, :, :]).then_inc(s["query_out"], 16)
                        sp.wait_ge(s["evac_act"], blocks(b) * 4 + 2 * (i + 1))
                        sp.wait_ge(s["evac_dve"], blocks(b) * 4 + 2 * (i + 1))
                        sp.dma_start(table[bass.ds(b * (NB * ET) + i * (P * ET), P * ET), :].rearrange("(p t) f -> p (t f)", t=ET),
                                     rows[:, i, :, :, :].rearrange("p t k f -> p (t k f)")).then_inc(s["table_out"][i], 16)
                sp.wait_ge(s["query_out"], (l + 1) * NBLK * 16)
                for i in range(2):
                    sp.wait_ge(s["table_out"][i], (l + 1) * NBLK * 16)

            @block.gpsimd
            def _(pool):
                pool.memset(bd[:, :, :, :], 0.0).then_inc(s["bd_zero"], 1)
                pool.memset(acc[:, :], 0.0).then_inc(s["acc_zero"], 1)

            @block.vector
            def _(dve):
                v = nc.vector

                def mask(b):
                    for t in range(NT):
                        v.scalar_tensor_tensor(masked[:, t, :], ntype_b[:, bass.ds(b * NB, NB)], float(t), x_t[:, bass.ds(b * NB, NB)],
                                               ALU.is_equal, ALU.mult).then_inc(s["masked"], 1)

                def evac(b):
                    for i in range(2):
                        for hf in range(2):
                            dve.wait_ge(s["tables_mm"], blocks(b) * 8 + (i * 4 + 2 + hf + 1))
                            if hf == 0:
                                yield i
                            v.tensor_copy(rows[:, i, 3 * hf:3 * hf + 3, 1, :], tab_ps[2 + hf][:, 0:HALF].rearrange("p (t f) -> p t f", f=D)).then_inc(s["evac_dve"], 1)

                mask(0)
                dve.wait_ge(s["w_in"], 16 * loads * (l + 1))
                v.scalar_tensor_tensor(bd[:, 0, :, :], bd[:, 0, :, :], 1.0 / float(HD) ** 0.5, prior[:, :].unsqueeze(2).to_broadcast([P, ET, D]),
                                       ALU.mult, ALU.mult).then_inc(s["bd_scaled"], 1)

                def block_of(b, more, reuse):
                    if more:
                        dve.wait_ge(s["kvq_done"], (blocks(b) + 1))
                        mask(b + 1)
                    for i in evac(b):
                        if reuse:
                            dve.wait_ge(s["table_out"][i], (blocks(b) * 16))

                block_of(0, True, l > 0)
                with dve.Fori(1, NBLK - 1) as b:
                    block_of(b, True, True)
                block_of(NBLK - 1, False, True)

            @block.tensor
            def _(pe):
                t_ = nc.tensor
                pe.wait_ge(s["w_in"], 16 * loads * (l + 1))
                pe.wait_ge(s["bd_scaled"], l + 1)

                def block_of(b, reuse):
                    pe.wait_ge(s["masked"], (blocks(b) + 1) * NT)
                    if reuse:
                        pe.wait_ge(s["q_sb"], blocks(b))
                        pe.wait_ge(s["kv_sb"], blocks(b))
                    for i, w in enumerate((wk, wv)):
                        for t in range(NT):
                            last = t_.matmul(kv_ps[:, i * NB:(i + 1) * NB], w[:, t, :], masked[:, t, :], start=(t == 0), stop=(t == NT - 1))
                    last.then_inc(s["tables_kv"], 1)
                    for i in range(2):
                        for t in range(NT):
                            last = t_.matmul(q_ps[:, i * D:(i + 1) * D], masked[:, t, i * P:(i + 1) * P], wq[:, t, :], start=(t == 0), stop=(t == NT - 1))
                    last.then_inc(s["kvq_done"], 1)
                    pe.wait_ge(s["kv_sb"], (blocks(b) + 1))
                    for i in range(2):
                        for kv in range(2):
                            for hf in range(2):
                                if i == 1:
                                    pe.wait_ge(s["evac_dve" if kv else "evac_act"], blocks(b) * 4 + (hf + 1))
                                elif reuse:
                                    pe.wait_ge(s["evac_dve" if kv else "evac_act"], blocks(b) * 4 - 2 + (hf + 1))
                                t_.matmul(tab_ps[2 * kv + hf][:, 0:HALF], kv_t[:, kv, i * P:(i + 1) * P],
                                          bd[:, kv, 3 * hf:3 * hf + 3, :].rearrange("p t f -> p (t f)"), start=True, stop=True).then_inc(s["tables_mm"], 1)

                block_of(0, l > 0)
                with pe.Fori(1, NBLK) as b:
                    block_of(b, True)

            @block.scalar
            def _(act):
                a = nc.scalar

                def block_of(b, reuse):
                    act.wait_ge(s["tables_kv"], (blocks(b) + 1))
                    if reuse:
                        act.wait_ge(s["tables_mm"], blocks(b) * 8)
                    a.activation(kv_t[:, :, :], kv_ps[:, :].rearrange("p (k n) -> p k n", k=2), ACT.Copy).then_inc(s["kv_sb"], 1)
                    act.wait_ge(s["kvq_done"], (blocks(b) + 1))
                    if reuse:
                        act.wait_ge(s["query_out"], (blocks(b) * 16))
                    a.activation(q_rows[:, :, :], q_ps[:, 0:2 * D].rearrange("p (i f) -> p i f", i=2), ACT.Copy).then_inc(s["q_sb"], 1)
                    for i in range(2):
                        for hf in range(2):
                            act.wait_ge(s["tables_mm"], blocks(b) * 8 + (i * 4 + hf + 1))
                            if hf == 0 and reuse:
                                act.wait_ge(s["table_out"][i], (blocks(b) * 16))
                            a.activation(rows[:, i, 3 * hf:3 * hf + 3, 0, :], tab_ps[hf][:, 0:HALF].rearrange("p (t f) -> p t f", f=D), ACT.Copy).then_inc(s["evac_act"], 1)

                block_of(0, l > 0)
                with act.Fori(1, NBLK) as b:
                    block_of(b, True)


def edge_semaphores(sem):
    one = ["onehot_dist", "onehot", "onehot_t", "onehot_t_sb", "q_spread", "products", "scores", "messages",
           "summed", "added", "stat_steps", "pe_steps", "act_steps", "carry_init"]
    s = {n: sem(n) for n in one}
    for n in ("ix_in", "masks_in"):
        s[n] = [sem(f"{n}_{p}") for p in range(2)]
    for n in ("rows_in", "queries_in"):
        s[n] = [[sem(f"{n}_{p}_{q}") for q in range(NQ)] for p in range(2)]
    return s


def edges(nc, l, s, banks, acc, edge_ix, windows, ident, ramp, tile_sel, head_sel, head_rep, head_exp,
          table, queries, edge_masks, tile_masks):
    with ExitStack() as ctx:
        def sb(name, shape, dt=F32):
            return ctx.enter_context(nc.sbuf_tensor(f"edge_{name}_{l}", shape, dt))

        ix = [sb(f"ix{p}", [P, 2 * CT], I32) for p in range(2)]
        em = [sb(f"em{p}", [P, M_W], BF16) for p in range(2)]
        tm = [sb(f"tm{p}", [H, R_W]) for p in range(2)]
        kv = [sb(f"kv{p}", [P, CT, ROW]) for p in range(2)]
        qw = [sb(f"qw{p}", [P, CT, D]) for p in range(2)]
        onehot = [sb(f"onehot{p}", [P, CT, TE]) for p in range(2)]
        dist = [sb(f"dist{i}", [P, QT, TE]) for i in range(2)]
        onehot_t = [sb(f"onehot_t{p}", [P, QT, TE]) for p in range(2)]
        prod = sb("prod", [P, QT, D])
        msg = [sb(f"msg{p}", [P, QT, D]) for p in range(2)]
        scores = sb("scores", [P, P])
        wave = {n: sb(n, [P, TE]) for n in ("max_f", "max_b", "max_1", "max_2", "shift", "ea", "sum_f", "sum_b", "sum_1", "sum_2", "inv", "wts")}
        wts_e = sb("wts_e", [P, P])
        ends = [sb(f"ends{i}", [P, 2, CT]) for i in range(2)]
        picked = [sb(f"picked{i}", [P, 2, CT]) for i in range(2)]
        cols = [sb(f"cols{i}", [P, 2]) for i in range(2)]
        state = [sb(f"state{i}", [H, CT + 1]) for i in range(2)]
        right = [sb(f"right{i}", [H, CT]) for i in range(2)]
        sides = [sb(f"sides{i}", [H, 2, CT]) for i in range(2)]
        alpha_arg = sb("alpha_arg", [H, 1])
        alpha = sb("alpha", [H, 1])
        factor = sb("factor", [H, 1])

        st_ps, qe_ps, ag_ps = banks[0:2], banks[2:4], banks[4:6]
        scores_t = banks[6][:, 0:P]
        wts_ps = banks[6][:, P:2 * P]
        rows_ps = [banks[7][0:H, 64 * i:64 * i + 2 * CT] for i in range(2)]
        cols_ps = [banks[7][:, 128 + 64 * i:128 + 64 * i + 2 * CT] for i in range(2)]
        factor_ps = banks[7][:, 256:257]
        K_ADD = CT + 1

        def stat(ch, name):
            return ch.all * K_DVE + (STEPS.index(name) + 1)

        def pe_stat(ch, name):
            return ch.all * K_PE + (PE_STEPS.index(name) + 1)

        def act_stat(ch, name):
            return ch.all * K_ACT + (ACT_STEPS.index(name) + 1)

        def old(ch):
            if isinstance(ch.c, int) and ch.c < 2:
                return None
            return Chunk(l, ch.c - 2, ch.par, ch.half - 1)

        with nc.Block() as block:
            @block.sync
            def _(sp):
                regs = [sp.alloc_register(f"sp_window_{l}_{k}") for k in range(QT)]

                def body(ch, prev, nxt):
                    if ch is None:
                        return
                    p, was = ch.par, old(ch)
                    if was:
                        sp.wait_ge(s["products"], was.quarters(NQ - 1))
                        sp.wait_ge(s["onehot"], was.quarters(NQ - 1))
                    sp.dma_start(ix[p][:, :], edge_ix[:, bass.ds(ch.c, 1), :].rearrange("p a k -> p (a k)")).then_inc(s["ix_in"][p], 16)
                    if was:
                        sp.wait_ge(s["stat_steps"], stat(was, STEPS[-1]))
                    sp.dma_start(em[p][:, :], edge_masks[bass.ds(ch.c * CT, CT), :].rearrange("t (a m) -> t a m", a=1).to_broadcast([CT, H, M_W])).then_inc(s["masks_in"][p], 16)
                    sp.dma_start(tm[p][:, :], tile_masks[bass.ds(ch.c, 1), :].to_broadcast([H, R_W])).then_inc(s["masks_in"][p], 16)
                    for q in range(NQ):
                        if was:
                            sp.wait_ge(s["q_spread"], was.quarters(q))
                        sp.load(regs, windows[0:1, bass.ds(ch.c * CT + q * QT, QT)])
                        for k in range(QT):
                            w = sp.snap(regs[k], min_val=0, max_val=N)
                            sp.dma_start(qw[p][:, q * QT + k, :], queries[bass.ds(w, TE), :]).then_inc(s["queries_in"][p][q], 16)

                over_chunks(sp, l, body)

            @block.gpsimd
            def _(pool):
                def body(ch, prev, nxt):
                    if ch is None:
                        return
                    p, was = ch.par, old(ch)
                    pool.wait_ge(s["ix_in"][p], (ch.use + 1) * 16)
                    pool.nop(nofuse=True)
                    for q in range(NQ):
                        if was:
                            pool.wait_ge(s["messages"], was.quarters(q))
                            pool.nop(nofuse=True)
                        for j in range(q * QT, (q + 1) * QT):
                            pool.indirect_dma_start(kv[p][:, j, :], None, table[:, :],
                                                    bass.IndirectOffsetOnAxis(ap=ix[p][:, j:j + 1], axis=0)).then_inc(s["rows_in"][p][q], 16)

                over_chunks(pool, l, body)

            @block.scalar
            def _(act):
                a = nc.scalar

                def build(ch, q):
                    if q == 0:
                        act.wait_ge(s["ix_in"][ch.par], (ch.use + 1) * 16)
                    was = old(ch)
                    if was:
                        act.wait_ge(s["summed"], was.quarters(q))
                    rel = ix[ch.par][:, CT:2 * CT].bitcast(F32)
                    wait(act, s["onehot"], ch.quarters(q) - 2)
                    for k in range(QT):
                        j = q * QT + k
                        last = a.activation(dist[q % 2][:, k, :], ramp[:, :], ACT.Abs, bias=rel[:, j:j + 1], scale=-1.0)
                    last.then_inc(s["onehot_dist"], 1)
                    act.wait_ge(s["onehot_dist"], ch.quarters(q))
                    a.activation(onehot[ch.par][:, q * QT:(q + 1) * QT, :], dist[q % 2][:, :, :], ACT.Relu, bias=1.0, scale=-1.0).then_inc(s["onehot"], 1)

                def turned(ch, q, first):
                    act.wait_ge(s["onehot_t"], ch.quarters(q))
                    if not first:
                        act.wait_ge(s["q_spread"], ch.quarters(q - 2))
                    a.activation(onehot_t[q % 2][:, :, :], st_ps[q % 2][:, :].rearrange("p (k n) -> p k n", k=QT), ACT.Copy).then_inc(s["onehot_t_sb"], 1)

                def body(ch, prev, nxt):
                    if ch and not prev:
                        for q in range(3):
                            build(ch, q)
                        turned(ch, 0, True)
                        turned(ch, 1, True)
                    if ch:
                        turned(ch, 2, False)
                        build(ch, 3)
                    if prev:
                        act.wait_ge(s["stat_steps"], stat(prev, "alpha_arg"))
                        a.activation(alpha[:, :], alpha_arg[:, :], ACT.Exp).then_inc(s["act_steps"], 1)
                        a.activation(wave["ea"][:, :], wave["shift"][:, :], ACT.Exp).then_inc(s["act_steps"], 1)
                    if ch:
                        turned(ch, 3, False)
                    if prev:
                        act.wait_ge(s["pe_steps"], pe_stat(prev, "weights_e"))
                        a.activation(wts_e[:, :], wts_ps, ACT.Copy).then_inc(s["act_steps"], 1)
                    if nxt:
                        build(nxt, 0)
                        build(nxt, 1)
                        turned(nxt, 0, False)
                        build(nxt, 2)
                        turned(nxt, 1, False)

                over_chunks(act, l, body)

            @block.tensor
            def _(pe):
                t_ = nc.tensor

                def turn(ch, q, first):
                    pe.wait_ge(s["onehot"], ch.quarters(q))
                    if not first:
                        pe.wait_ge(s["onehot_t_sb"], ch.quarters(q - 2))
                    for k in range(QT):
                        last = t_.transpose(st_ps[q % 2][:, k * TE:(k + 1) * TE], onehot[ch.par][:, q * QT + k, :], ident[:, :])
                    last.then_inc(s["onehot_t"], 1)

                def spread(ch, q, first):
                    pe.wait_ge(s["onehot_t_sb"], ch.quarters(q))
                    pe.wait_ge(s["queries_in"][ch.par][q], (ch.use + 1) * (16 * QT))
                    if not first:
                        pe.wait_ge(s["products"], ch.quarters(q - 2))
                    for k in range(QT):
                        last = t_.matmul(qe_ps[q % 2][:, k * D:(k + 1) * D], onehot_t[q % 2][:, k, :], qw[ch.par][:, q * QT + k, :], start=True, stop=True)
                    last.then_inc(s["q_spread"], 1)

                def sum_messages(ch, q, first):
                    pe.wait_ge(s["messages"], ch.quarters(q))
                    if not first:
                        done = (ch.all * K_ADD + (1 + (q - 1) * QT)) if q >= 2 else ((ch.all - 1) * K_ADD + (1 + (q + NQ - 1) * QT))
                        pe.wait_ge(s["added"], done)
                    for k in range(QT):
                        last = t_.matmul(ag_ps[q % 2][:, k * TE:(k + 1) * TE], msg[q % 2][:, k, :], onehot[ch.par][:, q * QT + k, :], start=True, stop=True)
                    last.then_inc(s["summed"], 1)

                def to_rows(ch, i, step):
                    pe.wait_ge(s["stat_steps"], stat(ch, step))
                    t_.matmul(rows_ps[i], head_sel[:, :], ends[i][:, :, :].rearrange("p a t -> p (a t)"), start=True, stop=True).then_inc(s["pe_steps"], 1)

                def to_cols(ch, i, step):
                    pe.wait_ge(s["stat_steps"], stat(ch, step))
                    t_.matmul(cols_ps[i], head_rep[:, :], sides[i][:, :, :].rearrange("p a t -> p (a t)"), start=True, stop=True).then_inc(s["pe_steps"], 1)

                def body(ch, prev, nxt):
                    alone = prev is None
                    tail = ch is None
                    start = alone
                    if ch and alone:
                        turn(ch, 0, True)
                        turn(ch, 1, True)
                        spread(ch, 0, True)
                    if prev:
                        pe.wait_ge(s["scores"], prev.quarters(NQ - 1))
                        t_.transpose(scores_t, scores[:, :], ident[:, :]).then_inc(s["pe_steps"], 1)
                    if ch:
                        turn(ch, 2, False)
                        spread(ch, 1, alone)
                    if prev:
                        to_rows(prev, 0, "max_edges")
                        to_cols(prev, 0, "max_right")
                    if ch:
                        turn(ch, 3, False)
                        spread(ch, 2, False)
                    if prev:
                        to_rows(prev, 1, "sum_edges")
                        to_cols(prev, 1, "sum_right")
                        pe.wait_ge(s["stat_steps"], stat(prev, "acc_factor"))
                        t_.matmul(factor_ps, head_exp[:, :], factor[:, :], start=True, stop=True).then_inc(s["pe_steps"], 1)
                        t_.transpose(wts_ps, wave["wts"][:, :], ident[:, :]).then_inc(s["pe_steps"], 1)
                        first = isinstance(prev.c, int) and prev.c == 0
                        sum_messages(prev, 0, first)
                        sum_messages(prev, 1, first)
                    if nxt:
                        turn(nxt, 0, False)
                    if ch:
                        spread(ch, 3, False)
                    if prev:
                        sum_messages(prev, 2, False)
                    if nxt:
                        turn(nxt, 1, False)
                        spread(nxt, 0, False)
                    if prev:
                        sum_messages(prev, 3, False)

                over_chunks(pe, l, body)

            @block.vector
            def _(dve):
                v = nc.vector
                regs = [dve.alloc_register(f"dve_window_{l}_{k}") for k in range(QT)]
                for i in range(2):
                    v.memset(state[i][:, 0:1], -BIG if i == 0 else 0.0).then_inc(s["carry_init"], 1)

                def product(ch, q):
                    dve.wait_ge(s["rows_in"][ch.par][q], (ch.use + 1) * (16 * QT))
                    dve.wait_ge(s["q_spread"], ch.quarters(q))
                    wait(dve, s["scores"], ch.quarters(q) - 1)
                    v.tensor_tensor(prod[:, :, :], kv[ch.par][:, q * QT:(q + 1) * QT, 0:D], qe_ps[q % 2][:, :].rearrange("p (k f) -> p k f", k=QT), ALU.mult).then_inc(s["products"], 1)

                def score(ch, q):
                    dve.wait_ge(s["products"], ch.quarters(q))
                    v.tensor_reduce(scores[:, q * QT * H:(q + 1) * QT * H], prod[:, :, :].rearrange("p k (h d) -> p (k h) d", h=H), X_AXIS, ALU.add).then_inc(s["scores"], 1)

                def message(ch, q):
                    w = wts_e[:, q * QT * H:(q + 1) * QT * H].rearrange("p (k h) -> p k h", h=H).unsqueeze(3).to_broadcast([P, QT, H, HD])
                    v.tensor_tensor(msg[q % 2][:, :, :].rearrange("p k (h d) -> p k h d", h=H),
                                    kv[ch.par][:, q * QT:(q + 1) * QT, D:2 * D].rearrange("p k (h d) -> p k h d", h=H), w, ALU.mult).then_inc(s["messages"], 1)

                def add(ch, q):
                    dve.load(regs, windows[0:1, bass.ds(ch.c * CT + q * QT, QT)])
                    dve.wait_ge(s["summed"], ch.quarters(q))
                    for k in range(QT):
                        w = dve.snap(regs[k], min_val=0, max_val=N)
                        dve.wait_ge(s["added"], ch.all * K_ADD + (1 + q * QT + k))
                        v.tensor_tensor(acc[:, bass.ds(w, TE)], acc[:, bass.ds(w, TE)], ag_ps[q % 2][:, k * TE:(k + 1) * TE], ALU.add).then_inc(s["added"], 1)

                def carried(ch):
                    dve.load(regs[0:1], windows[0:1, bass.ds(ch.c * CT, 1)])
                    w = dve.snap(regs[0], min_val=0, max_val=N)
                    dve.wait_ge(s["pe_steps"], pe_stat(ch, "factor_cols"))
                    if not (isinstance(ch.c, int) and ch.c == 0):
                        dve.wait_ge(s["added"], ch.all * K_ADD)
                    v.tensor_tensor(acc[:, bass.ds(w, 1)], acc[:, bass.ds(w, 1)], factor_ps, ALU.mult).then_inc(s["added"], 1)

                def stats(ch):
                    m, t = em[ch.par], tm[ch.par]
                    W = wave
                    f = R_W // 2

                    def step(name, ins, after=None):
                        ins().then_inc(s["stat_steps"], 1)

                    def own(name):
                        dve.wait_ge(s["stat_steps"], stat(ch, name))

                    def rev(ap, n=TE, o=0):
                        return ap[:, o + n - 1:(o - 1 if o else None):-1]

                    fwd_a, bwd_a = m[:, M_A:M_A + TE], m[:, M_A + 1:M_A + TE + 1]

                    dve.wait_ge(s["carry_init"], ch.all + 2 * (l + 1))
                    dve.wait_ge(s["masks_in"][ch.par], (ch.use + 1) * 32)
                    dve.wait_ge(s["pe_steps"], pe_stat(ch, "scores_t"))
                    v.tensor_tensor_scan(W["max_f"][:, :], fwd_a, scores_t, -BIG, ALU.add, ALU.max).then_inc(s["stat_steps"], 1)
                    own("run_max_fwd")
                    v.tensor_tensor_scan(rev(W["max_b"]), rev(m, TE, M_A + 1), rev(W["max_f"]), -BIG, ALU.add, ALU.max).then_inc(s["stat_steps"], 1)
                    own("run_max")
                    v.tensor_tensor(ends[0][:, :, :], W["max_b"][:, 0:TE:TE - 1].unsqueeze(2).to_broadcast([P, 2, CT]),
                                    tile_sel[:, :].unsqueeze(1).to_broadcast([P, 2, CT]), ALU.mult).then_inc(s["stat_steps"], 1)
                    yield
                    dve.wait_ge(s["pe_steps"], pe_stat(ch, "max_rows"))
                    v.tensor_tensor_scan(state[0][:, 1:CT + 1], t[:, R_A:R_A + CT], rows_ps[0][:, CT:2 * CT], state[0][:, 0:1], ALU.add, ALU.max).then_inc(s["stat_steps"], 1)
                    own("max_carry")
                    v.tensor_tensor(sides[0][:, 0, :], state[0][:, 0:CT], t[:, R_C:R_C + CT], ALU.add).then_inc(s["stat_steps"], 1)
                    v.tensor_tensor(right[0][:, :], t[:, R_CR:R_CR + CT], rows_ps[0][:, 1:CT + 1], ALU.add).then_inc(s["stat_steps"], 1)
                    own("max_right_in")
                    v.tensor_tensor(right[0][:, :], right[0][:, :], state[0][:, 1:CT + 1], ALU.max).then_inc(s["stat_steps"], 1)
                    own("max_right_top")
                    v.tensor_tensor_scan(rev(sides[0][:, 1, :], CT), rev(t, CT, R_AR), rev(right[0], CT), -BIG, ALU.add, ALU.max).then_inc(s["stat_steps"], 1)
                    v.tensor_copy(state[0][:, 0:1], state[0][:, CT:CT + 1]).then_inc(s["stat_steps"], 1)
                    yield
                    dve.wait_ge(s["pe_steps"], pe_stat(ch, "max_cols"))
                    v.tensor_tensor(picked[0][:, :, :], cols_ps[0].rearrange("p (a t) -> p a t", a=2), tile_sel[:, :].unsqueeze(1).to_broadcast([P, 2, CT]), ALU.mult).then_inc(s["stat_steps"], 1)
                    own("max_pick")
                    v.tensor_reduce(cols[0][:, :], picked[0][:, :, :], X_AXIS, ALU.add).then_inc(s["stat_steps"], 1)
                    own("max_picked")
                    v.scalar_tensor_tensor(W["max_1"][:, :], m[:, M_C:M_C + TE], cols[0][:, 0:1], W["max_b"][:, :], ALU.add, ALU.max).then_inc(s["stat_steps"], 1)
                    own("max_first")
                    v.scalar_tensor_tensor(W["max_2"][:, :], m[:, M_D:M_D + TE], cols[0][:, 1:2], W["max_1"][:, :], ALU.add, ALU.max).then_inc(s["stat_steps"], 1)
                    own("max_all")
                    v.tensor_tensor(W["shift"][:, :], scores_t, W["max_2"][:, :], ALU.subtract).then_inc(s["stat_steps"], 1)
                    v.tensor_tensor(alpha_arg[:, :], cols[0][0:H, 0:1], W["max_2"][0:H, 0:1], ALU.subtract).then_inc(s["stat_steps"], 1)
                    yield
                    dve.wait_ge(s["act_steps"], act_stat(ch, "exps"))
                    v.tensor_tensor_scan(W["sum_f"][:, :], m[:, M_AM:M_AM + TE], W["ea"][:, :], 0.0, ALU.mult, ALU.add).then_inc(s["stat_steps"], 1)
                    own("run_sum_fwd")
                    v.tensor_tensor_scan(rev(W["sum_b"]), rev(m, TE, M_A + 1), rev(W["sum_f"]), 0.0, ALU.add, ALU.max).then_inc(s["stat_steps"], 1)
                    own("run_sum")
                    v.tensor_tensor(ends[1][:, :, :], W["sum_b"][:, 0:TE:TE - 1].unsqueeze(2).to_broadcast([P, 2, CT]),
                                    tile_sel[:, :].unsqueeze(1).to_broadcast([P, 2, CT]), ALU.mult).then_inc(s["stat_steps"], 1)
                    v.tensor_tensor(state[1][:, 0:1], state[1][:, 0:1], alpha[:, :], ALU.mult).then_inc(s["stat_steps"], 1)
                    yield
                    dve.wait_ge(s["pe_steps"], pe_stat(ch, "sum_rows"))
                    own("sum_carry_in")
                    v.tensor_tensor_scan(state[1][:, 1:CT + 1], t[:, f + R_A:f + R_A + CT], rows_ps[1][:, CT:2 * CT], state[1][:, 0:1], ALU.mult, ALU.add).then_inc(s["stat_steps"], 1)
                    own("sum_carry")
                    v.tensor_tensor(sides[1][:, 0, :], state[1][:, 0:CT], t[:, f + R_C:f + R_C + CT], ALU.mult).then_inc(s["stat_steps"], 1)
                    v.tensor_tensor(right[1][:, :], t[:, f + R_CR:f + R_CR + CT], rows_ps[1][:, 1:CT + 1], ALU.mult).then_inc(s["stat_steps"], 1)
                    own("sum_right_in")
                    v.tensor_tensor(right[1][:, :], right[1][:, :], state[1][:, 1:CT + 1], ALU.add).then_inc(s["stat_steps"], 1)
                    own("sum_right_top")
                    v.tensor_tensor_scan(rev(sides[1][:, 1, :], CT), rev(t, CT, f + R_AR), rev(right[1], CT), 0.0, ALU.mult, ALU.max).then_inc(s["stat_steps"], 1)
                    yield
                    dve.wait_ge(s["pe_steps"], pe_stat(ch, "sum_cols"))
                    v.tensor_tensor(picked[1][:, :, :], cols_ps[1].rearrange("p (a t) -> p a t", a=2), tile_sel[:, :].unsqueeze(1).to_broadcast([P, 2, CT]), ALU.mult).then_inc(s["stat_steps"], 1)
                    own("sum_pick")
                    v.tensor_reduce(cols[1][:, :], picked[1][:, :, :], X_AXIS, ALU.add).then_inc(s["stat_steps"], 1)
                    own("sum_picked")
                    v.scalar_tensor_tensor(W["sum_1"][:, :], m[:, M_CM:M_CM + TE], cols[1][:, 0:1], W["sum_b"][:, :], ALU.mult, ALU.add).then_inc(s["stat_steps"], 1)
                    own("sum_first")
                    v.scalar_tensor_tensor(W["sum_2"][:, :], m[:, M_DM:M_DM + TE], cols[1][:, 1:2], W["sum_1"][:, :], ALU.mult, ALU.max).then_inc(s["stat_steps"], 1)
                    own("sum_all")
                    v.reciprocal(W["inv"][:, :], W["sum_2"][:, :]).then_inc(s["stat_steps"], 1)
                    own("sum_inverse")
                    v.tensor_tensor(W["wts"][:, :], W["ea"][:, :], W["inv"][:, :], ALU.mult).then_inc(s["stat_steps"], 1)
                    v.tensor_tensor(factor[:, :], state[1][:, 0:1], W["inv"][0:H, 0:1], ALU.mult).then_inc(s["stat_steps"], 1)
                    own("acc_factor")
                    v.tensor_copy(state[1][:, 0:1], state[1][:, CT:CT + 1]).then_inc(s["carry_init"], 1)
                    yield

                def body(ch, prev, nxt):
                    parts = stats(prev) if prev else iter(range(6))
                    if ch:
                        product(ch, 0)
                    next(parts)
                    if ch:
                        score(ch, 0)
                    next(parts)
                    if ch:
                        product(ch, 1)
                    next(parts)
                    if ch:
                        score(ch, 1)
                    next(parts)
                    if ch:
                        product(ch, 2)
                    next(parts)
                    if ch:
                        score(ch, 2)
                    next(parts)
                    if prev:
                        carried(prev)
                        dve.wait_ge(s["act_steps"], act_stat(prev, "weights_sb"))
                        message(prev, 0)
                        message(prev, 1)
                        add(prev, 0)
                        message(prev, 2)
                        add(prev, 1)
                    if ch:
                        product(ch, 3)
                        score(ch, 3)
                    if prev:
                        message(prev, 3)
                        add(prev, 2)
                        add(prev, 3)

                over_chunks(dve, l, body)


def node_out(nc, l, s, banks, x_t, acc, ntype_b, ident, Wa, skip, x, out):
    last_layer = l == L - 1
    with ExitStack() as ctx:
        def sb(name, shape, dt=F32):
            return ctx.enter_context(nc.sbuf_tensor(f"out_{name}_{l}", shape, dt))

        wa = sb("wa", [P, NT, D])
        gate_in = sb("gate_in", [P, NT])
        gate_exp = sb("gate_exp", [P, NT])
        gate = sb("gate", [P, NT])
        rest = sb("rest", [P, NT])
        w_h = sb("w_h", [P, NT, D])
        w_x = sb("w_x", [P, NT, D])
        masked = [sb(f"masked{i}", [P, 2 * NT, NB]) for i in range(2)]
        fresh = sb("fresh", [P, NB])
        rows = sb("x_rows", [P, D])
        resid = sb("resid", [P, D])
        stats = sb("stats", [P, 6])
        mv = sb("mv", [P, 2])
        eps = sb("eps", [P, 1])
        root = sb("root", [P, 1])
        inv = sb("inv", [P, 1])
        normed = sb("normed", [P, D])
        mix_ps, row_ps = banks[0:2], banks[2:4]
        used = NBLK if not last_layer else -(-N // NB)

        with nc.Block() as block:
            @block.sync
            def _(sp):
                sp.dma_start(wa[:, :, :], Wa[l].rearrange("t k n -> k t n")).then_inc(s["wa_in"], 16)
                sp.dma_start(gate_in[:, :], skip[l:l + 1, :].to_broadcast([P, NT])).then_inc(s["wa_in"], 16)
                if last_layer:
                    def tile(i, n):
                        sp.wait_ge(s["resid"], i)
                        sp.dma_start(rows[0:n, :], x[bass.ds(i * P, n), :]).then_inc(s["x_rows"], 16)
                        sp.wait_ge(s["normed"], i + 1)
                        sp.dma_start(out[bass.ds(i * P, n), :], normed[0:n, :]).then_inc(s["stored"], 16)
                    sp.dma_start(rows[:, :], x[0:P, :]).then_inc(s["x_rows"], 16)
                    sp.wait_ge(s["normed"], 1)
                    sp.dma_start(out[0:P, :], normed[:, :]).then_inc(s["stored"], 16)
                    with sp.Fori(1, XT - 1) as i:
                        tile(i, P)
                    tile(XT - 1, XR)
                    sp.wait_ge(s["stored"], 16 * XT)

            @block.vector
            def _(dve):
                v = nc.vector
                v.memset(eps[:, :], EPS).then_inc(s["gates"], 1)
                g = l * 4 + 1
                dve.wait_ge(s["neg_exp"], l + 1)
                v.tensor_scalar(gate_exp[:, :], gate_exp[:, :], 1.0, None, ALU.add).then_inc(s["gates"], 1)
                dve.wait_ge(s["gates"], g + 1)
                v.reciprocal(gate[:, :], gate_exp[:, :]).then_inc(s["gates"], 1)
                dve.wait_ge(s["gates"], g + 2)
                v.tensor_scalar(rest[:, :], gate[:, :], -1.0, 1.0, ALU.mult, ALU.add).then_inc(s["gates"], 1)
                dve.wait_ge(s["gates"], g + 3)
                for t in range(NT):
                    v.tensor_scalar(w_h[:, t, :], wa[:, t, :], gate[:, t:t + 1], None, ALU.mult).then_inc(s["wa_scaled"], 1)
                    v.tensor_scalar(w_x[:, t, :], ident[:, :], rest[:, t:t + 1], None, ALU.mult).then_inc(s["wa_scaled"], 1)

                def mask(b, i):
                    for k, of in enumerate((acc, x_t)):
                        for t in range(NT):
                            v.scalar_tensor_tensor(masked[i][:, k * NT + t, :], ntype_b[:, bass.ds(b * NB, NB)], float(t), of[:, bass.ds(b * NB, NB)],
                                                   ALU.is_equal, ALU.mult).then_inc(s["h_masked"], 1)

                def norm(i, k, n):
                    st = s["norm_step"]
                    dve.wait_ge(s["x_rows"], (i + 1) * 16)
                    dve.wait_ge(s["rows_t"], (i + 1))
                    wait(dve, s["normed"], i)
                    v.tensor_tensor(resid[0:n, :], rows[0:n, :], row_ps[k][0:n, 0:D], ALU.add).then_inc(s["resid"], 1)
                    dve.wait_ge(s["resid"], (i + 1))
                    v.bn_stats(stats[0:n, :], resid[0:n, :]).then_inc(st, 1)
                    dve.wait_ge(st, i * 3 + 1)
                    dve.nop(nofuse=True)
                    v.bn_aggr(mv[0:n, :], stats[0:n, :]).then_inc(st, 1)
                    dve.wait_ge(s["root"], (i + 1))
                    v.reciprocal(inv[0:n, :], root[0:n, :]).then_inc(st, 1)
                    dve.wait_ge(st, i * 3 + 3)
                    if not (isinstance(i, int) and i == 0):
                        dve.wait_ge(s["stored"], i * 16)
                    v.tensor_scalar(normed[0:n, :], resid[0:n, :], mv[0:n, 0:1], inv[0:n, 0:1], ALU.subtract, ALU.mult).then_inc(s["normed"], 1)

                if not last_layer:
                    mask(0, 0)
                    with dve.Fori(0, (NBLK - 1) // 2) as b:
                        dve.wait_ge(s["mixed"], b * 2 + 1)
                        mask(b * 2 + 1, 1)
                        dve.wait_ge(s["mixed"], b * 2 + 2)
                        mask(b * 2 + 2, 0)
                else:
                    m0 = NBLK
                    mask(0, 0)
                    with dve.Fori(0, (NBLK - 1) // 2) as b:
                        for i in range(2):
                            dve.wait_ge(s["mixed"], b * 2 + (m0 + i + 1))
                            mask(b * 2 + (i + 1), 1 - i)
                            for k in range(2):
                                norm(b * 4 + (i * 2 + k), k, P)
                    norm(XT - 1, 0, XR)

            @block.scalar
            def _(act):
                a = nc.scalar
                act.wait_ge(s["wa_in"], 32 * (l + 1))
                a.activation(gate_exp[:, :], gate_in[:, :], ACT.Exp, scale=-1.0).then_inc(s["neg_exp"], 1)

                def block_of(b, i, full=True):
                    act.wait_ge(s["mixed"], b + (l * NBLK + 1))
                    if not last_layer:
                        a.activation(x_t[:, bass.ds(b * NB, NB)], mix_ps[i][:, 0:NB], ACT.Copy).then_inc(s["x_new"], 1)
                        return
                    if not (isinstance(b, int) and b == 0):
                        act.wait_ge(s["rows_t"], b * 2)
                    a.activation(fresh[:, :], mix_ps[i][:, 0:NB], ACT.Copy).then_inc(s["x_new"], 1)
                    for k in range(2 if full else 1):
                        t = b * 2 + k
                        n = P if full else XR
                        act.wait_ge(s["norm_step"], t * 3 + 2)
                        a.activation(root[0:n, :], mv[0:n, 1:2], ACT.Sqrt, bias=eps[0:n, 0:1]).then_inc(s["root"], 1)

                block_of(0, 0)
                with act.Fori(0, (NBLK - 3) // 2) as b:
                    block_of(b * 2 + 1, 1)
                    block_of(b * 2 + 2, 0)
                block_of(NBLK - 2, 1)
                block_of(NBLK - 1, 0, False)

            @block.tensor
            def _(pe):
                t_ = nc.tensor
                pe.wait_ge(s["wa_scaled"], 2 * NT * (l + 1))

                def block_of(b, i, full=True):
                    pe.wait_ge(s["h_masked"], b * (2 * NT) + (l * NBLK + 1) * 2 * NT)
                    if not (isinstance(b, int) and b < 2 and l == 0):
                        pe.wait_ge(s["x_new"], b + (l * NBLK - 1))
                    for k in range(2 * NT):
                        w = w_h[:, k, :] if k < NT else w_x[:, k - NT, :]
                        last = t_.matmul(mix_ps[i][:, 0:NB], w, masked[i][:, k, :], start=(k == 0), stop=(k == 2 * NT - 1))
                    last.then_inc(s["mixed"], 1)
                    if last_layer:
                        pe.wait_ge(s["x_new"], b + (l * NBLK + 1))
                        if not (isinstance(b, int) and b == 0):
                            pe.wait_ge(s["resid"], b * 2)
                        for k in range(2 if full else 1):
                            n = P if full else XR
                            t_.transpose(row_ps[k][0:n, 0:D], fresh[:, k * P:k * P + n], ident[:, :]).then_inc(s["rows_t"], 1)

                block_of(0, 0)
                with pe.Fori(0, (NBLK - 3) // 2) as b:
                    block_of(b * 2 + 1, 1)
                    block_of(b * 2 + 2, 0)
                block_of(NBLK - 2, 1)
                block_of(NBLK - 1, 0, False)


_INS = ["x", "src", "dst", "edge_type_6", "node_type_3", "L0_gnn_Wk", "L0_gnn_Wq", "L0_gnn_Wv", "L0_gnn_Wa",
        "L0_gnn_pri", "L0_gnn_Watt", "L0_gnn_Wmsg", "L0_gnn_skip"]


def kernel(**inputs):
    import numpy as _np
    import concourse.bacc as _bacc
    from concourse import mybir as _mybir
    from concourse.bass_utils import run_bass_kernel_spmd as _run

    nc = _bacc.Bacc("TRN2", target_bir_lowering=False, num_devices=1)
    arrays, args = {}, []
    for name in _INS:
        a = _np.ascontiguousarray(inputs[name])
        arrays[f"in_{name}"] = a
        args.append(nc.dram_tensor(f"in_{name}", a.shape, _mybir.dt.from_np(a.dtype), kind="ExternalInput").ap())
    result = nc.dram_tensor("out_x", (N, D), _mybir.dt.float32, kind="ExternalOutput").ap()
    hgt_kernel(nc, *args, result)
    r = _run(nc, [arrays], core_ids=[0])
    return r.results[0]["out_x"]
```

```python
from contextlib import ExitStack

import concourse.bass as bass
from concourse import mybir

ALU = mybir.AluOpType
ACT = mybir.ActivationFunctionType
F32 = mybir.dt.float32
BF16 = mybir.dt.bfloat16
I32 = mybir.dt.int32
X_AXIS = mybir.AxisListType.X

P = 128
N, D, H = 6250, 128, 8
HD = D // H
NT, ET, L = 3, 6, 2
E = 206250
EPS = 1e-5
BIG = 2.0 ** 100

TE = P
CT = P // H
QT = 4
NQ = CT // QT
NCH = -(-E // (TE * CT))
TILES = NCH * CT
NG = -(-TILES // P)
FULL = E // TE
REST = E - FULL * TE
GL = TILES - (NG - 1) * P
NPAD = 6400
NB = 256
NBLK = NPAD // NB
XT = -(-N // P)
XR = N - (XT - 1) * P
ROW = 2 * D

M_A, M_C, M_D, M_AM, M_CM, M_DM, M_W = 0, 129, 257, 385, 513, 641, 770
R_A, R_C, R_CR, R_AR, R_W = 0, 16, 32, 48, 128

STEPS = [
    "run_max_fwd", "run_max", "max_edges", "max_carry", "max_left", "max_right_in", "max_right_top",
    "max_right", "max_carry_on", "max_pick", "max_picked", "max_first", "max_all", "shifted",
    "alpha_arg", "run_sum_fwd", "run_sum", "sum_edges", "sum_carry_in", "sum_carry", "sum_left",
    "sum_right_in", "sum_right_top", "sum_right", "sum_pick", "sum_picked", "sum_first", "sum_all",
    "sum_inverse", "weights", "acc_factor",
]
K_DVE = len(STEPS)
FEW = ("max_left", "sum_left", "sum_pick", "sum_picked", "sum_first", "sum_all", "max_first", "sum_right_top")
PE_STEPS = ["max_rows", "max_cols", "sum_rows", "sum_cols", "weights_e", "factor_cols"]
K_PE = len(PE_STEPS)
ACT_STEPS = ["alpha", "exps", "weights_sb"]
K_ACT = len(ACT_STEPS)


class Chunk:

    def __init__(self, l, turn, k):
        self.l, self.turn, self.k = l, turn, k
        self.c = turn * 6 + k
        self.par, self.tri = k % 2, k % 3
        self.all = l * NCH + self.c
        self.use = l * -(-(NCH - self.par) // 2) + (turn * 3 + k // 2)
        self.use3 = l * -(-(NCH - self.tri) // 3) + (turn * 2 + k // 3)

    def quarters(self, q):
        return self.all * NQ + (q + 1)

    def before(self, n):
        if isinstance(self.turn, int) and self.c < n:
            return None
        return Chunk(self.l, self.turn, self.k - n)


def wait(eng, sem, value):
    if not (isinstance(value, int) and value <= 0):
        eng.wait_ge(sem, value)


def over_chunks(eng, l, body):
    def step(turn, k):
        chunks = [Chunk(l, turn, n) for n in (k, k - 1, k - 2, k + 1)]
        if isinstance(turn, int):
            chunks = [ch if 0 <= ch.c < NCH else None for ch in chunks]
        body(*chunks)

    peeled = 3
    turns = (NCH - 1 - peeled) // 6
    for k in range(peeled):
        step(0, k)
    with eng.Fori(0, turns) as turn:
        for k in range(6):
            step(turn, peeled + k)
    for c in range(peeled + 6 * turns, NCH + 2):
        step(0, c)


def hgt_kernel(nc, x, src, dst, etype, ntype, Wk, Wq, Wv, Wa, pri, Watt, Wmsg, skip, out):
    table = nc.dram_tensor("kv_table", [NPAD * ET, ROW], F32).ap()
    queries = nc.dram_tensor("queries", [NPAD, D], F32).ap()
    dst_pad = nc.dram_tensor("dst_pad", [TILES, TE], I32).ap()
    places = nc.dram_tensor("places", [TILES, TE], BF16).ap()
    edge_masks = nc.dram_tensor("edge_masks", [TILES, M_W], BF16).ap()
    tile_masks = nc.dram_tensor("tile_masks", [NCH, R_W], F32).ap()

    with ExitStack() as kept:
        def sb(name, shape, dt=F32, ctx=kept):
            return ctx.enter_context(nc.sbuf_tensor(name, shape, dt))

        def sem(name):
            return kept.enter_context(nc.semaphore(name))

        banks = [kept.enter_context(nc.psum_tensor(f"bank{i}", [P, 512], F32)) for i in range(8)]

        x_t = sb("x_t", [P, NPAD])
        acc = sb("acc", [P, NPAD])
        ntype_b = sb("ntype_b", [P, NPAD], BF16)
        windows = sb("windows", [1, TILES], I32)
        edge_ix = sb("edge_ix", [P, NCH, 2 * CT], I32)
        ident = sb("ident", [P, P])
        ramp = sb("ramp", [P, TE])
        tile_sel = sb("tile_sel", [P, CT])
        head_sel = sb("head_sel", [P, H])
        head_rep = sb("head_rep", [H, P])
        head_exp = sb("head_exp", [H, P])
        head_sum = sb("head_sum", [P, 2 * P - H])
        lane = sb("lane", [P, 1])

        prepare(nc, sb, sem, banks, x, src, dst, etype, ntype, x_t, ntype_b, edge_ix, windows, ident,
                ramp, tile_sel, head_sel, head_rep, head_exp, head_sum, lane, dst_pad, places, edge_masks,
                tile_masks)
        node_sems = {n: sem(n) for n in (
            "w_in", "bd_zero", "bd_scaled", "masked", "tables_kv", "kvq_done", "kv_sb", "q_sb", "tables_mm", "evac_act",
            "evac_dve", "query_out", "acc_zero")}
        node_sems["table_out"] = [sem(f"table_out_{i}") for i in range(2)]
        edge_sems = edge_semaphores(sem)
        out_sems = {n: sem(n) for n in (
            "wa_in", "neg_exp", "gates", "wa_scaled", "h_masked", "mixed", "x_new", "x_rows", "rows_t",
            "resid", "stats", "aggr", "root", "norm_step", "normed", "stored")}
        for l in range(L):
            tables(nc, l, node_sems, banks, x_t, acc, ntype_b, Wk, Wq, Wv, pri, Watt, Wmsg, table, queries)
            edges(nc, l, edge_sems, banks, acc, edge_ix, windows, ident, ramp, tile_sel, head_sel,
                  head_rep, head_exp, head_sum, lane, table, queries, places, edge_masks, tile_masks)
            node_out(nc, l, out_sems, banks, x_t, acc, ntype_b, ident, Wa, skip, x, out)


def prepare(nc, sb, sem, banks, x, src, dst, etype, ntype, x_t, ntype_b, edge_ix, windows, ident, ramp,
            tile_sel, head_sel, head_rep, head_exp, head_sum, lane, dst_pad, places, edge_masks, tile_masks):
    with ExitStack() as ctx:
        dst_i = sb("dst_i", [P, NG, TE], I32, ctx)
        src_i = sb("src_i", [P, NG, TE], I32, ctx)
        et_i = sb("et_i", [P, NG, TE], I32, ctx)
        dst_f = sb("dst_f", [P, NG, TE], F32, ctx)
        row_f = sb("row_f", [P, NG, TE], F32, ctx)
        rel_f = sb("rel_f", [P, NG, TE], F32, ctx)
        rel_h = sb("rel_h", [P, NG, TE], BF16, ctx)
        ntype_i = sb("ntype_i", [P, N], I32, ctx)
        masks = sb("masks", [P, NG, M_W], BF16, ctx)
        x_in = sb("x_in", [P, XT, D], F32, ctx)
        first_i = sb("first_i", [NCH, CT], I32, ctx)
        last_i = sb("last_i", [NCH, CT + 1], I32, ctx)
        goes_on = sb("goes_on", [NCH, CT], F32, ctx)
        whole = sb("whole", [NCH, CT], F32, ctx)
        rowm = sb("rowm", [NCH, R_W], F32, ctx)

        filled = sem("filled")
        edges_in = sem("edges_in")
        x_loaded = sem("x_loaded")
        ntype_in = sem("ntype_in")
        dst_padded = sem("dst_padded")
        ends_in = sem("ends_in")
        windows_in = sem("windows_in")
        ident_step = sem("ident_step")
        consts = sem("consts")
        prep = sem("prep")
        turned = sem("turned")
        put = sem("put")
        rows_made = sem("rows_made")
        masks_out = sem("masks_out")
        sels = sem("sels")
        places_made = sem("places_made")

        def tiles_view(a, g0, g1):
            return a[g0 * P * TE:g1 * P * TE].rearrange("(g p e) -> p g e", p=P, e=TE)

        with nc.Block() as block:
            @block.sync
            def _(sp):
                sp.dma_start(x_in[:, 0:XT - 1, :], x[0:(XT - 1) * P, :].rearrange("(b p) f -> p b f", p=P)).then_inc(x_loaded, 16)
                sp.dma_start(x_in[0:XR, XT - 1, :], x[(XT - 1) * P:N, :]).then_inc(x_loaded, 16)
                sp.wait_ge(filled, 4)
                g = (NG - 1) * P
                for tile, a in ((dst_i, dst), (src_i, src), (et_i, etype)):
                    sp.dma_start(tile[:, 0:NG - 1, :], tiles_view(a, 0, NG - 1)).then_inc(edges_in, 16)
                    sp.dma_start(tile[0:FULL - g, NG - 1, :], a[g * TE:FULL * TE].rearrange("(p e) -> p e", e=TE)).then_inc(edges_in, 16)
                    sp.dma_start(tile[FULL - g:FULL - g + 1, NG - 1, 0:REST], a[FULL * TE:E].rearrange("(p e) -> p e", p=1)).then_inc(edges_in, 16)
                sp.dma_start(ntype_i[:, :], ntype.rearrange("(a n) -> a n", a=1).to_broadcast([P, N])).then_inc(ntype_in, 16)
                sp.wait_ge(edges_in, 16 * 9)
                sp.dma_start(dst_pad[0:g, :].rearrange("(g p) e -> p g e", p=P), dst_i[:, 0:NG - 1, :]).then_inc(dst_padded, 16)
                sp.dma_start(dst_pad[g:TILES, :], dst_i[0:GL, NG - 1, :]).then_inc(dst_padded, 16)
                sp.wait_ge(dst_padded, 32)
                with nc.allow_non_contiguous_dma(reason="one node of each tile, once"):
                    by_chunk = dst_pad.rearrange("(c t) e -> c t e", t=CT)
                    sp.dma_start(first_i[:, :], by_chunk[:, :, 0]).then_inc(ends_in, 16)
                    sp.dma_start(last_i[:, 1:CT + 1], by_chunk[:, :, TE - 1]).then_inc(ends_in, 16)
                    sp.dma_start(last_i[1:NCH, 0:1], by_chunk[0:NCH - 1, CT - 1:CT, TE - 1]).then_inc(ends_in, 16)
                    sp.dma_start(windows[0:1, :], dst_pad[:, 0:1].rearrange("t a -> a t")).then_inc(windows_in, 16)
                sp.wait_ge(prep, 15)
                sp.dma_start(edge_masks[0:g, :].rearrange("(g p) m -> p g m", p=P), masks[:, 0:NG - 1, :]).then_inc(masks_out, 16)
                sp.dma_start(edge_masks[g:TILES, :], masks[0:GL, NG - 1, :]).then_inc(masks_out, 16)
                sp.wait_ge(places_made, 1)
                sp.dma_start(places[0:g, :].rearrange("(g p) m -> p g m", p=P), rel_h[:, 0:NG - 1, :]).then_inc(masks_out, 16)
                sp.dma_start(places[g:TILES, :], rel_h[0:GL, NG - 1, :]).then_inc(masks_out, 16)
                sp.wait_ge(rows_made, 9)
                sp.dma_start(tile_masks[:, :], rowm[:, :]).then_inc(masks_out, 16)
                sp.wait_ge(masks_out, 80)
                sp.wait_ge(windows_in, 16)

            @block.gpsimd
            def _(pool):
                pool.memset(dst_i[:, :, :], N).then_inc(filled, 1)
                pool.memset(src_i[:, :, :], 0).then_inc(filled, 1)
                pool.memset(et_i[:, :, :], 0).then_inc(filled, 1)
                pool.memset(last_i[:, :], -1).then_inc(filled, 1)
                pool.memset(ident[:, :], 0.0).then_inc(ident_step, 1)
                pool.memset(head_rep[:, :], 0.0).then_inc(ident_step, 1)
                pool.memset(head_exp[:, :], 0.0).then_inc(ident_step, 1)
                pool.memset(head_sum[:, :], 0.0).then_inc(ident_step, 1)
                pool.wait_ge(ident_step, 4)
                mid = head_sum[:, P - H:P]
                pool.memset(mid, 1.0).then_inc(ident_step, 1)
                pool.affine_select(out=ident[:, :], in_=ident[:, :], compare_op=ALU.not_equal, fill=1.0,
                                   base=0, pattern=[[-1, P]], channel_multiplier=1).then_inc(consts, 1)
                v = head_rep[:, :].rearrange("p (t h) -> p t h", h=H)
                pool.affine_select(out=v, in_=v, compare_op=ALU.not_equal, fill=1.0, base=0,
                                   pattern=[[0, CT], [-1, H]], channel_multiplier=1).then_inc(consts, 1)
                v = head_exp[:, :].rearrange("p (h d) -> p h d", h=H)
                pool.affine_select(out=v, in_=v, compare_op=ALU.not_equal, fill=1.0, base=0,
                                   pattern=[[-1, H], [0, HD]], channel_multiplier=1).then_inc(consts, 1)
                pool.wait_ge(ident_step, 5)
                pool.affine_select(out=mid, in_=mid, compare_op=ALU.is_ge, fill=0.0, base=0,
                                   pattern=[[-HD, H]], channel_multiplier=1).then_inc(ident_step, 1)
                pool.wait_ge(ident_step, 6)
                pool.affine_select(out=mid, in_=mid, compare_op=ALU.is_ge, fill=0.0, base=HD - 1,
                                   pattern=[[HD, H]], channel_multiplier=-1).then_inc(ident_step, 1)
                pool.iota(lane[:, :], [[0, 1]], base=0, channel_multiplier=-1,
                          allow_small_or_imprecise_dtypes=True).then_inc(ident_step, 1)
                pool.iota(ramp[:, :], [[1, TE]], base=0, channel_multiplier=0,
                          allow_small_or_imprecise_dtypes=True).then_inc(consts, 1)
                pool.memset(x_t[:, N:NPAD], 0.0).then_inc(consts, 1)
                pool.memset(ntype_b[:, N:NPAD], 0.0).then_inc(consts, 1)

            @block.vector
            def _(dve):
                v = nc.vector
                dve.wait_ge(consts, 1)
                v.tensor_reduce(tile_sel[:, :], ident[:, :].rearrange("p (t h) -> p t h", h=H), X_AXIS, ALU.add).then_inc(sels, 1)
                v.tensor_reduce(head_sel[:, :], ident[:, :].rearrange("p (t h) -> p h t", h=H), X_AXIS, ALU.add).then_inc(sels, 1)
                dve.wait_ge(edges_in, 16 * 9)
                v.tensor_copy(dst_f[:, :, :], dst_i[:, :, :]).then_inc(prep, 1)
                v.scalar_tensor_tensor(row_f[:, :, :], src_i[:, :, :], float(ET), et_i[:, :, :], ALU.mult, ALU.add).then_inc(prep, 1)
                dve.wait_ge(prep, 1)
                first = dst_f[:, :, 0:1].to_broadcast([P, NG, TE])
                last = dst_f[:, :, TE - 1:TE].to_broadcast([P, NG, TE])
                d = dst_f[:, :, :]
                v.tensor_tensor(rel_f[:, :, :], d, first, ALU.subtract).then_inc(prep, 1)
                dve.wait_ge(prep, 3)
                v.tensor_copy(rel_h[:, :, :], rel_f[:, :, :]).then_inc(places_made, 1)
                dve.wait_ge(ntype_in, 16)
                v.tensor_copy(ntype_b[:, 0:N], ntype_i[:, :]).then_inc(places_made, 1)
                v.memset(masks[:, :, M_A:M_A + TE + 1], -BIG).then_inc(prep, 1)
                v.memset(masks[:, :, M_AM:M_AM + 1], 0.0).then_inc(prep, 1)
                v.memset(masks[:, :, M_DM + TE:M_W], 0.0).then_inc(prep, 1)
                v.tensor_tensor(masks[:, :, M_AM + 1:M_AM + TE], dst_f[:, :, 1:TE], dst_f[:, :, 0:TE - 1], ALU.is_equal).then_inc(prep, 1)
                v.tensor_tensor(masks[:, :, M_CM:M_CM + TE], d, first, ALU.is_equal).then_inc(prep, 1)
                v.tensor_tensor(masks[:, :, M_DM:M_DM + TE], d, last, ALU.is_equal).then_inc(prep, 1)
                dve.wait_ge(prep, 9)
                for k, (to, of, n) in enumerate(((M_A + 1, M_AM + 1, TE - 1), (M_C, M_CM, TE), (M_D, M_DM, TE))):
                    v.tensor_scalar(masks[:, :, to:to + n], masks[:, :, of:of + n], 1.0, BIG, ALU.subtract, ALU.mult).then_inc(prep, 2)
                dve.wait_ge(ends_in, 48)
                v.memset(rowm[:, :], 0.0).then_inc(rows_made, 1)
                v.tensor_tensor(goes_on[:, :], first_i[:, :], last_i[:, 0:CT], ALU.is_equal).then_inc(rows_made, 1)
                v.tensor_tensor(whole[:, :], first_i[:, :], last_i[:, 1:CT + 1], ALU.is_equal).then_inc(rows_made, 1)
                dve.wait_ge(rows_made, 3)
                f = R_W // 2
                v.tensor_tensor(rowm[:, f + R_A:f + R_A + CT], goes_on[:, :], whole[:, :], ALU.mult).then_inc(rows_made, 1)
                v.tensor_copy(rowm[:, f + R_C:f + R_C + CT], goes_on[:, :]).then_inc(rows_made, 1)
                v.tensor_copy(rowm[:, f + R_CR:f + R_CR + CT - 1], goes_on[:, 1:CT]).then_inc(rows_made, 1)
                v.tensor_tensor(rowm[:, f + R_AR:f + R_AR + CT - 1], goes_on[:, 1:CT], whole[:, 1:CT], ALU.mult).then_inc(rows_made, 1)
                dve.wait_ge(rows_made, 7)
                v.tensor_scalar(rowm[:, 0:f], rowm[:, f:2 * f], 1.0, BIG, ALU.subtract, ALU.mult).then_inc(rows_made, 2)

            @block.tensor
            def _(pe):
                pe.wait_ge(consts, 1)
                pe.wait_ge(x_loaded, 32)
                for g in range(NT_GROUPS):
                    if g >= 2:
                        pe.wait_ge(put, g - 1)
                    for k, b in enumerate(range(g * 4, min(g * 4 + 4, XT))):
                        n = P if b < XT - 1 else XR
                        last = nc.tensor.transpose(banks[g % 2][:, k * P:k * P + n], x_in[0:n, b, :], ident[0:n, 0:n])
                    last.then_inc(turned, 1)
                pe.wait_ge(prep, 3)
                for g in range(NG):
                    pe.wait_ge(put, NT_GROUPS + g - 1)
                    n = P if g < NG - 1 else GL
                    bank = banks[(NT_GROUPS + g) % 2]
                    nc.tensor.transpose(bank[:, 0:n], row_f[0:n, g, :], ident[0:n, 0:n])
                    nc.tensor.transpose(bank[:, P:P + n], rel_f[0:n, g, :], ident[0:n, 0:n]).then_inc(turned, 1)

            @block.scalar
            def _(act):
                a = nc.scalar
                for g in range(NT_GROUPS):
                    act.wait_ge(turned, g + 1)
                    n = min(N, (g + 1) * 4 * P) - g * 4 * P
                    a.activation(x_t[:, g * 4 * P:g * 4 * P + n], banks[g % 2][:, 0:n], ACT.Copy).then_inc(put, 1)
                for g in range(NG):
                    act.wait_ge(turned, NT_GROUPS + g + 1)
                    n = P if g < NG - 1 else GL
                    c0, c1 = g * P // CT, (g * P + n) // CT
                    bank = banks[(NT_GROUPS + g) % 2]
                    a.activation(edge_ix[:, c0:c1, 0:CT], bank[:, 0:n].rearrange("p (c t) -> p c t", t=CT), ACT.Copy)
                    a.activation(edge_ix[:, c0:c1, CT:2 * CT].bitcast(F32), bank[:, P:P + n].rearrange("p (c t) -> p c t", t=CT), ACT.Copy).then_inc(put, 1)


NT_GROUPS = -(-XT // 4)


def tables(nc, l, s, banks, x_t, acc, ntype_b, Wk, Wq, Wv, pri, Watt, Wmsg, table, queries):
    HALF = ET // 2 * D
    with ExitStack() as ctx:
        def sb(name, shape, dt=F32):
            return ctx.enter_context(nc.sbuf_tensor(f"tab_{name}_{l}", shape, dt))

        wk, wq, wv = sb("wk", [P, NT, D]), sb("wq", [P, NT, D]), sb("wv", [P, NT, D])
        bd = sb("bd", [P, 2, ET, D])
        prior = sb("prior", [P, ET])
        masked = sb("masked", [P, NT, NB])
        kv_t = sb("kv_t", [P, 2, NB])
        q_rows = sb("q_rows", [P, 2, D])
        rows = sb("rows", [P, 2, ET, 2, D])
        kv_ps, q_ps, tab_ps = banks[0], banks[1], banks[2:6]
        loads = 3 + 1 + 2 * H

        def blocks(b):
            return l * NBLK + b

        with nc.Block() as block:
            @block.sync
            def _(sp):
                for w, a in ((wk, Wk), (wv, Wv), (wq, Wq)):
                    sp.dma_start(w[:, :, :], a[l].rearrange("t k n -> k t n")).then_inc(s["w_in"], 16)
                with nc.allow_non_contiguous_dma(reason="48 values"):
                    sp.dma_start(prior[:, :], pri[l].rearrange("h (a t) -> h a t", a=1).to_broadcast([H, HD, ET])).then_inc(s["w_in"], 16)
                sp.wait_ge(s["bd_zero"], l + 1)
                for i, a in ((0, Watt), (1, Wmsg)):
                    for h in range(H):
                        r = slice(h * HD, (h + 1) * HD)
                        sp.dma_start(bd[r, i, :, r], a[l, h].rearrange("t d o -> d t o")).then_inc(s["w_in"], 16)
                with sp.Fori(0, NBLK) as b:
                    for i in range(2):
                        if i == 0:
                            sp.wait_ge(s["q_sb"], (blocks(b) + 1))
                            sp.dma_start(queries[bass.ds(b * NB, NB), :].rearrange("(i p) f -> p i f", p=P), q_rows[:, :, :]).then_inc(s["query_out"], 16)
                        sp.wait_ge(s["evac_act"], blocks(b) * 4 + 2 * (i + 1))
                        sp.wait_ge(s["evac_dve"], blocks(b) * 4 + 2 * (i + 1))
                        sp.dma_start(table[bass.ds(b * (NB * ET) + i * (P * ET), P * ET), :].rearrange("(p t) f -> p (t f)", t=ET),
                                     rows[:, i, :, :, :].rearrange("p t k f -> p (t k f)")).then_inc(s["table_out"][i], 16)
                sp.wait_ge(s["query_out"], (l + 1) * NBLK * 16)
                for i in range(2):
                    sp.wait_ge(s["table_out"][i], (l + 1) * NBLK * 16)

            @block.gpsimd
            def _(pool):
                pool.memset(bd[:, :, :, :], 0.0).then_inc(s["bd_zero"], 1)
                pool.memset(acc[:, :], 0.0).then_inc(s["acc_zero"], 1)

            @block.vector
            def _(dve):
                v = nc.vector

                def mask(b):
                    for t in range(NT):
                        v.scalar_tensor_tensor(masked[:, t, :], ntype_b[:, bass.ds(b * NB, NB)], float(t), x_t[:, bass.ds(b * NB, NB)],
                                               ALU.is_equal, ALU.mult).then_inc(s["masked"], 1)

                def evac(b):
                    for i in range(2):
                        for hf in range(2):
                            dve.wait_ge(s["tables_mm"], blocks(b) * 8 + (i * 4 + 2 + hf + 1))
                            if hf == 0:
                                yield i
                            v.tensor_copy(rows[:, i, 3 * hf:3 * hf + 3, 1, :], tab_ps[2 + hf][:, 0:HALF].rearrange("p (t f) -> p t f", f=D)).then_inc(s["evac_dve"], 1)

                mask(0)
                dve.wait_ge(s["w_in"], 16 * loads * (l + 1))
                v.scalar_tensor_tensor(bd[:, 0, :, :], bd[:, 0, :, :], 1.0 / float(HD) ** 0.5, prior[:, :].unsqueeze(2).to_broadcast([P, ET, D]),
                                       ALU.mult, ALU.mult).then_inc(s["bd_scaled"], 1)

                def block_of(b, more, reuse):
                    if more:
                        dve.wait_ge(s["kvq_done"], (blocks(b) + 1))
                        mask(b + 1)
                    for i in evac(b):
                        if reuse:
                            dve.wait_ge(s["table_out"][i], (blocks(b) * 16))

                block_of(0, True, l > 0)
                with dve.Fori(1, NBLK - 1) as b:
                    block_of(b, True, True)
                block_of(NBLK - 1, False, True)

            @block.tensor
            def _(pe):
                t_ = nc.tensor
                pe.wait_ge(s["w_in"], 16 * loads * (l + 1))
                pe.wait_ge(s["bd_scaled"], l + 1)

                def block_of(b, reuse):
                    pe.wait_ge(s["masked"], (blocks(b) + 1) * NT)
                    if reuse:
                        pe.wait_ge(s["q_sb"], blocks(b))
                        pe.wait_ge(s["kv_sb"], blocks(b))
                    for i, w in enumerate((wk, wv)):
                        for t in range(NT):
                            last = t_.matmul(kv_ps[:, i * NB:(i + 1) * NB], w[:, t, :], masked[:, t, :], start=(t == 0), stop=(t == NT - 1))
                    last.then_inc(s["tables_kv"], 1)
                    for i in range(2):
                        for t in range(NT):
                            last = t_.matmul(q_ps[:, i * D:(i + 1) * D], masked[:, t, i * P:(i + 1) * P], wq[:, t, :], start=(t == 0), stop=(t == NT - 1))
                    last.then_inc(s["kvq_done"], 1)
                    pe.wait_ge(s["kv_sb"], (blocks(b) + 1))
                    for i in range(2):
                        for kv in range(2):
                            for hf in range(2):
                                if i == 1:
                                    pe.wait_ge(s["evac_dve" if kv else "evac_act"], blocks(b) * 4 + (hf + 1))
                                elif reuse:
                                    pe.wait_ge(s["evac_dve" if kv else "evac_act"], blocks(b) * 4 - 2 + (hf + 1))
                                t_.matmul(tab_ps[2 * kv + hf][:, 0:HALF], kv_t[:, kv, i * P:(i + 1) * P],
                                          bd[:, kv, 3 * hf:3 * hf + 3, :].rearrange("p t f -> p (t f)"), start=True, stop=True).then_inc(s["tables_mm"], 1)

                block_of(0, l > 0)
                with pe.Fori(1, NBLK) as b:
                    block_of(b, True)

            @block.scalar
            def _(act):
                a = nc.scalar

                def block_of(b, reuse):
                    act.wait_ge(s["tables_kv"], (blocks(b) + 1))
                    if reuse:
                        act.wait_ge(s["tables_mm"], blocks(b) * 8)
                    a.activation(kv_t[:, :, :], kv_ps[:, :].rearrange("p (k n) -> p k n", k=2), ACT.Copy).then_inc(s["kv_sb"], 1)
                    act.wait_ge(s["kvq_done"], (blocks(b) + 1))
                    if reuse:
                        act.wait_ge(s["query_out"], (blocks(b) * 16))
                    a.activation(q_rows[:, :, :], q_ps[:, 0:2 * D].rearrange("p (i f) -> p i f", i=2), ACT.Copy).then_inc(s["q_sb"], 1)
                    for i in range(2):
                        for hf in range(2):
                            act.wait_ge(s["tables_mm"], blocks(b) * 8 + (i * 4 + hf + 1))
                            if hf == 0 and reuse:
                                act.wait_ge(s["table_out"][i], (blocks(b) * 16))
                            a.activation(rows[:, i, 3 * hf:3 * hf + 3, 0, :], tab_ps[hf][:, 0:HALF].rearrange("p (t f) -> p t f", f=D), ACT.Copy).then_inc(s["evac_act"], 1)

                block_of(0, l > 0)
                with act.Fori(1, NBLK) as b:
                    block_of(b, True)


def edge_semaphores(sem):
    one = ["indexed", "onehot_dist", "onehot", "spread_dist", "spread_made", "q_spread", "q_spread_sb", "keys_t", "products",
           "scores", "messages",
           "summed", "added", "stat_steps", "pe_steps", "act_steps", "carry_init"]
    s = {n: sem(n) for n in one}
    for n in ("masks_in", "places_in"):
        s[n] = [sem(f"{n}_{p}") for p in range(2)]
    for n, ring in (("rows_in", 3), ("queries_in", 2)):
        s[n] = [[sem(f"{n}_{p}_{q}") for q in range(NQ)] for p in range(ring)]
    return s


def edges(nc, l, s, banks, acc, edge_ix, windows, ident, ramp, tile_sel, head_sel, head_rep, head_exp,
          head_sum, lane, table, queries, places, edge_masks, tile_masks):
    with ExitStack() as ctx:
        def sb(name, shape, dt=F32):
            return ctx.enter_context(nc.sbuf_tensor(f"edge_{name}_{l}", shape, dt))

        ix = [sb(f"ix{p}", [P, CT], I32) for p in range(3)]
        em = [sb(f"em{p}", [P, M_W], BF16) for p in range(2)]
        tm = [sb(f"tm{p}", [H, R_W]) for p in range(2)]
        pl = [sb(f"pl{p}", [P, CT * TE], BF16) for p in range(2)]
        kv = [sb(f"kv{p}", [P, CT, ROW]) for p in range(3)]
        qw = [sb(f"qw{p}", [P, CT, D]) for p in range(2)]
        onehot = [sb(f"onehot{p}", [P, CT, TE]) for p in range(2)]
        dist = [sb(f"dist{i}", [P, QT, TE], BF16) for i in range(2)]
        spread = [sb(f"spread{i}", [P, QT, TE]) for i in range(2)]
        dist_s = [sb(f"dist_s{i}", [P, QT * TE], BF16) for i in range(2)]
        qe = [sb(f"qe{i}", [P, QT * TE]) for i in range(2)]
        prod = [sb(f"prod{i}", [P, QT * TE]) for i in range(2)]
        msg = sb("msg", [P, CT, D])
        wave = {n: sb(n, [P, TE]) for n in ("fwd", "run", "first", "all", "shift", "ea", "inv", "wts")}
        wts_e = sb("wts_e", [P, P])
        ends = [sb(f"ends{i}", [P, 2, CT]) for i in range(2)]
        picked = [sb(f"picked{i}", [P, 2, CT]) for i in range(2)]
        cols = [sb(f"cols{i}", [P, 2]) for i in range(2)]
        state = [sb(f"state{i}", [H, CT + 1]) for i in range(2)]
        right = [sb(f"right{i}", [H, CT]) for i in range(2)]
        sides = [sb(f"sides{i}", [H, 2, CT]) for i in range(2)]
        alpha_arg = sb("alpha_arg", [H, 1])
        alpha = sb("alpha", [H, 1])
        factor = sb("factor", [H, 1])

        kt_ps, qe_ps, ag_ps, chunk_ps = banks[0:2], banks[2:4], banks[4:6], banks[6:8]

        def scores_t(ch):
            return chunk_ps[ch.par][:, 0:P]

        def wts_ps(ch):
            return chunk_ps[ch.par][:, P:2 * P]

        def rows_ps(ch, i):
            return chunk_ps[ch.par][0:H, 2 * P + 32 * i:2 * P + 32 * i + 2 * CT]

        def cols_ps(ch, i):
            return chunk_ps[ch.par][:, 2 * P + 64 + 32 * i:2 * P + 64 + 32 * i + 2 * CT]

        def factor_ps(ch):
            return chunk_ps[ch.par][:, 3 * P:3 * P + 1]

        K_ADD = CT + 1

        def stat(ch, name):
            return ch.all * K_DVE + (STEPS.index(name) + 1)

        def pe_stat(ch, name):
            return ch.all * K_PE + (PE_STEPS.index(name) + 1)

        def act_stat(ch, name):
            return ch.all * K_ACT + (ACT_STEPS.index(name) + 1)

        with nc.Block() as block:
            @block.sync
            def _(sp):
                regs = [sp.alloc_register(f"sp_window_{l}_{k}") for k in range(QT)]

                def body(ch, prev, older, nxt):
                    if ch is None:
                        return
                    p, was = ch.par, ch.before(2)
                    if was:
                        sp.wait_ge(s["spread_made"], was.quarters(NQ - 1))
                    sp.dma_start(pl[p][:, :], places[bass.ds(ch.c * CT, CT), :].rearrange("(a t) e -> a (t e)", a=1).to_broadcast([P, CT * TE])).then_inc(s["places_in"][p], 16)
                    for q in range(NQ):
                        if was:
                            sp.wait_ge(s["q_spread"], was.quarters(q))
                        sp.load(regs, windows[0:1, bass.ds(ch.c * CT + q * QT, QT)])
                        for k in range(QT):
                            w = sp.snap(regs[k], min_val=0, max_val=N)
                            sp.dma_start(qw[p][:, q * QT + k, :], queries[bass.ds(w, TE), :]).then_inc(s["queries_in"][p][q], 16)
                    if was:
                        sp.wait_ge(s["stat_steps"], stat(was, STEPS[-1]))
                    sp.dma_start(em[p][:, :], edge_masks[bass.ds(ch.c * CT, CT), :].rearrange("t (a m) -> t a m", a=1).to_broadcast([CT, H, M_W])).then_inc(s["masks_in"][p], 16)
                    sp.dma_start(tm[p][:, :], tile_masks[bass.ds(ch.c, 1), :].to_broadcast([H, R_W])).then_inc(s["masks_in"][p], 16)

                over_chunks(sp, l, body)

            @block.gpsimd
            def _(pool):
                def index(ch):
                    was = ch.before(3)
                    if was:
                        pool.wait_ge(s["keys_t"], was.quarters(NQ - 1))
                    pool.tensor_copy(ix[ch.tri][:, :], edge_ix[:, bass.ds(ch.c, 1), 0:CT].rearrange("p a k -> p (a k)")).then_inc(s["indexed"], 1)

                def body(ch, prev, older, nxt):
                    if ch is None:
                        return
                    was = ch.before(3)
                    if not ch.before(1):
                        index(ch)
                    pool.wait_ge(s["indexed"], ch.all + 1)
                    pool.nop(nofuse=True)
                    for q in range(NQ):
                        if was:
                            pool.wait_ge(s["messages"], was.quarters(q))
                            pool.nop(nofuse=True)
                        for j in range(q * QT, (q + 1) * QT):
                            pool.indirect_dma_start(kv[ch.tri][:, j, :], None, table[:, :],
                                                    bass.IndirectOffsetOnAxis(ap=ix[ch.tri][:, j:j + 1], axis=0)).then_inc(s["rows_in"][ch.tri][q], 16)
                        if nxt and q == 1:
                            index(nxt)

                over_chunks(pool, l, body)

            @block.scalar
            def _(act):
                a = nc.scalar

                def build(ch, q):
                    was = ch.before(2)
                    if was:
                        act.wait_ge(s["summed"], was.quarters(q))
                    rel = edge_ix[:, bass.ds(ch.c, 1), CT:2 * CT].rearrange("p a k -> p (a k)").bitcast(F32)
                    wait(act, s["onehot"], ch.quarters(q) - 2)
                    for k in range(QT):
                        j = q * QT + k
                        last = a.activation(dist[q % 2][:, k, :], ramp[:, :], ACT.Abs, bias=rel[:, j:j + 1], scale=-1.0)
                    last.then_inc(s["onehot_dist"], 1)
                    act.wait_ge(s["onehot_dist"], ch.quarters(q))
                    a.activation(onehot[ch.par][:, q * QT:(q + 1) * QT, :], dist[q % 2][:, :, :], ACT.Relu, bias=1.0, scale=-1.0).then_inc(s["onehot"], 1)

                def build_spread(ch, q, first):
                    if q == 0:
                        act.wait_ge(s["places_in"][ch.par], (ch.use + 1) * 16)
                    wait(act, s["spread_made"], ch.quarters(q) - 2)
                    a.activation(dist_s[q % 2][:, :], pl[ch.par][:, q * QT * TE:(q + 1) * QT * TE], ACT.Abs, bias=lane[:, 0:1]).then_inc(s["spread_dist"], 1)
                    act.wait_ge(s["spread_dist"], ch.quarters(q))
                    if not first:
                        act.wait_ge(s["q_spread"], ch.quarters(q) - 2)
                    a.activation(spread[q % 2][:, :, :].rearrange("p k e -> p (k e)"), dist_s[q % 2][:, :], ACT.Relu, bias=1.0, scale=-1.0).then_inc(s["spread_made"], 1)

                def query_out(ch, q, first):
                    act.wait_ge(s["q_spread"], ch.quarters(q))
                    if not first:
                        act.wait_ge(s["products"], ch.quarters(q) - 2)
                    a.activation(qe[q % 2][:, :], qe_ps[q % 2][:, :], ACT.Copy).then_inc(s["q_spread_sb"], 1)

                def body(ch, prev, older, nxt):
                    first = ch is not None and not ch.before(1)
                    if first:
                        build_spread(ch, 0, True)
                        build_spread(ch, 1, True)
                        query_out(ch, 0, True)
                        query_out(ch, 1, True)
                    if ch:
                        build_spread(ch, 2, False)
                    if prev:
                        build(prev, 0)
                    if ch:
                        query_out(ch, 2, False)
                        build_spread(ch, 3, False)
                    if prev:
                        act.wait_ge(s["stat_steps"], stat(prev, "alpha_arg"))
                        a.activation(alpha[:, :], alpha_arg[:, :], ACT.Exp).then_inc(s["act_steps"], 1)
                        a.activation(wave["ea"][:, :], wave["shift"][:, :], ACT.Exp).then_inc(s["act_steps"], 1)
                    if ch:
                        query_out(ch, 3, False)
                    if prev:
                        build(prev, 1)
                    if nxt:
                        build_spread(nxt, 0, False)
                        build_spread(nxt, 1, False)
                    if prev:
                        act.wait_ge(s["pe_steps"], pe_stat(prev, "weights_e"))
                        a.activation(wts_e[:, :], wts_ps(prev), ACT.Copy).then_inc(s["act_steps"], 1)
                    if nxt:
                        query_out(nxt, 0, False)
                    if prev:
                        build(prev, 2)
                    if nxt:
                        query_out(nxt, 1, False)
                    if prev:
                        build(prev, 3)

                over_chunks(act, l, body)

            @block.tensor
            def _(pe):
                t_ = nc.tensor

                def spread_queries(ch, q, first):
                    pe.wait_ge(s["spread_made"], ch.quarters(q))
                    pe.wait_ge(s["queries_in"][ch.par][q], (ch.use + 1) * (16 * QT))
                    if not first:
                        pe.wait_ge(s["q_spread_sb"], ch.quarters(q) - 2)
                    for k in range(QT):
                        last = t_.matmul(qe_ps[q % 2][:, k * TE:(k + 1) * TE], qw[ch.par][:, q * QT + k, :], spread[q % 2][:, k, :], start=True, stop=True)
                    last.then_inc(s["q_spread"], 1)

                def turn_keys(ch, q, first):
                    pe.wait_ge(s["rows_in"][ch.tri][q], (ch.use3 + 1) * (16 * QT))
                    if not first:
                        pe.wait_ge(s["products"], ch.quarters(q) - 2)
                    for k in range(QT):
                        last = t_.transpose(kt_ps[q % 2][:, k * TE:(k + 1) * TE], kv[ch.tri][:, q * QT + k, 0:D], ident[:, :])
                    last.then_inc(s["keys_t"], 1)

                def sum_heads(ch, q):
                    pe.wait_ge(s["products"], ch.quarters(q))
                    for k in range(QT):
                        j = q * QT + k
                        last = t_.matmul(scores_t(ch), head_sum[:, P - H - H * j:2 * P - H - H * j], prod[q % 2][:, k * TE:(k + 1) * TE],
                                         start=(j == 0), stop=(j == CT - 1))
                    last.then_inc(s["scores"], 1)

                def sum_messages(ch, q, first):
                    pe.wait_ge(s["messages"], ch.quarters(q))
                    pe.wait_ge(s["onehot"], ch.quarters(q))
                    if not first:
                        done = (ch.all * K_ADD + (1 + (q - 1) * QT)) if q >= 2 else ((ch.all - 1) * K_ADD + (1 + (q + NQ - 1) * QT))
                        pe.wait_ge(s["added"], done)
                    for k in range(QT):
                        last = t_.matmul(ag_ps[q % 2][:, k * TE:(k + 1) * TE], msg[:, q * QT + k, :], onehot[ch.par][:, q * QT + k, :], start=True, stop=True)
                    last.then_inc(s["summed"], 1)

                def to_rows(ch, i, step):
                    pe.wait_ge(s["stat_steps"], stat(ch, step))
                    t_.matmul(rows_ps(ch, i), head_sel[:, :], ends[i][:, :, :].rearrange("p a t -> p (a t)"), start=True, stop=True).then_inc(s["pe_steps"], 1)

                def to_cols(ch, i, step):
                    pe.wait_ge(s["stat_steps"], stat(ch, step))
                    t_.matmul(cols_ps(ch, i), head_rep[:, :], sides[i][:, :, :].rearrange("p a t -> p (a t)"), start=True, stop=True).then_inc(s["pe_steps"], 1)

                def body(ch, prev, older, nxt):
                    first = ch is not None and not ch.before(1)
                    if first:
                        for q in range(2):
                            spread_queries(ch, q, True)
                            turn_keys(ch, q, True)
                    if prev:
                        to_rows(prev, 0, "max_edges")
                    if ch:
                        spread_queries(ch, 2, False)
                        turn_keys(ch, 2, False)
                        sum_heads(ch, 0)
                    if prev:
                        to_cols(prev, 0, "max_right")
                    if older:
                        sum_messages(older, 2, False)
                    if ch:
                        sum_heads(ch, 1)
                        spread_queries(ch, 3, False)
                        turn_keys(ch, 3, False)
                    if older:
                        sum_messages(older, 3, False)
                    if prev:
                        to_rows(prev, 1, "sum_edges")
                    if ch:
                        sum_heads(ch, 2)
                    if prev:
                        to_cols(prev, 1, "sum_right")
                    if ch:
                        sum_heads(ch, 3)
                    if nxt:
                        spread_queries(nxt, 0, False)
                        turn_keys(nxt, 0, False)
                    if prev:
                        pe.wait_ge(s["stat_steps"], stat(prev, "weights"))
                        t_.transpose(wts_ps(prev), wave["wts"][:, :], ident[:, :]).then_inc(s["pe_steps"], 1)
                        pe.wait_ge(s["stat_steps"], stat(prev, "acc_factor"))
                        pe.wait_ge(s["act_steps"], act_stat(prev, "weights_sb"))
                        t_.matmul(factor_ps(prev), head_exp[:, :], factor[:, :], start=True, stop=True).then_inc(s["pe_steps"], 1)
                    if nxt:
                        spread_queries(nxt, 1, False)
                        turn_keys(nxt, 1, False)
                    if prev:
                        begun = not prev.before(1)
                        sum_messages(prev, 0, begun)
                        sum_messages(prev, 1, begun)

                over_chunks(pe, l, body)

            @block.vector
            def _(dve):
                v = nc.vector
                regs = [dve.alloc_register(f"dve_window_{l}_{k}") for k in range(CT + 1)]
                for i in range(2):
                    v.memset(state[i][:, 0:1], -BIG if i == 0 else 0.0).then_inc(s["carry_init"], 1)

                def product(ch, q):
                    dve.wait_ge(s["keys_t"], ch.quarters(q))
                    dve.wait_ge(s["q_spread_sb"], ch.quarters(q))
                    wait(dve, s["scores"], ch.quarters(q) - 2)
                    v.tensor_tensor(prod[q % 2][:, :], kt_ps[q % 2][:, :], qe[q % 2][:, :], ALU.mult).then_inc(s["products"], 1)

                def message(ch, q):
                    w = wts_e[:, q * QT * H:(q + 1) * QT * H].rearrange("p (k h) -> p k h", h=H).unsqueeze(3).to_broadcast([P, QT, H, HD])
                    was = ch.quarters(q) - NQ
                    wait(dve, s["summed"], was)
                    v.tensor_tensor(msg[:, q * QT:(q + 1) * QT, :].rearrange("p k (h d) -> p k h d", h=H),
                                    kv[ch.tri][:, q * QT:(q + 1) * QT, D:2 * D].rearrange("p k (h d) -> p k h d", h=H), w, ALU.mult).then_inc(s["messages"], 1)

                def add(ch, j, at):
                    q, k = j // QT, j % QT
                    if k == 0:
                        dve.wait_ge(s["summed"], ch.quarters(q))
                    dve.wait_ge(s["added"], ch.all * K_ADD + (1 + j))
                    v.tensor_tensor(acc[:, bass.ds(at[j], TE)], acc[:, bass.ds(at[j], TE)], ag_ps[q % 2][:, k * TE:(k + 1) * TE], ALU.add).then_inc(s["added"], 1)

                def adds(ch):
                    at = [dve.snap(r, min_val=0, max_val=N) for r in regs[0:CT]]
                    for j in range(CT):
                        yield add(ch, j, at)

                def carried(ch):
                    w = dve.snap(regs[CT], min_val=0, max_val=N)
                    dve.wait_ge(s["pe_steps"], pe_stat(ch, "factor_cols"))
                    if ch.before(1):
                        dve.wait_ge(s["added"], ch.all * K_ADD)
                    v.tensor_tensor(acc[:, bass.ds(w, 1)], acc[:, bass.ds(w, 1)], factor_ps(ch), ALU.mult).then_inc(s["added"], 1)

                def stats(ch, more):
                    m, t = em[ch.par], tm[ch.par]
                    W = wave
                    f = R_W // 2

                    def own(name):
                        if STEPS.index(name) < STEPS.index("sum_inverse") and name not in FEW:
                            next(more, None)
                        dve.wait_ge(s["stat_steps"], stat(ch, name))

                    def rev(ap, n=TE, o=0):
                        return ap[:, o + n - 1:(o - 1 if o else None):-1]

                    fwd_a = m[:, M_A:M_A + TE]

                    dve.wait_ge(s["carry_init"], ch.all + 2 * (l + 1))
                    dve.wait_ge(s["masks_in"][ch.par], (ch.use + 1) * 32)
                    dve.wait_ge(s["scores"], ch.quarters(NQ - 1))
                    v.tensor_tensor_scan(W["fwd"][:, :], fwd_a, scores_t(ch), -BIG, ALU.add, ALU.max).then_inc(s["stat_steps"], 1)
                    own("run_max_fwd")
                    v.tensor_tensor_scan(rev(W["run"]), rev(m, TE, M_A + 1), rev(W["fwd"]), -BIG, ALU.add, ALU.max).then_inc(s["stat_steps"], 1)
                    own("run_max")
                    v.tensor_tensor(ends[0][:, :, :], W["run"][:, 0:TE:TE - 1].unsqueeze(2).to_broadcast([P, 2, CT]),
                                    tile_sel[:, :].unsqueeze(1).to_broadcast([P, 2, CT]), ALU.mult).then_inc(s["stat_steps"], 1)
                    yield
                    dve.wait_ge(s["pe_steps"], pe_stat(ch, "max_rows"))
                    v.tensor_tensor_scan(state[0][:, 1:CT + 1], t[:, R_A:R_A + CT], rows_ps(ch, 0)[:, CT:2 * CT], state[0][:, 0:1], ALU.add, ALU.max).then_inc(s["stat_steps"], 1)
                    own("max_carry")
                    v.tensor_tensor(sides[0][:, 0, :], state[0][:, 0:CT], t[:, R_C:R_C + CT], ALU.add).then_inc(s["stat_steps"], 1)
                    v.tensor_tensor(right[0][:, :], t[:, R_CR:R_CR + CT], rows_ps(ch, 0)[:, 1:CT + 1], ALU.add).then_inc(s["stat_steps"], 1)
                    own("max_right_in")
                    v.tensor_tensor(right[0][:, :], right[0][:, :], state[0][:, 1:CT + 1], ALU.max).then_inc(s["stat_steps"], 1)
                    own("max_right_top")
                    v.tensor_tensor_scan(rev(sides[0][:, 1, :], CT), rev(t, CT, R_AR), rev(right[0], CT), -BIG, ALU.add, ALU.max).then_inc(s["stat_steps"], 1)
                    v.tensor_copy(state[0][:, 0:1], state[0][:, CT:CT + 1]).then_inc(s["stat_steps"], 1)
                    yield
                    dve.wait_ge(s["pe_steps"], pe_stat(ch, "max_cols"))
                    v.tensor_tensor(picked[0][:, :, :], cols_ps(ch, 0).rearrange("p (a t) -> p a t", a=2), tile_sel[:, :].unsqueeze(1).to_broadcast([P, 2, CT]), ALU.mult).then_inc(s["stat_steps"], 1)
                    own("max_pick")
                    v.tensor_reduce(cols[0][:, :], picked[0][:, :, :], X_AXIS, ALU.add).then_inc(s["stat_steps"], 1)
                    own("max_picked")
                    v.scalar_tensor_tensor(W["first"][:, :], m[:, M_C:M_C + TE], cols[0][:, 0:1], W["run"][:, :], ALU.add, ALU.max).then_inc(s["stat_steps"], 1)
                    own("max_first")
                    v.scalar_tensor_tensor(W["all"][:, :], m[:, M_D:M_D + TE], cols[0][:, 1:2], W["first"][:, :], ALU.add, ALU.max).then_inc(s["stat_steps"], 1)
                    own("max_all")
                    v.tensor_tensor(W["shift"][:, :], scores_t(ch), W["all"][:, :], ALU.subtract).then_inc(s["stat_steps"], 1)
                    v.tensor_tensor(alpha_arg[:, :], cols[0][0:H, 0:1], W["all"][0:H, 0:1], ALU.subtract).then_inc(s["stat_steps"], 1)
                    yield
                    dve.wait_ge(s["act_steps"], act_stat(ch, "exps"))
                    v.tensor_tensor_scan(W["fwd"][:, :], m[:, M_AM:M_AM + TE], W["ea"][:, :], 0.0, ALU.mult, ALU.add).then_inc(s["stat_steps"], 1)
                    own("run_sum_fwd")
                    v.tensor_tensor_scan(rev(W["run"]), rev(m, TE, M_A + 1), rev(W["fwd"]), 0.0, ALU.add, ALU.max).then_inc(s["stat_steps"], 1)
                    own("run_sum")
                    v.tensor_tensor(ends[1][:, :, :], W["run"][:, 0:TE:TE - 1].unsqueeze(2).to_broadcast([P, 2, CT]),
                                    tile_sel[:, :].unsqueeze(1).to_broadcast([P, 2, CT]), ALU.mult).then_inc(s["stat_steps"], 1)
                    v.tensor_tensor(state[1][:, 0:1], state[1][:, 0:1], alpha[:, :], ALU.mult).then_inc(s["stat_steps"], 1)
                    yield
                    dve.wait_ge(s["pe_steps"], pe_stat(ch, "sum_rows"))
                    own("sum_carry_in")
                    v.tensor_tensor_scan(state[1][:, 1:CT + 1], t[:, f + R_A:f + R_A + CT], rows_ps(ch, 1)[:, CT:2 * CT], state[1][:, 0:1], ALU.mult, ALU.add).then_inc(s["stat_steps"], 1)
                    own("sum_carry")
                    v.tensor_tensor(sides[1][:, 0, :], state[1][:, 0:CT], t[:, f + R_C:f + R_C + CT], ALU.mult).then_inc(s["stat_steps"], 1)
                    v.tensor_tensor(right[1][:, :], t[:, f + R_CR:f + R_CR + CT], rows_ps(ch, 1)[:, 1:CT + 1], ALU.mult).then_inc(s["stat_steps"], 1)
                    own("sum_right_in")
                    v.tensor_tensor(right[1][:, :], right[1][:, :], state[1][:, 1:CT + 1], ALU.add).then_inc(s["stat_steps"], 1)
                    own("sum_right_top")
                    v.tensor_tensor_scan(rev(sides[1][:, 1, :], CT), rev(t, CT, f + R_AR), rev(right[1], CT), 0.0, ALU.mult, ALU.max).then_inc(s["stat_steps"], 1)
                    yield
                    dve.wait_ge(s["pe_steps"], pe_stat(ch, "sum_cols"))
                    v.tensor_tensor(picked[1][:, :, :], cols_ps(ch, 1).rearrange("p (a t) -> p a t", a=2), tile_sel[:, :].unsqueeze(1).to_broadcast([P, 2, CT]), ALU.mult).then_inc(s["stat_steps"], 1)
                    own("sum_pick")
                    v.tensor_reduce(cols[1][:, :], picked[1][:, :, :], X_AXIS, ALU.add).then_inc(s["stat_steps"], 1)
                    own("sum_picked")
                    v.scalar_tensor_tensor(W["first"][:, :], m[:, M_CM:M_CM + TE], cols[1][:, 0:1], W["run"][:, :], ALU.mult, ALU.add).then_inc(s["stat_steps"], 1)
                    own("sum_first")
                    v.scalar_tensor_tensor(W["all"][:, :], m[:, M_DM:M_DM + TE], cols[1][:, 1:2], W["first"][:, :], ALU.mult, ALU.max).then_inc(s["stat_steps"], 1)
                    own("sum_all")
                    v.reciprocal(W["inv"][:, :], W["all"][:, :]).then_inc(s["stat_steps"], 1)
                    own("sum_inverse")
                    v.tensor_tensor(W["wts"][:, :], W["ea"][:, :], W["inv"][:, :], ALU.mult).then_inc(s["stat_steps"], 1)
                    v.tensor_tensor(factor[:, :], state[1][:, 0:1], W["inv"][0:H, 0:1], ALU.mult).then_inc(s["stat_steps"], 1)
                    own("acc_factor")
                    v.tensor_copy(state[1][:, 0:1], state[1][:, CT:CT + 1]).then_inc(s["carry_init"], 1)
                    yield

                def body(ch, prev, older, nxt):
                    if older and prev:
                        dve.load(regs, windows[0:1, bass.ds(older.c * CT, CT + 1)])
                    elif older:
                        dve.load(regs[0:CT], windows[0:1, bass.ds(older.c * CT, CT)])
                    elif prev:
                        dve.load(regs[CT:], windows[0:1, bass.ds(prev.c * CT, 1)])
                    more = adds(older) if older else iter(())
                    parts = stats(prev, more) if prev else iter(range(6))
                    for part in range(6):
                        next(parts)
                        if ch and part < NQ:
                            product(ch, part)
                    for _ in more:
                        pass
                    if prev:
                        dve.wait_ge(s["act_steps"], act_stat(prev, "weights_sb"))
                        for q in range(NQ):
                            message(prev, q)
                        carried(prev)

                over_chunks(dve, l, body)


def node_out(nc, l, s, banks, x_t, acc, ntype_b, ident, Wa, skip, x, out):
    last_layer = l == L - 1
    with ExitStack() as ctx:
        def sb(name, shape, dt=F32):
            return ctx.enter_context(nc.sbuf_tensor(f"out_{name}_{l}", shape, dt))

        wa = sb("wa", [P, NT, D])
        gate_in = sb("gate_in", [P, NT])
        gate_exp = sb("gate_exp", [P, NT])
        gate = sb("gate", [P, NT])
        rest = sb("rest", [P, NT])
        w_h = sb("w_h", [P, NT, D])
        w_x = sb("w_x", [P, NT, D])
        masked = [sb(f"masked{i}", [P, 2 * NT, NB]) for i in range(2)]
        fresh = sb("fresh", [P, NB])
        rows = sb("x_rows", [P, D])
        resid = sb("resid", [P, D])
        stats = sb("stats", [P, 6])
        mv = sb("mv", [P, 2])
        eps = sb("eps", [P, 1])
        root = sb("root", [P, 1])
        inv = sb("inv", [P, 1])
        normed = sb("normed", [P, D])
        mix_ps, row_ps = banks[0:2], banks[2:4]
        used = NBLK if not last_layer else -(-N // NB)

        with nc.Block() as block:
            @block.sync
            def _(sp):
                sp.dma_start(wa[:, :, :], Wa[l].rearrange("t k n -> k t n")).then_inc(s["wa_in"], 16)
                sp.dma_start(gate_in[:, :], skip[l:l + 1, :].to_broadcast([P, NT])).then_inc(s["wa_in"], 16)
                if last_layer:
                    def tile(i, n):
                        sp.wait_ge(s["resid"], i)
                        sp.dma_start(rows[0:n, :], x[bass.ds(i * P, n), :]).then_inc(s["x_rows"], 16)
                        sp.wait_ge(s["normed"], i + 1)
                        sp.dma_start(out[bass.ds(i * P, n), :], normed[0:n, :]).then_inc(s["stored"], 16)
                    sp.dma_start(rows[:, :], x[0:P, :]).then_inc(s["x_rows"], 16)
                    sp.wait_ge(s["normed"], 1)
                    sp.dma_start(out[0:P, :], normed[:, :]).then_inc(s["stored"], 16)
                    with sp.Fori(1, XT - 1) as i:
                        tile(i, P)
                    tile(XT - 1, XR)
                    sp.wait_ge(s["stored"], 16 * XT)

            @block.vector
            def _(dve):
                v = nc.vector
                v.memset(eps[:, :], EPS).then_inc(s["gates"], 1)
                g = l * 4 + 1
                dve.wait_ge(s["neg_exp"], l + 1)
                v.tensor_scalar(gate_exp[:, :], gate_exp[:, :], 1.0, None, ALU.add).then_inc(s["gates"], 1)
                dve.wait_ge(s["gates"], g + 1)
                v.reciprocal(gate[:, :], gate_exp[:, :]).then_inc(s["gates"], 1)
                dve.wait_ge(s["gates"], g + 2)
                v.tensor_scalar(rest[:, :], gate[:, :], -1.0, 1.0, ALU.mult, ALU.add).then_inc(s["gates"], 1)
                dve.wait_ge(s["gates"], g + 3)
                for t in range(NT):
                    v.tensor_scalar(w_h[:, t, :], wa[:, t, :], gate[:, t:t + 1], None, ALU.mult).then_inc(s["wa_scaled"], 1)
                    v.tensor_scalar(w_x[:, t, :], ident[:, :], rest[:, t:t + 1], None, ALU.mult).then_inc(s["wa_scaled"], 1)

                def mask(b, i):
                    for k, of in enumerate((acc, x_t)):
                        for t in range(NT):
                            v.scalar_tensor_tensor(masked[i][:, k * NT + t, :], ntype_b[:, bass.ds(b * NB, NB)], float(t), of[:, bass.ds(b * NB, NB)],
                                                   ALU.is_equal, ALU.mult).then_inc(s["h_masked"], 1)

                def norm(i, k, n):
                    st = s["norm_step"]
                    dve.wait_ge(s["x_rows"], (i + 1) * 16)
                    dve.wait_ge(s["rows_t"], (i + 1))
                    wait(dve, s["normed"], i)
                    v.tensor_tensor(resid[0:n, :], rows[0:n, :], row_ps[k][0:n, 0:D], ALU.add).then_inc(s["resid"], 1)
                    dve.wait_ge(s["resid"], (i + 1))
                    v.bn_stats(stats[0:n, :], resid[0:n, :]).then_inc(st, 1)
                    dve.wait_ge(st, i * 3 + 1)
                    dve.nop(nofuse=True)
                    v.bn_aggr(mv[0:n, :], stats[0:n, :]).then_inc(st, 1)
                    dve.wait_ge(s["root"], (i + 1))
                    v.reciprocal(inv[0:n, :], root[0:n, :]).then_inc(st, 1)
                    dve.wait_ge(st, i * 3 + 3)
                    if not (isinstance(i, int) and i == 0):
                        dve.wait_ge(s["stored"], i * 16)
                    v.tensor_scalar(normed[0:n, :], resid[0:n, :], mv[0:n, 0:1], inv[0:n, 0:1], ALU.subtract, ALU.mult).then_inc(s["normed"], 1)

                if not last_layer:
                    mask(0, 0)
                    with dve.Fori(0, (NBLK - 1) // 2) as b:
                        dve.wait_ge(s["mixed"], b * 2 + 1)
                        mask(b * 2 + 1, 1)
                        dve.wait_ge(s["mixed"], b * 2 + 2)
                        mask(b * 2 + 2, 0)
                else:
                    m0 = NBLK
                    mask(0, 0)
                    with dve.Fori(0, (NBLK - 1) // 2) as b:
                        for i in range(2):
                            dve.wait_ge(s["mixed"], b * 2 + (m0 + i + 1))
                            mask(b * 2 + (i + 1), 1 - i)
                            for k in range(2):
                                norm(b * 4 + (i * 2 + k), k, P)
                    norm(XT - 1, 0, XR)

            @block.scalar
            def _(act):
                a = nc.scalar
                act.wait_ge(s["wa_in"], 32 * (l + 1))
                a.activation(gate_exp[:, :], gate_in[:, :], ACT.Exp, scale=-1.0).then_inc(s["neg_exp"], 1)

                def block_of(b, i, full=True):
                    act.wait_ge(s["mixed"], b + (l * NBLK + 1))
                    if not last_layer:
                        a.activation(x_t[:, bass.ds(b * NB, NB)], mix_ps[i][:, 0:NB], ACT.Copy).then_inc(s["x_new"], 1)
                        return
                    if not (isinstance(b, int) and b == 0):
                        act.wait_ge(s["rows_t"], b * 2)
                    a.activation(fresh[:, :], mix_ps[i][:, 0:NB], ACT.Copy).then_inc(s["x_new"], 1)
                    for k in range(2 if full else 1):
                        t = b * 2 + k
                        n = P if full else XR
                        act.wait_ge(s["norm_step"], t * 3 + 2)
                        a.activation(root[0:n, :], mv[0:n, 1:2], ACT.Sqrt, bias=eps[0:n, 0:1]).then_inc(s["root"], 1)

                block_of(0, 0)
                with act.Fori(0, (NBLK - 3) // 2) as b:
                    block_of(b * 2 + 1, 1)
                    block_of(b * 2 + 2, 0)
                block_of(NBLK - 2, 1)
                block_of(NBLK - 1, 0, False)

            @block.tensor
            def _(pe):
                t_ = nc.tensor
                pe.wait_ge(s["wa_scaled"], 2 * NT * (l + 1))

                def block_of(b, i, full=True):
                    pe.wait_ge(s["h_masked"], b * (2 * NT) + (l * NBLK + 1) * 2 * NT)
                    if not (isinstance(b, int) and b < 2 and l == 0):
                        pe.wait_ge(s["x_new"], b + (l * NBLK - 1))
                    for k in range(2 * NT):
                        w = w_h[:, k, :] if k < NT else w_x[:, k - NT, :]
                        last = t_.matmul(mix_ps[i][:, 0:NB], w, masked[i][:, k, :], start=(k == 0), stop=(k == 2 * NT - 1))
                    last.then_inc(s["mixed"], 1)
                    if last_layer:
                        pe.wait_ge(s["x_new"], b + (l * NBLK + 1))
                        if not (isinstance(b, int) and b == 0):
                            pe.wait_ge(s["resid"], b * 2)
                        for k in range(2 if full else 1):
                            n = P if full else XR
                            t_.transpose(row_ps[k][0:n, 0:D], fresh[:, k * P:k * P + n], ident[:, :]).then_inc(s["rows_t"], 1)

                block_of(0, 0)
                with pe.Fori(0, (NBLK - 3) // 2) as b:
                    block_of(b * 2 + 1, 1)
                    block_of(b * 2 + 2, 0)
                block_of(NBLK - 2, 1)
                block_of(NBLK - 1, 0, False)


_INS = ["x", "src", "dst", "edge_type_6", "node_type_3", "L0_gnn_Wk", "L0_gnn_Wq", "L0_gnn_Wv", "L0_gnn_Wa",
        "L0_gnn_pri", "L0_gnn_Watt", "L0_gnn_Wmsg", "L0_gnn_skip"]


def kernel(**inputs):
    import numpy as _np
    import concourse.bacc as _bacc
    from concourse import mybir as _mybir
    from concourse.bass_utils import run_bass_kernel_spmd as _run

    nc = _bacc.Bacc("TRN2", target_bir_lowering=False, num_devices=1)
    arrays, args = {}, []
    for name in _INS:
        a = _np.ascontiguousarray(inputs[name])
        arrays[f"in_{name}"] = a
        args.append(nc.dram_tensor(f"in_{name}", a.shape, _mybir.dt.from_np(a.dtype), kind="ExternalInput").ap())
    result = nc.dram_tensor("out_x", (N, D), _mybir.dt.float32, kind="ExternalOutput").ap()
    hgt_kernel(nc, *args, result)
    r = _run(nc, [arrays], core_ids=[0])
    return r.results[0]["out_x"]
```

```python
from contextlib import ExitStack

import concourse.bass as bass
from concourse import mybir

ALU = mybir.AluOpType
ACT = mybir.ActivationFunctionType
F32 = mybir.dt.float32
BF16 = mybir.dt.bfloat16
I32 = mybir.dt.int32
X_AXIS = mybir.AxisListType.X

P = 128
N, D, H = 6250, 128, 8
HD = D // H
NT, ET, L = 3, 6, 2
E = 206250
EPS = 1e-5
BIG = 2.0 ** 100

TE = P
CT = P // H
QT = 4
NQ = CT // QT
NCH = -(-E // (TE * CT))
TILES = NCH * CT
NG = -(-TILES // P)
FULL = E // TE
REST = E - FULL * TE
GL = TILES - (NG - 1) * P
NPAD = 6400
NB = 256
NBLK = NPAD // NB
XT = -(-N // P)
XR = N - (XT - 1) * P
ROW = 2 * D

M_A, M_C, M_D, M_AM, M_CM, M_DM, M_W = 0, 129, 257, 385, 513, 641, 770
R_A, R_C, R_CR, R_AR, R_W = 0, 16, 32, 48, 128

STEPS = [
    "run_max_fwd", "run_max", "max_edges", "max_carry", "max_left", "max_right_in", "max_right_top",
    "max_right", "max_carry_on", "max_pick", "max_picked", "max_first", "max_all", "shifted",
    "alpha_arg", "run_sum_fwd", "run_sum", "sum_edges", "sum_carry_in", "sum_carry", "sum_left",
    "sum_right_in", "sum_right_top", "sum_right", "sum_pick", "sum_picked", "sum_first", "sum_all",
    "sum_inverse", "weights", "acc_factor",
]
K_DVE = len(STEPS)
FILLED = ("run_max_fwd", "run_max", "max_carry", "max_right_in", "max_right_top", "max_pick", "max_picked",
          "max_all", "sum_carry_in", "sum_carry", "sum_right_in", "sum_pick", "sum_picked")
PE_STEPS = ["max_rows", "max_cols", "sum_rows", "sum_cols", "weights_e", "factor_cols"]
K_PE = len(PE_STEPS)
ACT_STEPS = ["alpha", "exps", "weights_sb"]
K_ACT = len(ACT_STEPS)


class Chunk:

    def __init__(self, l, turn, k):
        self.l, self.turn, self.k = l, turn, k
        self.c = turn * 6 + k
        self.par, self.tri = k % 2, k % 3
        self.all = l * NCH + self.c
        self.use = l * -(-(NCH - self.par) // 2) + (turn * 3 + k // 2)
        self.use3 = l * -(-(NCH - self.tri) // 3) + (turn * 2 + k // 3)

    def quarters(self, q):
        return self.all * NQ + (q + 1)

    def before(self, n):
        if isinstance(self.turn, int) and self.c < n:
            return None
        return Chunk(self.l, self.turn, self.k - n)


def wait(eng, sem, value):
    if not (isinstance(value, int) and value <= 0):
        eng.wait_ge(sem, value)


def over_chunks(eng, l, body):
    def step(turn, k):
        chunks = [Chunk(l, turn, n) for n in (k, k - 1, k - 2, k + 1)]
        if isinstance(turn, int):
            chunks = [ch if 0 <= ch.c < NCH else None for ch in chunks]
        body(*chunks)

    peeled = 3
    turns = (NCH - 1 - peeled) // 6
    for k in range(peeled):
        step(0, k)
    with eng.Fori(0, turns) as turn:
        for k in range(6):
            step(turn, peeled + k)
    for c in range(peeled + 6 * turns, NCH + 2):
        step(0, c)


def hgt_kernel(nc, x, src, dst, etype, ntype, Wk, Wq, Wv, Wa, pri, Watt, Wmsg, skip, out):
    table = nc.dram_tensor("kv_table", [NPAD * ET, ROW], F32).ap()
    queries = nc.dram_tensor("queries", [NPAD, D], F32).ap()
    dst_pad = nc.dram_tensor("dst_pad", [TILES, TE], I32).ap()
    places = nc.dram_tensor("places", [TILES, TE], BF16).ap()
    edge_masks = nc.dram_tensor("edge_masks", [TILES, M_W], BF16).ap()
    tile_masks = nc.dram_tensor("tile_masks", [NCH, R_W], F32).ap()

    with ExitStack() as kept:
        def sb(name, shape, dt=F32, ctx=kept):
            return ctx.enter_context(nc.sbuf_tensor(name, shape, dt))

        def sem(name):
            return kept.enter_context(nc.semaphore(name))

        banks = [kept.enter_context(nc.psum_tensor(f"bank{i}", [P, 512], F32)) for i in range(8)]

        x_t = sb("x_t", [P, NPAD])
        acc = sb("acc", [P, NPAD])
        ntype_b = sb("ntype_b", [P, NPAD], BF16)
        windows = sb("windows", [1, TILES], I32)
        edge_ix = sb("edge_ix", [P, NCH, 2 * CT], I32)
        ident = sb("ident", [P, P])
        ramp = sb("ramp", [P, TE])
        tile_sel = sb("tile_sel", [P, CT])
        head_sel = sb("head_sel", [P, H])
        head_rep = sb("head_rep", [H, P])
        head_exp = sb("head_exp", [H, P])
        head_sum = sb("head_sum", [P, 2 * P - H])
        lane = sb("lane", [P, 1])

        prepare(nc, sb, sem, banks, x, src, dst, etype, ntype, x_t, ntype_b, edge_ix, windows, ident,
                ramp, tile_sel, head_sel, head_rep, head_exp, head_sum, lane, dst_pad, places, edge_masks,
                tile_masks)
        node_sems = {n: sem(n) for n in (
            "w_in", "bd_zero", "bd_scaled", "masked", "tables_kv", "kvq_done", "kv_sb", "q_sb", "tables_mm", "evac_act",
            "evac_dve", "query_out", "acc_zero")}
        node_sems["table_out"] = [sem(f"table_out_{i}") for i in range(2)]
        edge_sems = edge_semaphores(sem)
        out_sems = {n: sem(n) for n in (
            "wa_in", "neg_exp", "gates", "wa_scaled", "cols_masked", "mixed", "x_new", "x_rows", "rows_t",
            "resid", "eps", "stats", "aggr", "root", "inverse", "normed")}
        out_sems["stored"] = [sem(f"stored_{i}") for i in range(2)]
        for l in range(L):
            tables(nc, l, node_sems, banks, x_t, acc, ntype_b, Wk, Wq, Wv, pri, Watt, Wmsg, table, queries)
            edges(nc, l, edge_sems, banks, acc, edge_ix, windows, ident, ramp, tile_sel, head_sel,
                  head_rep, head_exp, head_sum, lane, table, queries, places, edge_masks, tile_masks)
            node_out(nc, l, out_sems, banks, x_t, acc, ntype_b, ident, Wa, skip, x, out)


def prepare(nc, sb, sem, banks, x, src, dst, etype, ntype, x_t, ntype_b, edge_ix, windows, ident, ramp,
            tile_sel, head_sel, head_rep, head_exp, head_sum, lane, dst_pad, places, edge_masks, tile_masks):
    with ExitStack() as ctx:
        dst_i = sb("dst_i", [P, NG, TE], I32, ctx)
        src_i = sb("src_i", [P, NG, TE], I32, ctx)
        et_i = sb("et_i", [P, NG, TE], I32, ctx)
        dst_f = sb("dst_f", [P, NG, TE], F32, ctx)
        row_f = sb("row_f", [P, NG, TE], F32, ctx)
        rel_f = sb("rel_f", [P, NG, TE], F32, ctx)
        rel_h = sb("rel_h", [P, NG, TE], BF16, ctx)
        ntype_i = sb("ntype_i", [P, N], I32, ctx)
        masks = sb("masks", [P, NG, M_W], BF16, ctx)
        x_in = sb("x_in", [P, XT, D], F32, ctx)
        first_i = sb("first_i", [NCH, CT], I32, ctx)
        last_i = sb("last_i", [NCH, CT + 1], I32, ctx)
        goes_on = sb("goes_on", [NCH, CT], F32, ctx)
        whole = sb("whole", [NCH, CT], F32, ctx)
        rowm = sb("rowm", [NCH, R_W], F32, ctx)

        filled = sem("filled")
        edges_in = sem("edges_in")
        x_loaded = sem("x_loaded")
        ntype_in = sem("ntype_in")
        dst_padded = sem("dst_padded")
        ends_in = sem("ends_in")
        windows_in = sem("windows_in")
        ident_step = sem("ident_step")
        consts = sem("consts")
        prep = sem("prep")
        turned = sem("turned")
        put = sem("put")
        rows_made = sem("rows_made")
        masks_out = sem("masks_out")
        sels = sem("sels")
        places_made = sem("places_made")

        def tiles_view(a, g0, g1):
            return a[g0 * P * TE:g1 * P * TE].rearrange("(g p e) -> p g e", p=P, e=TE)

        with nc.Block() as block:
            @block.sync
            def _(sp):
                sp.dma_start(x_in[:, 0:XT - 1, :], x[0:(XT - 1) * P, :].rearrange("(b p) f -> p b f", p=P)).then_inc(x_loaded, 16)
                sp.dma_start(x_in[0:XR, XT - 1, :], x[(XT - 1) * P:N, :]).then_inc(x_loaded, 16)
                sp.wait_ge(filled, 4)
                g = (NG - 1) * P
                for tile, a in ((dst_i, dst), (src_i, src), (et_i, etype)):
                    sp.dma_start(tile[:, 0:NG - 1, :], tiles_view(a, 0, NG - 1)).then_inc(edges_in, 16)
                    sp.dma_start(tile[0:FULL - g, NG - 1, :], a[g * TE:FULL * TE].rearrange("(p e) -> p e", e=TE)).then_inc(edges_in, 16)
                    sp.dma_start(tile[FULL - g:FULL - g + 1, NG - 1, 0:REST], a[FULL * TE:E].rearrange("(p e) -> p e", p=1)).then_inc(edges_in, 16)
                sp.dma_start(ntype_i[:, :], ntype.rearrange("(a n) -> a n", a=1).to_broadcast([P, N])).then_inc(ntype_in, 16)
                sp.wait_ge(edges_in, 16 * 9)
                sp.dma_start(dst_pad[0:g, :].rearrange("(g p) e -> p g e", p=P), dst_i[:, 0:NG - 1, :]).then_inc(dst_padded, 16)
                sp.dma_start(dst_pad[g:TILES, :], dst_i[0:GL, NG - 1, :]).then_inc(dst_padded, 16)
                sp.wait_ge(dst_padded, 32)
                with nc.allow_non_contiguous_dma(reason="one node of each tile, once"):
                    by_chunk = dst_pad.rearrange("(c t) e -> c t e", t=CT)
                    sp.dma_start(first_i[:, :], by_chunk[:, :, 0]).then_inc(ends_in, 16)
                    sp.dma_start(last_i[:, 1:CT + 1], by_chunk[:, :, TE - 1]).then_inc(ends_in, 16)
                    sp.dma_start(last_i[1:NCH, 0:1], by_chunk[0:NCH - 1, CT - 1:CT, TE - 1]).then_inc(ends_in, 16)
                    sp.dma_start(windows[0:1, :], dst_pad[:, 0:1].rearrange("t a -> a t")).then_inc(windows_in, 16)
                sp.wait_ge(prep, 15)
                sp.dma_start(edge_masks[0:g, :].rearrange("(g p) m -> p g m", p=P), masks[:, 0:NG - 1, :]).then_inc(masks_out, 16)
                sp.dma_start(edge_masks[g:TILES, :], masks[0:GL, NG - 1, :]).then_inc(masks_out, 16)
                sp.wait_ge(places_made, 1)
                sp.dma_start(places[0:g, :].rearrange("(g p) m -> p g m", p=P), rel_h[:, 0:NG - 1, :]).then_inc(masks_out, 16)
                sp.dma_start(places[g:TILES, :], rel_h[0:GL, NG - 1, :]).then_inc(masks_out, 16)
                sp.wait_ge(rows_made, 9)
                sp.dma_start(tile_masks[:, :], rowm[:, :]).then_inc(masks_out, 16)
                sp.wait_ge(masks_out, 80)
                sp.wait_ge(windows_in, 16)

            @block.gpsimd
            def _(pool):
                pool.memset(dst_i[:, :, :], N).then_inc(filled, 1)
                pool.memset(src_i[:, :, :], 0).then_inc(filled, 1)
                pool.memset(et_i[:, :, :], 0).then_inc(filled, 1)
                pool.memset(last_i[:, :], -1).then_inc(filled, 1)
                pool.memset(ident[:, :], 0.0).then_inc(ident_step, 1)
                pool.memset(head_rep[:, :], 0.0).then_inc(ident_step, 1)
                pool.memset(head_exp[:, :], 0.0).then_inc(ident_step, 1)
                pool.memset(head_sum[:, :], 0.0).then_inc(ident_step, 1)
                pool.wait_ge(ident_step, 4)
                mid = head_sum[:, P - H:P]
                pool.memset(mid, 1.0).then_inc(ident_step, 1)
                pool.affine_select(out=ident[:, :], in_=ident[:, :], compare_op=ALU.not_equal, fill=1.0,
                                   base=0, pattern=[[-1, P]], channel_multiplier=1).then_inc(consts, 1)
                v = head_rep[:, :].rearrange("p (t h) -> p t h", h=H)
                pool.affine_select(out=v, in_=v, compare_op=ALU.not_equal, fill=1.0, base=0,
                                   pattern=[[0, CT], [-1, H]], channel_multiplier=1).then_inc(consts, 1)
                v = head_exp[:, :].rearrange("p (h d) -> p h d", h=H)
                pool.affine_select(out=v, in_=v, compare_op=ALU.not_equal, fill=1.0, base=0,
                                   pattern=[[-1, H], [0, HD]], channel_multiplier=1).then_inc(consts, 1)
                pool.wait_ge(ident_step, 5)
                pool.affine_select(out=mid, in_=mid, compare_op=ALU.is_ge, fill=0.0, base=0,
                                   pattern=[[-HD, H]], channel_multiplier=1).then_inc(ident_step, 1)
                pool.wait_ge(ident_step, 6)
                pool.affine_select(out=mid, in_=mid, compare_op=ALU.is_ge, fill=0.0, base=HD - 1,
                                   pattern=[[HD, H]], channel_multiplier=-1).then_inc(ident_step, 1)
                pool.iota(lane[:, :], [[0, 1]], base=0, channel_multiplier=-1,
                          allow_small_or_imprecise_dtypes=True).then_inc(ident_step, 1)
                pool.iota(ramp[:, :], [[1, TE]], base=0, channel_multiplier=0,
                          allow_small_or_imprecise_dtypes=True).then_inc(consts, 1)
                pool.memset(x_t[:, N:NPAD], 0.0).then_inc(consts, 1)
                pool.memset(ntype_b[:, N:NPAD], 0.0).then_inc(consts, 1)

            @block.vector
            def _(dve):
                v = nc.vector
                dve.wait_ge(consts, 1)
                v.tensor_reduce(tile_sel[:, :], ident[:, :].rearrange("p (t h) -> p t h", h=H), X_AXIS, ALU.add).then_inc(sels, 1)
                v.tensor_reduce(head_sel[:, :], ident[:, :].rearrange("p (t h) -> p h t", h=H), X_AXIS, ALU.add).then_inc(sels, 1)
                dve.wait_ge(edges_in, 16 * 9)
                v.tensor_copy(dst_f[:, :, :], dst_i[:, :, :]).then_inc(prep, 1)
                v.scalar_tensor_tensor(row_f[:, :, :], src_i[:, :, :], float(ET), et_i[:, :, :], ALU.mult, ALU.add).then_inc(prep, 1)
                dve.wait_ge(prep, 1)
                first = dst_f[:, :, 0:1].to_broadcast([P, NG, TE])
                last = dst_f[:, :, TE - 1:TE].to_broadcast([P, NG, TE])
                d = dst_f[:, :, :]
                v.tensor_tensor(rel_f[:, :, :], d, first, ALU.subtract).then_inc(prep, 1)
                dve.wait_ge(prep, 3)
                v.tensor_copy(rel_h[:, :, :], rel_f[:, :, :]).then_inc(places_made, 1)
                v.memset(masks[:, :, M_A:M_A + TE + 1], -BIG).then_inc(prep, 1)
                v.memset(masks[:, :, M_AM:M_AM + 1], 0.0).then_inc(prep, 1)
                v.memset(masks[:, :, M_DM + TE:M_W], 0.0).then_inc(prep, 1)
                v.tensor_tensor(masks[:, :, M_AM + 1:M_AM + TE], dst_f[:, :, 1:TE], dst_f[:, :, 0:TE - 1], ALU.is_equal).then_inc(prep, 1)
                v.tensor_tensor(masks[:, :, M_CM:M_CM + TE], d, first, ALU.is_equal).then_inc(prep, 1)
                v.tensor_tensor(masks[:, :, M_DM:M_DM + TE], d, last, ALU.is_equal).then_inc(prep, 1)
                dve.wait_ge(prep, 9)
                for k, (to, of, n) in enumerate(((M_A + 1, M_AM + 1, TE - 1), (M_C, M_CM, TE), (M_D, M_DM, TE))):
                    v.tensor_scalar(masks[:, :, to:to + n], masks[:, :, of:of + n], 1.0, BIG, ALU.subtract, ALU.mult).then_inc(prep, 2)
                dve.wait_ge(ntype_in, 16)
                v.tensor_copy(ntype_b[:, 0:N], ntype_i[:, :]).then_inc(places_made, 1)
                dve.wait_ge(ends_in, 48)
                v.memset(rowm[:, :], 0.0).then_inc(rows_made, 1)
                v.tensor_tensor(goes_on[:, :], first_i[:, :], last_i[:, 0:CT], ALU.is_equal).then_inc(rows_made, 1)
                v.tensor_tensor(whole[:, :], first_i[:, :], last_i[:, 1:CT + 1], ALU.is_equal).then_inc(rows_made, 1)
                dve.wait_ge(rows_made, 3)
                f = R_W // 2
                v.tensor_tensor(rowm[:, f + R_A:f + R_A + CT], goes_on[:, :], whole[:, :], ALU.mult).then_inc(rows_made, 1)
                v.tensor_copy(rowm[:, f + R_C:f + R_C + CT], goes_on[:, :]).then_inc(rows_made, 1)
                v.tensor_copy(rowm[:, f + R_CR:f + R_CR + CT - 1], goes_on[:, 1:CT]).then_inc(rows_made, 1)
                v.tensor_tensor(rowm[:, f + R_AR:f + R_AR + CT - 1], goes_on[:, 1:CT], whole[:, 1:CT], ALU.mult).then_inc(rows_made, 1)
                dve.wait_ge(rows_made, 7)
                v.tensor_scalar(rowm[:, 0:f], rowm[:, f:2 * f], 1.0, BIG, ALU.subtract, ALU.mult).then_inc(rows_made, 2)

            @block.tensor
            def _(pe):
                pe.wait_ge(consts, 1)
                pe.wait_ge(x_loaded, 32)
                for g in range(NT_GROUPS):
                    if g >= 2:
                        pe.wait_ge(put, g - 1)
                    for k, b in enumerate(range(g * 4, min(g * 4 + 4, XT))):
                        n = P if b < XT - 1 else XR
                        last = nc.tensor.transpose(banks[g % 2][:, k * P:k * P + n], x_in[0:n, b, :], ident[0:n, 0:n])
                    last.then_inc(turned, 1)
                pe.wait_ge(prep, 3)
                for g in range(NG):
                    pe.wait_ge(put, NT_GROUPS + g - 1)
                    n = P if g < NG - 1 else GL
                    bank = banks[(NT_GROUPS + g) % 2]
                    nc.tensor.transpose(bank[:, 0:n], row_f[0:n, g, :], ident[0:n, 0:n])
                    nc.tensor.transpose(bank[:, P:P + n], rel_f[0:n, g, :], ident[0:n, 0:n]).then_inc(turned, 1)

            @block.scalar
            def _(act):
                a = nc.scalar
                for g in range(NT_GROUPS):
                    act.wait_ge(turned, g + 1)
                    n = min(N, (g + 1) * 4 * P) - g * 4 * P
                    a.activation(x_t[:, g * 4 * P:g * 4 * P + n], banks[g % 2][:, 0:n], ACT.Copy).then_inc(put, 1)
                for g in range(NG):
                    act.wait_ge(turned, NT_GROUPS + g + 1)
                    n = P if g < NG - 1 else GL
                    c0, c1 = g * P // CT, (g * P + n) // CT
                    bank = banks[(NT_GROUPS + g) % 2]
                    a.activation(edge_ix[:, c0:c1, 0:CT], bank[:, 0:n].rearrange("p (c t) -> p c t", t=CT), ACT.Copy)
                    a.activation(edge_ix[:, c0:c1, CT:2 * CT].bitcast(F32), bank[:, P:P + n].rearrange("p (c t) -> p c t", t=CT), ACT.Copy).then_inc(put, 1)


NT_GROUPS = -(-XT // 4)


def tables(nc, l, s, banks, x_t, acc, ntype_b, Wk, Wq, Wv, pri, Watt, Wmsg, table, queries):
    HALF = ET // 2 * D
    with ExitStack() as ctx:
        def sb(name, shape, dt=F32):
            return ctx.enter_context(nc.sbuf_tensor(f"tab_{name}_{l}", shape, dt))

        wk, wq, wv = sb("wk", [P, NT, D]), sb("wq", [P, NT, D]), sb("wv", [P, NT, D])
        bd = sb("bd", [P, 2, ET, D])
        prior = sb("prior", [P, ET])
        masked = sb("masked", [P, NT, NB])
        kv_t = sb("kv_t", [P, 2, NB])
        q_rows = sb("q_rows", [P, 2, D])
        rows = sb("rows", [P, 2, ET, 2, D])
        kv_ps, q_ps, tab_ps = banks[0], banks[1], banks[2:6]
        loads = 3 + 1 + 2 * H

        def blocks(b):
            return l * NBLK + b

        def load_transform(eng, i, a):
            eng.wait_ge(s["bd_zero"], l + 1)
            for h in range(H):
                r = slice(h * HD, (h + 1) * HD)
                eng.dma_start(bd[r, i, :, r], a[l, h].rearrange("t d o -> d t o")).then_inc(s["w_in"], 16)

        with nc.Block() as block:
            @block.sync
            def _(sp):
                for w, a in ((wk, Wk), (wv, Wv), (wq, Wq)):
                    sp.dma_start(w[:, :, :], a[l].rearrange("t k n -> k t n")).then_inc(s["w_in"], 16)
                with nc.allow_non_contiguous_dma(reason="48 values"):
                    sp.dma_start(prior[:, :], pri[l].rearrange("h (a t) -> h a t", a=1).to_broadcast([H, HD, ET])).then_inc(s["w_in"], 16)
                load_transform(sp, 0, Watt)
                with sp.Fori(0, NBLK) as b:
                    for i in range(2):
                        if i == 0:
                            sp.wait_ge(s["q_sb"], (blocks(b) + 1))
                            sp.dma_start(queries[bass.ds(b * NB, NB), :].rearrange("(i p) f -> p i f", p=P), q_rows[:, :, :]).then_inc(s["query_out"], 16)
                        sp.wait_ge(s["evac_act"], blocks(b) * 4 + 2 * (i + 1))
                        sp.wait_ge(s["evac_dve"], blocks(b) * 4 + 2 * (i + 1))
                        sp.dma_start(table[bass.ds(b * (NB * ET) + i * (P * ET), P * ET), :].rearrange("(p t) f -> p (t f)", t=ET),
                                     rows[:, i, :, :, :].rearrange("p t k f -> p (t k f)")).then_inc(s["table_out"][i], 16)
                sp.wait_ge(s["query_out"], (l + 1) * NBLK * 16)
                for i in range(2):
                    sp.wait_ge(s["table_out"][i], (l + 1) * NBLK * 16)

            @block.gpsimd
            def _(pool):
                pool.memset(bd[:, :, :, :], 0.0).then_inc(s["bd_zero"], 1)
                pool.memset(acc[:, :], 0.0).then_inc(s["acc_zero"], 1)

            @block.vector
            def _(dve):
                v = nc.vector

                def mask(b):
                    for t in range(NT):
                        v.scalar_tensor_tensor(masked[:, t, :], ntype_b[:, bass.ds(b * NB, NB)], float(t), x_t[:, bass.ds(b * NB, NB)],
                                               ALU.is_equal, ALU.mult).then_inc(s["masked"], 1)

                def evac(b):
                    for i in range(2):
                        for hf in range(2):
                            dve.wait_ge(s["tables_mm"], blocks(b) * 8 + (i * 4 + 2 + hf + 1))
                            if hf == 0:
                                yield i
                            v.tensor_copy(rows[:, i, 3 * hf:3 * hf + 3, 1, :], tab_ps[2 + hf][:, 0:HALF].rearrange("p (t f) -> p t f", f=D)).then_inc(s["evac_dve"], 1)

                mask(0)
                dve.wait_ge(s["w_in"], 16 * loads * (l + 1))
                v.scalar_tensor_tensor(bd[:, 0, :, :], bd[:, 0, :, :], 1.0 / float(HD) ** 0.5, prior[:, :].unsqueeze(2).to_broadcast([P, ET, D]),
                                       ALU.mult, ALU.mult).then_inc(s["bd_scaled"], 1)

                def block_of(b, more, reuse):
                    if more:
                        dve.wait_ge(s["kvq_done"], (blocks(b) + 1))
                        mask(b + 1)
                    for i in evac(b):
                        if reuse:
                            dve.wait_ge(s["table_out"][i], (blocks(b) * 16))

                block_of(0, True, l > 0)
                with dve.Fori(1, NBLK - 1) as b:
                    block_of(b, True, True)
                block_of(NBLK - 1, False, True)

            @block.tensor
            def _(pe):
                t_ = nc.tensor
                pe.wait_ge(s["w_in"], 16 * loads * (l + 1))
                pe.wait_ge(s["bd_scaled"], l + 1)

                def block_of(b, reuse):
                    pe.wait_ge(s["masked"], (blocks(b) + 1) * NT)
                    if reuse:
                        pe.wait_ge(s["q_sb"], blocks(b))
                        pe.wait_ge(s["kv_sb"], blocks(b))
                    for i, w in enumerate((wk, wv)):
                        for t in range(NT):
                            last = t_.matmul(kv_ps[:, i * NB:(i + 1) * NB], w[:, t, :], masked[:, t, :], start=(t == 0), stop=(t == NT - 1))
                    last.then_inc(s["tables_kv"], 1)
                    for i in range(2):
                        for t in range(NT):
                            last = t_.matmul(q_ps[:, i * D:(i + 1) * D], masked[:, t, i * P:(i + 1) * P], wq[:, t, :], start=(t == 0), stop=(t == NT - 1))
                    last.then_inc(s["kvq_done"], 1)
                    pe.wait_ge(s["kv_sb"], (blocks(b) + 1))
                    for i in range(2):
                        for kv in range(2):
                            for hf in range(2):
                                if i == 1:
                                    pe.wait_ge(s["evac_dve" if kv else "evac_act"], blocks(b) * 4 + (hf + 1))
                                elif reuse:
                                    pe.wait_ge(s["evac_dve" if kv else "evac_act"], blocks(b) * 4 - 2 + (hf + 1))
                                t_.matmul(tab_ps[2 * kv + hf][:, 0:HALF], kv_t[:, kv, i * P:(i + 1) * P],
                                          bd[:, kv, 3 * hf:3 * hf + 3, :].rearrange("p t f -> p (t f)"), start=True, stop=True).then_inc(s["tables_mm"], 1)

                block_of(0, l > 0)
                with pe.Fori(1, NBLK) as b:
                    block_of(b, True)

            @block.scalar
            def _(act):
                a = nc.scalar
                load_transform(act, 1, Wmsg)

                def block_of(b, reuse):
                    act.wait_ge(s["tables_kv"], (blocks(b) + 1))
                    if reuse:
                        act.wait_ge(s["tables_mm"], blocks(b) * 8)
                    a.activation(kv_t[:, :, :], kv_ps[:, :].rearrange("p (k n) -> p k n", k=2), ACT.Copy).then_inc(s["kv_sb"], 1)
                    act.wait_ge(s["kvq_done"], (blocks(b) + 1))
                    if reuse:
                        act.wait_ge(s["query_out"], (blocks(b) * 16))
                    a.activation(q_rows[:, :, :], q_ps[:, 0:2 * D].rearrange("p (i f) -> p i f", i=2), ACT.Copy).then_inc(s["q_sb"], 1)
                    for i in range(2):
                        for hf in range(2):
                            act.wait_ge(s["tables_mm"], blocks(b) * 8 + (i * 4 + hf + 1))
                            if hf == 0 and reuse:
                                act.wait_ge(s["table_out"][i], (blocks(b) * 16))
                            a.activation(rows[:, i, 3 * hf:3 * hf + 3, 0, :], tab_ps[hf][:, 0:HALF].rearrange("p (t f) -> p t f", f=D), ACT.Copy).then_inc(s["evac_act"], 1)

                block_of(0, l > 0)
                with act.Fori(1, NBLK) as b:
                    block_of(b, True)


def edge_semaphores(sem):
    one = ["indexed", "onehot_dist", "onehot", "spread_dist", "spread_made", "q_spread", "q_spread_sb", "keys_t", "products",
           "scores", "messages",
           "summed", "added", "stat_steps", "pe_steps", "act_steps", "carry_init"]
    s = {n: sem(n) for n in one}
    for n in ("masks_in", "places_in"):
        s[n] = [sem(f"{n}_{p}") for p in range(2)]
    for n, ring in (("rows_in", 3), ("queries_in", 2)):
        s[n] = [[sem(f"{n}_{p}_{q}") for q in range(NQ)] for p in range(ring)]
    return s


def edges(nc, l, s, banks, acc, edge_ix, windows, ident, ramp, tile_sel, head_sel, head_rep, head_exp,
          head_sum, lane, table, queries, places, edge_masks, tile_masks):
    with ExitStack() as ctx:
        def sb(name, shape, dt=F32):
            return ctx.enter_context(nc.sbuf_tensor(f"edge_{name}_{l}", shape, dt))

        ix = [sb(f"ix{p}", [P, CT], I32) for p in range(3)]
        em = [sb(f"em{p}", [P, M_W], BF16) for p in range(2)]
        tm = [sb(f"tm{p}", [H, R_W]) for p in range(2)]
        pl = [sb(f"pl{p}", [P, CT * TE], BF16) for p in range(2)]
        kv = [sb(f"kv{p}", [P, CT, ROW]) for p in range(3)]
        qw = [sb(f"qw{p}", [P, CT, D]) for p in range(2)]
        onehot = [sb(f"onehot{p}", [P, CT, TE]) for p in range(2)]
        dist = [sb(f"dist{i}", [P, QT, TE], BF16) for i in range(2)]
        spread = [sb(f"spread{i}", [P, QT, TE]) for i in range(2)]
        dist_s = [sb(f"dist_s{i}", [P, QT * TE], BF16) for i in range(2)]
        qe = [sb(f"qe{i}", [P, QT * TE]) for i in range(2)]
        prod = [sb(f"prod{i}", [P, QT * TE]) for i in range(2)]
        msg = sb("msg", [P, CT, D])
        wave = {n: sb(n, [P, TE]) for n in ("fwd", "run", "first", "all", "shift", "ea", "inv", "wts")}
        wts_e = sb("wts_e", [P, P])
        ends = [sb(f"ends{i}", [P, 2, CT]) for i in range(2)]
        picked = [sb(f"picked{i}", [P, 2, CT]) for i in range(2)]
        cols = [sb(f"cols{i}", [P, 2]) for i in range(2)]
        state = [sb(f"state{i}", [H, CT + 1]) for i in range(2)]
        right = [sb(f"right{i}", [H, CT]) for i in range(2)]
        sides = [sb(f"sides{i}", [H, 2, CT]) for i in range(2)]
        alpha_arg = sb("alpha_arg", [H, 1])
        alpha = sb("alpha", [H, 1])
        factor = sb("factor", [H, 1])

        kt_ps, qe_ps, ag_ps, chunk_ps = banks[0:2], banks[2:4], banks[4:6], banks[6:8]

        def scores_t(ch):
            return chunk_ps[ch.par][:, 0:P]

        def wts_ps(ch):
            return chunk_ps[ch.par][:, P:2 * P]

        def rows_ps(ch, i):
            return chunk_ps[ch.par][0:H, 2 * P + 32 * i:2 * P + 32 * i + 2 * CT]

        def cols_ps(ch, i):
            return chunk_ps[ch.par][:, 2 * P + 64 + 32 * i:2 * P + 64 + 32 * i + 2 * CT]

        def factor_ps(ch):
            return chunk_ps[ch.par][:, 3 * P:3 * P + 1]

        K_ADD = CT + 1

        def stat(ch, name):
            return ch.all * K_DVE + (STEPS.index(name) + 1)

        def pe_stat(ch, name):
            return ch.all * K_PE + (PE_STEPS.index(name) + 1)

        def act_stat(ch, name):
            return ch.all * K_ACT + (ACT_STEPS.index(name) + 1)

        with nc.Block() as block:
            @block.sync
            def _(sp):
                regs = [sp.alloc_register(f"sp_window_{l}_{k}") for k in range(QT)]

                def body(ch, prev, older, nxt):
                    if ch is None:
                        return
                    p, was = ch.par, ch.before(2)
                    if was:
                        sp.wait_ge(s["spread_made"], was.quarters(NQ - 1))
                    sp.dma_start(pl[p][:, :], places[bass.ds(ch.c * CT, CT), :].rearrange("(a t) e -> a (t e)", a=1).to_broadcast([P, CT * TE])).then_inc(s["places_in"][p], 16)
                    for q in range(NQ):
                        if was:
                            sp.wait_ge(s["q_spread"], was.quarters(q))
                        sp.load(regs, windows[0:1, bass.ds(ch.c * CT + q * QT, QT)])
                        for k in range(QT):
                            w = sp.snap(regs[k], min_val=0, max_val=N)
                            sp.dma_start(qw[p][:, q * QT + k, :], queries[bass.ds(w, TE), :]).then_inc(s["queries_in"][p][q], 16)
                    if was:
                        sp.wait_ge(s["stat_steps"], stat(was, STEPS[-1]))
                    sp.dma_start(em[p][:, :], edge_masks[bass.ds(ch.c * CT, CT), :].rearrange("t (a m) -> t a m", a=1).to_broadcast([CT, H, M_W])).then_inc(s["masks_in"][p], 16)
                    sp.dma_start(tm[p][:, :], tile_masks[bass.ds(ch.c, 1), :].to_broadcast([H, R_W])).then_inc(s["masks_in"][p], 16)

                over_chunks(sp, l, body)

            @block.gpsimd
            def _(pool):
                def index(ch):
                    was = ch.before(3)
                    if was:
                        pool.wait_ge(s["keys_t"], was.quarters(NQ - 1))
                    pool.tensor_copy(ix[ch.tri][:, :], edge_ix[:, bass.ds(ch.c, 1), 0:CT].rearrange("p a k -> p (a k)")).then_inc(s["indexed"], 1)

                def body(ch, prev, older, nxt):
                    if ch is None:
                        return
                    was = ch.before(3)
                    if not ch.before(1):
                        index(ch)
                    pool.wait_ge(s["indexed"], ch.all + 1)
                    pool.nop(nofuse=True)
                    for q in range(NQ):
                        if was:
                            pool.wait_ge(s["messages"], was.quarters(q))
                            pool.nop(nofuse=True)
                        for j in range(q * QT, (q + 1) * QT):
                            pool.indirect_dma_start(kv[ch.tri][:, j, :], None, table[:, :],
                                                    bass.IndirectOffsetOnAxis(ap=ix[ch.tri][:, j:j + 1], axis=0)).then_inc(s["rows_in"][ch.tri][q], 16)
                        if nxt and q == 1:
                            index(nxt)

                over_chunks(pool, l, body)

            @block.scalar
            def _(act):
                a = nc.scalar

                def build(ch, q):
                    was = ch.before(2)
                    if was:
                        act.wait_ge(s["summed"], was.quarters(q))
                    rel = edge_ix[:, bass.ds(ch.c, 1), CT:2 * CT].rearrange("p a k -> p (a k)").bitcast(F32)
                    wait(act, s["onehot"], ch.quarters(q) - 2)
                    for k in range(QT):
                        j = q * QT + k
                        last = a.activation(dist[q % 2][:, k, :], ramp[:, :], ACT.Abs, bias=rel[:, j:j + 1], scale=-1.0)
                    last.then_inc(s["onehot_dist"], 1)
                    act.wait_ge(s["onehot_dist"], ch.quarters(q))
                    a.activation(onehot[ch.par][:, q * QT:(q + 1) * QT, :], dist[q % 2][:, :, :], ACT.Relu, bias=1.0, scale=-1.0).then_inc(s["onehot"], 1)

                def build_spread(ch, q, first):
                    if q == 0:
                        act.wait_ge(s["places_in"][ch.par], (ch.use + 1) * 16)
                    wait(act, s["spread_made"], ch.quarters(q) - 2)
                    a.activation(dist_s[q % 2][:, :], pl[ch.par][:, q * QT * TE:(q + 1) * QT * TE], ACT.Abs, bias=lane[:, 0:1]).then_inc(s["spread_dist"], 1)
                    act.wait_ge(s["spread_dist"], ch.quarters(q))
                    if not first:
                        act.wait_ge(s["q_spread"], ch.quarters(q) - 2)
                    a.activation(spread[q % 2][:, :, :].rearrange("p k e -> p (k e)"), dist_s[q % 2][:, :], ACT.Relu, bias=1.0, scale=-1.0).then_inc(s["spread_made"], 1)

                def query_out(ch, q, first):
                    act.wait_ge(s["q_spread"], ch.quarters(q))
                    if not first:
                        act.wait_ge(s["products"], ch.quarters(q) - 2)
                    a.activation(qe[q % 2][:, :], qe_ps[q % 2][:, :], ACT.Copy).then_inc(s["q_spread_sb"], 1)

                def body(ch, prev, older, nxt):
                    first = ch is not None and not ch.before(1)
                    if first:
                        build_spread(ch, 0, True)
                        build_spread(ch, 1, True)
                        query_out(ch, 0, True)
                        query_out(ch, 1, True)
                    if ch:
                        build_spread(ch, 2, False)
                    if older:
                        build(older, 3)
                    if ch:
                        query_out(ch, 2, False)
                        build_spread(ch, 3, False)
                    if prev:
                        act.wait_ge(s["stat_steps"], stat(prev, "alpha_arg"))
                        a.activation(alpha[:, :], alpha_arg[:, :], ACT.Exp).then_inc(s["act_steps"], 1)
                        a.activation(wave["ea"][:, :], wave["shift"][:, :], ACT.Exp).then_inc(s["act_steps"], 1)
                    if ch:
                        query_out(ch, 3, False)
                    if prev:
                        build(prev, 0)
                    if nxt:
                        build_spread(nxt, 0, False)
                        build_spread(nxt, 1, False)
                    if prev:
                        build(prev, 1)
                        act.wait_ge(s["pe_steps"], pe_stat(prev, "weights_e"))
                        a.activation(wts_e[:, :], wts_ps(prev), ACT.Copy).then_inc(s["act_steps"], 1)
                    if nxt:
                        query_out(nxt, 0, False)
                    if prev:
                        build(prev, 2)
                    if nxt:
                        query_out(nxt, 1, False)

                over_chunks(act, l, body)

            @block.tensor
            def _(pe):
                t_ = nc.tensor

                def spread_queries(ch, q, first):
                    pe.wait_ge(s["spread_made"], ch.quarters(q))
                    pe.wait_ge(s["queries_in"][ch.par][q], (ch.use + 1) * (16 * QT))
                    if not first:
                        pe.wait_ge(s["q_spread_sb"], ch.quarters(q) - 2)
                    for k in range(QT):
                        last = t_.matmul(qe_ps[q % 2][:, k * TE:(k + 1) * TE], qw[ch.par][:, q * QT + k, :], spread[q % 2][:, k, :], start=True, stop=True)
                    last.then_inc(s["q_spread"], 1)

                def turn_keys(ch, q, first):
                    pe.wait_ge(s["rows_in"][ch.tri][q], (ch.use3 + 1) * (16 * QT))
                    if not first:
                        pe.wait_ge(s["products"], ch.quarters(q) - 2)
                    for k in range(QT):
                        last = t_.transpose(kt_ps[q % 2][:, k * TE:(k + 1) * TE], kv[ch.tri][:, q * QT + k, 0:D], ident[:, :])
                    last.then_inc(s["keys_t"], 1)

                def sum_heads(ch, q):
                    pe.wait_ge(s["products"], ch.quarters(q))
                    for k in range(QT):
                        j = q * QT + k
                        last = t_.matmul(scores_t(ch), head_sum[:, P - H - H * j:2 * P - H - H * j], prod[q % 2][:, k * TE:(k + 1) * TE],
                                         start=(j == 0), stop=(j == CT - 1))
                    last.then_inc(s["scores"], 1)

                def sum_messages(ch, q, first):
                    pe.wait_ge(s["messages"], ch.quarters(q))
                    pe.wait_ge(s["onehot"], ch.quarters(q))
                    if not first:
                        done = (ch.all * K_ADD + (1 + (q - 1) * QT)) if q >= 2 else ((ch.all - 1) * K_ADD + (1 + (q + NQ - 1) * QT))
                        pe.wait_ge(s["added"], done)
                    for k in range(QT):
                        last = t_.matmul(ag_ps[q % 2][:, k * TE:(k + 1) * TE], msg[:, q * QT + k, :], onehot[ch.par][:, q * QT + k, :], start=True, stop=True)
                    last.then_inc(s["summed"], 1)

                def to_rows(ch, i, step):
                    pe.wait_ge(s["stat_steps"], stat(ch, step))
                    t_.matmul(rows_ps(ch, i), head_sel[:, :], ends[i][:, :, :].rearrange("p a t -> p (a t)"), start=True, stop=True).then_inc(s["pe_steps"], 1)

                def to_cols(ch, i, step):
                    pe.wait_ge(s["stat_steps"], stat(ch, step))
                    t_.matmul(cols_ps(ch, i), head_rep[:, :], sides[i][:, :, :].rearrange("p a t -> p (a t)"), start=True, stop=True).then_inc(s["pe_steps"], 1)

                def body(ch, prev, older, nxt):
                    first = ch is not None and not ch.before(1)
                    if first:
                        for q in range(2):
                            spread_queries(ch, q, True)
                            turn_keys(ch, q, True)
                    if prev:
                        to_rows(prev, 0, "max_edges")
                    if ch:
                        spread_queries(ch, 2, False)
                        turn_keys(ch, 2, False)
                    if prev:
                        to_cols(prev, 0, "max_right")
                    if ch:
                        sum_heads(ch, 0)
                        sum_heads(ch, 1)
                        spread_queries(ch, 3, False)
                        turn_keys(ch, 3, False)
                    if older:
                        sum_messages(older, 2, False)
                    if prev:
                        to_rows(prev, 1, "sum_edges")
                    if older:
                        sum_messages(older, 3, False)
                    if ch:
                        sum_heads(ch, 2)
                    if prev:
                        to_cols(prev, 1, "sum_right")
                    if ch:
                        sum_heads(ch, 3)
                    if nxt:
                        for q in range(2):
                            spread_queries(nxt, q, False)
                            turn_keys(nxt, q, False)
                    if prev:
                        pe.wait_ge(s["stat_steps"], stat(prev, "weights"))
                        t_.transpose(wts_ps(prev), wave["wts"][:, :], ident[:, :]).then_inc(s["pe_steps"], 1)
                        pe.wait_ge(s["stat_steps"], stat(prev, "acc_factor"))
                        pe.wait_ge(s["act_steps"], act_stat(prev, "weights_sb"))
                        t_.matmul(factor_ps(prev), head_exp[:, :], factor[:, :], start=True, stop=True).then_inc(s["pe_steps"], 1)
                        begun = not prev.before(1)
                        sum_messages(prev, 0, begun)
                        sum_messages(prev, 1, begun)

                over_chunks(pe, l, body)

            @block.vector
            def _(dve):
                v = nc.vector
                regs = [dve.alloc_register(f"dve_window_{l}_{k}") for k in range(CT + 1)]
                for i in range(2):
                    v.memset(state[i][:, 0:1], -BIG if i == 0 else 0.0).then_inc(s["carry_init"], 1)

                def product(ch, q):
                    dve.wait_ge(s["keys_t"], ch.quarters(q))
                    dve.wait_ge(s["q_spread_sb"], ch.quarters(q))
                    wait(dve, s["scores"], ch.quarters(q) - 2)
                    v.tensor_tensor(prod[q % 2][:, :], kt_ps[q % 2][:, :], qe[q % 2][:, :], ALU.mult).then_inc(s["products"], 1)

                def message(ch, q):
                    w = wts_e[:, q * QT * H:(q + 1) * QT * H].rearrange("p (k h) -> p k h", h=H).unsqueeze(3).to_broadcast([P, QT, H, HD])
                    was = ch.quarters(q) - NQ
                    wait(dve, s["summed"], was)
                    v.tensor_tensor(msg[:, q * QT:(q + 1) * QT, :].rearrange("p k (h d) -> p k h d", h=H),
                                    kv[ch.tri][:, q * QT:(q + 1) * QT, D:2 * D].rearrange("p k (h d) -> p k h d", h=H), w, ALU.mult).then_inc(s["messages"], 1)

                def add(ch, j, at):
                    q, k = j // QT, j % QT
                    if k == 0:
                        dve.wait_ge(s["summed"], ch.quarters(q))
                    dve.wait_ge(s["added"], ch.all * K_ADD + (1 + j))
                    v.tensor_tensor(acc[:, bass.ds(at[j], TE)], acc[:, bass.ds(at[j], TE)], ag_ps[q % 2][:, k * TE:(k + 1) * TE], ALU.add).then_inc(s["added"], 1)

                def adds(ch):
                    at = [dve.snap(r, min_val=0, max_val=N) for r in regs[0:CT]]
                    for j in range(CT):
                        yield add(ch, j, at)

                def carried(ch):
                    w = dve.snap(regs[CT], min_val=0, max_val=N)
                    dve.wait_ge(s["pe_steps"], pe_stat(ch, "factor_cols"))
                    if ch.before(1):
                        dve.wait_ge(s["added"], ch.all * K_ADD)
                    v.tensor_tensor(acc[:, bass.ds(w, 1)], acc[:, bass.ds(w, 1)], factor_ps(ch), ALU.mult).then_inc(s["added"], 1)

                def stats(ch, more):
                    m, t = em[ch.par], tm[ch.par]
                    W = wave
                    f = R_W // 2

                    def own(name):
                        if name in FILLED:
                            next(more, None)
                        dve.wait_ge(s["stat_steps"], stat(ch, name))

                    def rev(ap, n=TE, o=0):
                        return ap[:, o + n - 1:(o - 1 if o else None):-1]

                    fwd_a = m[:, M_A:M_A + TE]

                    dve.wait_ge(s["carry_init"], ch.all + 2 * (l + 1))
                    dve.wait_ge(s["masks_in"][ch.par], (ch.use + 1) * 32)
                    dve.wait_ge(s["scores"], ch.quarters(NQ - 1))
                    v.tensor_tensor_scan(W["fwd"][:, :], fwd_a, scores_t(ch), -BIG, ALU.add, ALU.max).then_inc(s["stat_steps"], 1)
                    own("run_max_fwd")
                    v.tensor_tensor_scan(rev(W["run"]), rev(m, TE, M_A + 1), rev(W["fwd"]), -BIG, ALU.add, ALU.max).then_inc(s["stat_steps"], 1)
                    own("run_max")
                    v.tensor_tensor(ends[0][:, :, :], W["run"][:, 0:TE:TE - 1].unsqueeze(2).to_broadcast([P, 2, CT]),
                                    tile_sel[:, :].unsqueeze(1).to_broadcast([P, 2, CT]), ALU.mult).then_inc(s["stat_steps"], 1)
                    yield
                    dve.wait_ge(s["pe_steps"], pe_stat(ch, "max_rows"))
                    v.tensor_tensor_scan(state[0][:, 1:CT + 1], t[:, R_A:R_A + CT], rows_ps(ch, 0)[:, CT:2 * CT], state[0][:, 0:1], ALU.add, ALU.max).then_inc(s["stat_steps"], 1)
                    own("max_carry")
                    v.tensor_tensor(sides[0][:, 0, :], state[0][:, 0:CT], t[:, R_C:R_C + CT], ALU.add).then_inc(s["stat_steps"], 1)
                    v.tensor_tensor(right[0][:, :], t[:, R_CR:R_CR + CT], rows_ps(ch, 0)[:, 1:CT + 1], ALU.add).then_inc(s["stat_steps"], 1)
                    own("max_right_in")
                    v.tensor_tensor(right[0][:, :], right[0][:, :], state[0][:, 1:CT + 1], ALU.max).then_inc(s["stat_steps"], 1)
                    own("max_right_top")
                    v.tensor_tensor_scan(rev(sides[0][:, 1, :], CT), rev(t, CT, R_AR), rev(right[0], CT), -BIG, ALU.add, ALU.max).then_inc(s["stat_steps"], 1)
                    v.tensor_copy(state[0][:, 0:1], state[0][:, CT:CT + 1]).then_inc(s["stat_steps"], 1)
                    yield
                    dve.wait_ge(s["pe_steps"], pe_stat(ch, "max_cols"))
                    v.tensor_tensor(picked[0][:, :, :], cols_ps(ch, 0).rearrange("p (a t) -> p a t", a=2), tile_sel[:, :].unsqueeze(1).to_broadcast([P, 2, CT]), ALU.mult).then_inc(s["stat_steps"], 1)
                    own("max_pick")
                    v.tensor_reduce(cols[0][:, :], picked[0][:, :, :], X_AXIS, ALU.add).then_inc(s["stat_steps"], 1)
                    own("max_picked")
                    v.scalar_tensor_tensor(W["first"][:, :], m[:, M_C:M_C + TE], cols[0][:, 0:1], W["run"][:, :], ALU.add, ALU.max).then_inc(s["stat_steps"], 1)
                    own("max_first")
                    v.scalar_tensor_tensor(W["all"][:, :], m[:, M_D:M_D + TE], cols[0][:, 1:2], W["first"][:, :], ALU.add, ALU.max).then_inc(s["stat_steps"], 1)
                    own("max_all")
                    v.tensor_tensor(W["shift"][:, :], scores_t(ch), W["all"][:, :], ALU.subtract).then_inc(s["stat_steps"], 1)
                    v.tensor_tensor(alpha_arg[:, :], cols[0][0:H, 0:1], W["all"][0:H, 0:1], ALU.subtract).then_inc(s["stat_steps"], 1)
                    yield
                    dve.wait_ge(s["act_steps"], act_stat(ch, "exps"))
                    v.tensor_tensor_scan(W["fwd"][:, :], m[:, M_AM:M_AM + TE], W["ea"][:, :], 0.0, ALU.mult, ALU.add).then_inc(s["stat_steps"], 1)
                    own("run_sum_fwd")
                    v.tensor_tensor_scan(rev(W["run"]), rev(m, TE, M_A + 1), rev(W["fwd"]), 0.0, ALU.add, ALU.max).then_inc(s["stat_steps"], 1)
                    own("run_sum")
                    v.tensor_tensor(ends[1][:, :, :], W["run"][:, 0:TE:TE - 1].unsqueeze(2).to_broadcast([P, 2, CT]),
                                    tile_sel[:, :].unsqueeze(1).to_broadcast([P, 2, CT]), ALU.mult).then_inc(s["stat_steps"], 1)
                    v.tensor_tensor(state[1][:, 0:1], state[1][:, 0:1], alpha[:, :], ALU.mult).then_inc(s["stat_steps"], 1)
                    yield
                    dve.wait_ge(s["pe_steps"], pe_stat(ch, "sum_rows"))
                    own("sum_carry_in")
                    v.tensor_tensor_scan(state[1][:, 1:CT + 1], t[:, f + R_A:f + R_A + CT], rows_ps(ch, 1)[:, CT:2 * CT], state[1][:, 0:1], ALU.mult, ALU.add).then_inc(s["stat_steps"], 1)
                    own("sum_carry")
                    v.tensor_tensor(sides[1][:, 0, :], state[1][:, 0:CT], t[:, f + R_C:f + R_C + CT], ALU.mult).then_inc(s["stat_steps"], 1)
                    v.tensor_tensor(right[1][:, :], t[:, f + R_CR:f + R_CR + CT], rows_ps(ch, 1)[:, 1:CT + 1], ALU.mult).then_inc(s["stat_steps"], 1)
                    own("sum_right_in")
                    v.tensor_tensor(right[1][:, :], right[1][:, :], state[1][:, 1:CT + 1], ALU.add).then_inc(s["stat_steps"], 1)
                    own("sum_right_top")
                    v.tensor_tensor_scan(rev(sides[1][:, 1, :], CT), rev(t, CT, f + R_AR), rev(right[1], CT), 0.0, ALU.mult, ALU.max).then_inc(s["stat_steps"], 1)
                    yield
                    dve.wait_ge(s["pe_steps"], pe_stat(ch, "sum_cols"))
                    v.tensor_tensor(picked[1][:, :, :], cols_ps(ch, 1).rearrange("p (a t) -> p a t", a=2), tile_sel[:, :].unsqueeze(1).to_broadcast([P, 2, CT]), ALU.mult).then_inc(s["stat_steps"], 1)
                    own("sum_pick")
                    v.tensor_reduce(cols[1][:, :], picked[1][:, :, :], X_AXIS, ALU.add).then_inc(s["stat_steps"], 1)
                    own("sum_picked")
                    v.scalar_tensor_tensor(W["first"][:, :], m[:, M_CM:M_CM + TE], cols[1][:, 0:1], W["run"][:, :], ALU.mult, ALU.add).then_inc(s["stat_steps"], 1)
                    own("sum_first")
                    v.scalar_tensor_tensor(W["all"][:, :], m[:, M_DM:M_DM + TE], cols[1][:, 1:2], W["first"][:, :], ALU.mult, ALU.max).then_inc(s["stat_steps"], 1)
                    own("sum_all")
                    v.reciprocal(W["inv"][:, :], W["all"][:, :]).then_inc(s["stat_steps"], 1)
                    own("sum_inverse")
                    v.tensor_tensor(W["wts"][:, :], W["ea"][:, :], W["inv"][:, :], ALU.mult).then_inc(s["stat_steps"], 1)
                    v.tensor_tensor(factor[:, :], state[1][:, 0:1], W["inv"][0:H, 0:1], ALU.mult).then_inc(s["stat_steps"], 1)
                    own("acc_factor")
                    v.tensor_copy(state[1][:, 0:1], state[1][:, CT:CT + 1]).then_inc(s["carry_init"], 1)
                    yield

                def body(ch, prev, older, nxt):
                    if older and prev:
                        dve.load(regs, windows[0:1, bass.ds(older.c * CT, CT + 1)])
                    elif older:
                        dve.load(regs[0:CT], windows[0:1, bass.ds(older.c * CT, CT)])
                    elif prev:
                        dve.load(regs[CT:], windows[0:1, bass.ds(prev.c * CT, 1)])
                    more = adds(older) if older else iter(())
                    parts = stats(prev, more) if prev else iter(range(6))
                    for part in range(6):
                        next(parts)
                        if ch and part < NQ:
                            product(ch, part)
                    for _ in more:
                        pass
                    if prev:
                        dve.wait_ge(s["act_steps"], act_stat(prev, "weights_sb"))
                        for q in range(NQ):
                            message(prev, q)
                        carried(prev)

                over_chunks(dve, l, body)


def node_out(nc, l, s, banks, x_t, acc, ntype_b, ident, Wa, skip, x, out):
    last_layer = l == L - 1
    with ExitStack() as ctx:
        def sb(name, shape, dt=F32):
            return ctx.enter_context(nc.sbuf_tensor(f"out_{name}_{l}", shape, dt))

        wa = sb("wa", [P, NT, D])
        gate_in = sb("gate_in", [P, NT])
        gate_exp = sb("gate_exp", [P, NT])
        gate = sb("gate", [P, NT])
        rest = sb("rest", [P, NT])
        w_h = sb("w_h", [P, NT, D])
        w_x = sb("w_x", [P, NT, D])
        masked = [sb(f"masked{i}", [P, 2 * NT, NB]) for i in range(2)]
        mix_ps, row_ps = banks[0:2], banks[2:4]
        if last_layer:
            fresh = [sb(f"fresh{i}", [P, NB]) for i in range(2)]
            rows = sb("x_rows", [P, XT * D])
            eps = sb("eps", [P, 1])
            resid = [sb(f"resid{i}", [P, 2, D]) for i in range(2)]
            stats = [sb(f"stats{i}", [P, 2, 6]) for i in range(2)]
            mv = [sb(f"mv{i}", [P, 2, 2]) for i in range(2)]
            root = [sb(f"root{i}", [P, 2]) for i in range(2)]
            inv = [sb(f"inv{i}", [P, 2]) for i in range(2)]
            normed = [sb(f"normed{i}", [P, 2, D]) for i in range(2)]

        def mixed(b):
            return b + (l * NBLK + 1)

        with nc.Block() as block:
            @block.sync
            def _(sp):
                sp.dma_start(wa[:, :, :], Wa[l].rearrange("t k n -> k t n")).then_inc(s["wa_in"], 16)
                sp.dma_start(gate_in[:, :], skip[l:l + 1, :].to_broadcast([P, NT])).then_inc(s["wa_in"], 16)
                if last_layer:
                    by_tile = rows[:, :].rearrange("p (t f) -> p t f", f=D)
                    full = XT - 1
                    sp.dma_start(by_tile[:, 0:full, :], x[0:full * P, :].rearrange("(t p) f -> p t f", p=P)).then_inc(s["x_rows"], 16)
                    sp.dma_start(by_tile[0:XR, full, :], x[full * P:N, :]).then_inc(s["x_rows"], 16)

                    def store(b, i):
                        sp.wait_ge(s["normed"], b + 1)
                        sp.dma_start(out[bass.ds(b * NB, NB), :].rearrange("(t p) f -> p t f", p=P), normed[i][:, :, :]).then_inc(s["stored"][i], 16)
                    with sp.Fori(0, NBLK // 2) as b:
                        for i in range(2):
                            store(b * 2 + i, i)
                    sp.wait_ge(s["normed"], NBLK)
                    sp.dma_start(out[full * P:N, :], normed[0][0:XR, 0, :]).then_inc(s["stored"][0], 16)
                    for i in range(2):
                        sp.wait_ge(s["stored"][i], 16 * ((NBLK + 1 - i) // 2))

            @block.vector
            def _(dve):
                v = nc.vector
                g = l * 3
                dve.wait_ge(s["neg_exp"], l + 1)
                v.tensor_scalar(gate_exp[:, :], gate_exp[:, :], 1.0, None, ALU.add).then_inc(s["gates"], 1)
                dve.wait_ge(s["gates"], g + 1)
                v.reciprocal(gate[:, :], gate_exp[:, :]).then_inc(s["gates"], 1)
                dve.wait_ge(s["gates"], g + 2)
                v.tensor_scalar(rest[:, :], gate[:, :], -1.0, 1.0, ALU.mult, ALU.add).then_inc(s["gates"], 1)
                dve.wait_ge(s["gates"], g + 3)
                for t in range(NT):
                    v.tensor_scalar(w_h[:, t, :], wa[:, t, :], gate[:, t:t + 1], None, ALU.mult).then_inc(s["wa_scaled"], 1)
                    v.tensor_scalar(w_x[:, t, :], ident[:, :], rest[:, t:t + 1], None, ALU.mult).then_inc(s["wa_scaled"], 1)

                def mask(b, i):
                    if not (isinstance(b, int) and b < 2):
                        dve.wait_ge(s["mixed"], mixed(b - 2))
                    for k, of in enumerate((x_t, acc)):
                        for t in range(NT):
                            last = v.scalar_tensor_tensor(masked[i][:, k * NT + t, :], ntype_b[:, bass.ds(b * NB, NB)], float(t), of[:, bass.ds(b * NB, NB)],
                                                          ALU.is_equal, ALU.mult)
                    last.then_inc(s["cols_masked"], 1)

                def residual(b, i, full=True):
                    n, tiles = (P, 2) if full else (XR, 1)
                    dve.wait_ge(s["rows_t"], b + 1)
                    if not (isinstance(b, int) and b < 2):
                        dve.wait_ge(s["normed"], b - 1)
                    v.tensor_tensor(resid[i][0:n, 0:tiles, :], rows[0:n, bass.ds(b * NB, tiles * D)].rearrange("p (t f) -> p t f", f=D),
                                    row_ps[i][0:n, 0:tiles * D].rearrange("p (t f) -> p t f", f=D), ALU.add).then_inc(s["resid"], 1)
                    dve.wait_ge(s["resid"], b + 1)
                    dve.nop(nofuse=True)
                    for k in range(tiles):
                        v.bn_stats(stats[i][0:n, k, :], resid[i][0:n, k, :]).then_inc(s["stats"], 1)
                    for k in range(tiles):
                        dve.wait_ge(s["stats"], b * 2 + (k + 1))
                        dve.nop(nofuse=True)
                        v.bn_aggr(mv[i][0:n, k, :], stats[i][0:n, k, :]).then_inc(s["aggr"], 1)

                def norm(turn, i, full=True):
                    b = turn * 2 + i
                    n, tiles = (P, 2) if full else (XR, 1)
                    dve.wait_ge(s["root"], b + 1)
                    v.reciprocal(inv[i][0:n, 0:tiles], root[i][0:n, 0:tiles]).then_inc(s["inverse"], 1)
                    dve.wait_ge(s["inverse"], b + 1)
                    if not (isinstance(turn, int) and turn < 1):
                        dve.wait_ge(s["stored"][i], turn * 16)
                    for k in range(tiles):
                        last = v.tensor_scalar(normed[i][0:n, k, :], resid[i][0:n, k, :], mv[i][0:n, k, 0:1], inv[i][0:n, k:k + 1],
                                               ALU.subtract, ALU.mult)
                    last.then_inc(s["normed"], 1)

                if last_layer:
                    v.memset(eps[:, :], EPS).then_inc(s["eps"], 1)
                    dve.wait_ge(s["x_rows"], 32)
                for b in range(4):
                    mask(b, b % 2)
                    if last_layer and b >= 2:
                        residual(b - 2, b % 2)
                    if last_layer and b >= 3:
                        norm(0, b - 3)
                with dve.Fori(2, NBLK // 2) as b:
                    for i in range(2):
                        mask(b * 2 + i, i)
                        if last_layer:
                            residual(b * 2 + (i - 2), i)
                            norm(b - (2 - i), 1 - i)
                mask(NBLK - 1, 0)
                if last_layer:
                    for b in range(NBLK - 3, NBLK):
                        residual(b, b % 2, b < NBLK - 1)
                        norm((b - 1) // 2, 1 - b % 2)
                    norm(NBLK // 2, 0, False)

            @block.scalar
            def _(act):
                a = nc.scalar
                act.wait_ge(s["wa_in"], 32 * (l + 1))
                a.activation(gate_exp[:, :], gate_in[:, :], ACT.Exp, scale=-1.0).then_inc(s["neg_exp"], 1)

                def block_of(b, i):
                    act.wait_ge(s["mixed"], mixed(b))
                    if not last_layer:
                        a.activation(x_t[:, bass.ds(b * NB, NB)], mix_ps[i][:, 0:NB], ACT.Copy).then_inc(s["x_new"], 1)
                        return
                    if not (isinstance(b, int) and b < 2):
                        act.wait_ge(s["rows_t"], b - 1)
                    a.activation(fresh[i][:, :], mix_ps[i][:, 0:NB], ACT.Copy).then_inc(s["x_new"], 1)

                def deviation(b, i, full=True):
                    n, tiles = (P, 2) if full else (XR, 1)
                    if not last_layer:
                        return
                    act.wait_ge(s["aggr"], b * 2 + tiles)
                    if not (isinstance(b, int) and b < 2):
                        act.wait_ge(s["inverse"], b - 1)
                    a.activation(root[i][0:n, 0:tiles], mv[i][0:n, 0:tiles, 1:2].rearrange("p t a -> p (t a)"), ACT.Sqrt, bias=eps[0:n, 0:1]).then_inc(s["root"], 1)

                if last_layer:
                    act.wait_ge(s["eps"], 1)
                for b in range(4):
                    block_of(b, b % 2)
                    if b >= 2:
                        deviation(b - 2, b % 2)
                with act.Fori(2, NBLK // 2) as b:
                    for i in range(2):
                        block_of(b * 2 + i, i)
                        deviation(b * 2 + (i - 2), i)
                block_of(NBLK - 1, 0)
                for b in range(NBLK - 3, NBLK):
                    deviation(b, b % 2, b < NBLK - 1)

            @block.tensor
            def _(pe):
                t_ = nc.tensor
                pe.wait_ge(s["wa_scaled"], 2 * NT * (l + 1))

                def mix(b, i):
                    if not (isinstance(b, int) and b < 2):
                        pe.wait_ge(s["x_new"], mixed(b - 2))
                    pe.wait_ge(s["cols_masked"], mixed(b))
                    for k in range(2 * NT):
                        w = w_x[:, k, :] if k < NT else w_h[:, k - NT, :]
                        last = t_.matmul(mix_ps[i][:, 0:NB], w, masked[i][:, k, :], start=(k == 0), stop=(k == 2 * NT - 1))
                    last.then_inc(s["mixed"], 1)

                def turn(b, i, full=True):
                    if not last_layer:
                        return
                    pe.wait_ge(s["x_new"], mixed(b))
                    if not (isinstance(b, int) and b < 2):
                        pe.wait_ge(s["resid"], b - 1)
                    n = P if full else XR
                    for k in range(2 if full else 1):
                        last = t_.transpose(row_ps[i][0:n, k * D:(k + 1) * D], fresh[i][:, k * P:k * P + n], ident[:, :])
                    last.then_inc(s["rows_t"], 1)

                mix(0, 0)
                mix(1, 1)
                turn(0, 0)
                mix(2, 0)
                turn(1, 1)
                with pe.Fori(1, NBLK // 2) as b:
                    for i in range(2):
                        mix(b * 2 + (i + 1), 1 - i)
                        turn(b * 2 + i, i)
                turn(NBLK - 1, 0, False)


_INS = ["x", "src", "dst", "edge_type_6", "node_type_3", "L0_gnn_Wk", "L0_gnn_Wq", "L0_gnn_Wv", "L0_gnn_Wa",
        "L0_gnn_pri", "L0_gnn_Watt", "L0_gnn_Wmsg", "L0_gnn_skip"]


def kernel(**inputs):
    import numpy as _np
    import concourse.bacc as _bacc
    from concourse import mybir as _mybir
    from concourse.bass_utils import run_bass_kernel_spmd as _run

    nc = _bacc.Bacc("TRN2", target_bir_lowering=False, num_devices=1)
    arrays, args = {}, []
    for name in _INS:
        a = _np.ascontiguousarray(inputs[name])
        arrays[f"in_{name}"] = a
        args.append(nc.dram_tensor(f"in_{name}", a.shape, _mybir.dt.from_np(a.dtype), kind="ExternalInput").ap())
    result = nc.dram_tensor("out_x", (N, D), _mybir.dt.float32, kind="ExternalOutput").ap()
    hgt_kernel(nc, *args, result)
    r = _run(nc, [arrays], core_ids=[0])
    return r.results[0]["out_x"]
```
